# Optimizing a Trainium2 kernel written in Bass

```python
import numpy as np
import jax
import jax.numpy as jnp

def _softmax(x, axis=-1):
    return jax.nn.softmax(x, axis=axis)

def _gelu(x):
    return jax.nn.gelu(x, approximate=True)

def _silu(x):
    return jax.nn.silu(x)

def _sigmoid(x):
    return jax.nn.sigmoid(x)

def _layernorm(x, axis=-1, eps=1e-05):
    m = jnp.mean(x, axis=axis, keepdims=True)
    v = jnp.var(x, axis=axis, keepdims=True)
    return (x - m) / jnp.sqrt(v + eps)

def _scatter_add(tgt, idx, src, axis=0):
    return tgt.at[idx].add(src)

def _segment_sum(src, seg, n):
    return jax.ops.segment_sum(src, seg, n)
kernel_name = 'mk_decoder_preln_d1_seqx_r4_87102c'

def setup_inputs(seed: int=0):
    np.random.seed(seed)
    _w = jnp.asarray

    def _rec_inputs():
        import jax
        import jax.numpy as jnp
        _rk = jax.random.key(seed)
        x = 7.22e-05 + 1 * jax.random.normal(jax.random.fold_in(_rk, 1), (8, 100, 512), jnp.float32)
        _lenS = 100 - jax.random.randint(jax.random.fold_in(_rk, 7), (8,), 0, max(1, 100 // 4) + 1, jnp.int32)
        _lenS2 = 361 - jax.random.randint(jax.random.fold_in(_rk, 8), (8,), 0, max(1, 361 // 4) + 1, jnp.int32)
        _ctx_1024P = jax.random.normal(jax.random.fold_in(_rk, 11), (8, 16, 256), jnp.float32)
        _ctx_1024c = jax.random.dirichlet(jax.random.fold_in(_rk, 511), 0.3 * jnp.ones((16,), jnp.float32), (8, 361))
        _ctx_1024t = jnp.einsum('bsk,bkd->bsd', _ctx_1024c, _ctx_1024P)
        _ctx_1024t = _ctx_1024t * jax.lax.rsqrt(jnp.mean(jnp.square(_ctx_1024t)) + 1e-12) * 0.953939
        ctx_1024 = -0.000673644 + 1.00013 * (_ctx_1024t + 0.3 * jax.random.normal(jax.random.fold_in(_rk, 611), (8, 361, 256), jnp.float32))
        return (x, ctx_1024)
    x, ctx_1024 = _rec_inputs()

    def _L0_attn_setup():
        import jax, jax.numpy as jnp
        import numpy as np
        D_MODEL = 512
        N_HEADS = 16
        N_KV = 4
        GROUP = N_HEADS // N_KV
        D_K = D_MODEL // N_HEADS
        D_V = D_MODEL // N_KV
        THETA = 10000.0
        Q_DIM = N_HEADS * D_K
        K_DIM = N_KV * D_K
        V_DIM = N_KV * D_V

        def _apply_rope(t, sin, cos):
            half = t.shape[-1] // 2
            x1, x2 = (t[..., :half], t[..., half:])
            rot = jnp.concatenate([-x2, x1], axis=-1)
            return t * cos + rot * sin
        key = jax.random.key(seed)
        k1, k2, k3 = jax.random.split(key, 3)
        x = jax.random.normal(k1, (2, 512, D_MODEL), dtype=jnp.float32)
        W_attn = jax.random.normal(k2, (D_MODEL, Q_DIM + K_DIM + V_DIM), dtype=jnp.float32) * 0.02
        W_out = jax.random.normal(k3, (N_HEADS * D_V, D_MODEL), dtype=jnp.float32) * 0.02
        b_out = jnp.zeros((D_MODEL,), dtype=jnp.float32)
        return {'x': x, 'W_attn': W_attn, 'W_out': W_out, 'b_out': b_out}
    _L0_attn_all = _L0_attn_setup()
    _L0_attn_in = {k: v for k, v in _L0_attn_all.items() if k in ('W_attn', 'W_out', 'b_out')}
    del _L0_attn_all

    def _L0_xattn_setup():
        import jax, jax.numpy as jnp
        import numpy as np
        B, S1, S2, DCA = (2, 512, 256, 16)
        QDIM, KDIM, H = (512, 256, 16)
        HD = QDIM // H
        SCALE = HD ** (-0.5)
        EPS = 1e-06
        DCA_WEIGHT = 1.0

        def _ln(t, w, b):
            m = jnp.mean(t, axis=-1, keepdims=True)
            v = jnp.var(t, axis=-1, keepdims=True)
            return (t - m) * jax.lax.rsqrt(v + EPS) * w + b

        def _attn(q, k, v):
            s = jnp.einsum('bhqd,bhkd->bhqk', q, k) * SCALE
            p = jax.nn.softmax(s, axis=-1)
            return jnp.einsum('bhqk,bhkd->bhqd', p, v)
        key = jax.random.key(seed)
        ks = jax.random.split(key, 8)
        w = lambda k, shape: jax.random.normal(k, shape, jnp.float32) * 0.02
        return {'x': jax.random.normal(ks[0], (B, S1, QDIM), jnp.float32), 'y': jax.random.normal(ks[1], (B, S2 + DCA, KDIM), jnp.float32), 'Wq': w(ks[2], (QDIM, QDIM)), 'bq': jnp.zeros((QDIM,), jnp.float32), 'Wk': w(ks[3], (KDIM, QDIM)), 'bk': jnp.zeros((QDIM,), jnp.float32), 'Wv': w(ks[4], (KDIM, QDIM)), 'bv': jnp.zeros((QDIM,), jnp.float32), 'Wkv_dca': w(ks[5], (KDIM, 2 * QDIM)), 'bkv_dca': jnp.zeros((2 * QDIM,), jnp.float32), 'qn_w': jnp.ones((HD,), jnp.float32), 'qn_b': jnp.zeros((HD,), jnp.float32), 'kn_w': jnp.ones((HD,), jnp.float32), 'kn_b': jnp.zeros((HD,), jnp.float32), 'kn_dca_w': jnp.ones((HD,), jnp.float32), 'kn_dca_b': jnp.zeros((HD,), jnp.float32), 'Wo': w(ks[6], (QDIM, QDIM)), 'bo': jnp.zeros((QDIM,), jnp.float32)}
    _L0_xattn_all = _L0_xattn_setup()
    _L0_xattn_in = {k: v for k, v in _L0_xattn_all.items() if k in ('Wq', 'bq', 'Wk', 'bk', 'Wv', 'bv', 'Wkv_dca', 'bkv_dca', 'qn_w', 'qn_b', 'kn_w', 'kn_b', 'kn_dca_w', 'kn_dca_b', 'Wo', 'bo')}
    del _L0_xattn_all

    def _L0_ffn_setup():
        import jax, jax.numpy as jnp
        import numpy as np
        TOP_K = 4
        key = jax.random.key(seed)
        ks = jax.random.split(key, 8)
        B, S, H = (1, 256, 512)
        E, I = (60, 352)
        I_SH = 1408
        s = 0.02
        return {'hidden_states': jax.random.normal(ks[0], (B, S, H), jnp.float32), 'gate_w': jax.random.normal(ks[1], (E, H), jnp.float32) * s, 'shared_gate_w': jax.random.normal(ks[2], (1, H), jnp.float32) * s, 'w13': jax.random.normal(ks[3], (E, 2 * I, H), jnp.float32) * s, 'w2': jax.random.normal(ks[4], (E, H, I), jnp.float32) * s, 'se_gate_up_w': jax.random.normal(ks[5], (2 * I_SH, H), jnp.float32) * s, 'se_down_w': jax.random.normal(ks[6], (H, I_SH), jnp.float32) * s}
    _L0_ffn_all = _L0_ffn_setup()
    _L0_ffn_in = {k: v for k, v in _L0_ffn_all.items() if k in ('gate_w', 'shared_gate_w', 'w13', 'w2', 'se_gate_up_w', 'se_down_w')}
    del _L0_ffn_all
    return {'x': x, 'ctx_1024': ctx_1024, 'L0_attn_W_attn': _L0_attn_in['W_attn'], 'L0_attn_W_out': _L0_attn_in['W_out'], 'L0_attn_b_out': _L0_attn_in['b_out'], 'L0_xattn_Wq': _L0_xattn_in['Wq'], 'L0_xattn_bq': _L0_xattn_in['bq'], 'L0_xattn_Wk': _L0_xattn_in['Wk'], 'L0_xattn_bk': _L0_xattn_in['bk'], 'L0_xattn_Wv': _L0_xattn_in['Wv'], 'L0_xattn_bv': _L0_xattn_in['bv'], 'L0_xattn_Wkv_dca': _L0_xattn_in['Wkv_dca'], 'L0_xattn_bkv_dca': _L0_xattn_in['bkv_dca'], 'L0_xattn_qn_w': _L0_xattn_in['qn_w'], 'L0_xattn_qn_b': _L0_xattn_in['qn_b'], 'L0_xattn_kn_w': _L0_xattn_in['kn_w'], 'L0_xattn_kn_b': _L0_xattn_in['kn_b'], 'L0_xattn_kn_dca_w': _L0_xattn_in['kn_dca_w'], 'L0_xattn_kn_dca_b': _L0_xattn_in['kn_dca_b'], 'L0_xattn_Wo': _L0_xattn_in['Wo'], 'L0_xattn_bo': _L0_xattn_in['bo'], 'L0_ffn_gate_w': _L0_ffn_in['gate_w'], 'L0_ffn_shared_gate_w': _L0_ffn_in['shared_gate_w'], 'L0_ffn_w13': _L0_ffn_in['w13'], 'L0_ffn_w2': _L0_ffn_in['w2'], 'L0_ffn_se_gate_up_w': _L0_ffn_in['se_gate_up_w'], 'L0_ffn_se_down_w': _L0_ffn_in['se_down_w']}

def reference(x, ctx_1024, L0_attn_W_attn, L0_attn_W_out, L0_attn_b_out, L0_xattn_Wq, L0_xattn_bq, L0_xattn_Wk, L0_xattn_bk, L0_xattn_Wv, L0_xattn_bv, L0_xattn_Wkv_dca, L0_xattn_bkv_dca, L0_xattn_qn_w, L0_xattn_qn_b, L0_xattn_kn_w, L0_xattn_kn_b, L0_xattn_kn_dca_w, L0_xattn_kn_dca_b, L0_xattn_Wo, L0_xattn_bo, L0_ffn_gate_w, L0_ffn_shared_gate_w, L0_ffn_w13, L0_ffn_w2, L0_ffn_se_gate_up_w, L0_ffn_se_down_w):
    import jax
    import jax.numpy as jnp

    def _L0_attn_ref(x, W_attn, W_out, b_out):
        import jax, jax.numpy as jnp
        import numpy as np
        D_MODEL = 512
        N_HEADS = 16
        N_KV = 4
        GROUP = N_HEADS // N_KV
        D_K = D_MODEL // N_HEADS
        D_V = D_MODEL // N_KV
        THETA = 10000.0
        Q_DIM = N_HEADS * D_K
        K_DIM = N_KV * D_K
        V_DIM = N_KV * D_V

        def _apply_rope(t, sin, cos):
            half = t.shape[-1] // 2
            x1, x2 = (t[..., :half], t[..., half:])
            rot = jnp.concatenate([-x2, x1], axis=-1)
            return t * cos + rot * sin
        B, L, _ = x.shape
        qkv = x @ W_attn
        q = qkv[..., :Q_DIM].reshape(B, L, N_HEADS, D_K).transpose(0, 2, 1, 3)
        k = qkv[..., Q_DIM:Q_DIM + K_DIM].reshape(B, L, N_KV, D_K).transpose(0, 2, 1, 3)
        v = qkv[..., Q_DIM + K_DIM:].reshape(B, L, N_KV, D_V).transpose(0, 2, 1, 3)
        inv_freq = 1.0 / THETA ** (jnp.arange(0, D_K, 2, dtype=jnp.float32) / D_K)
        freqs = jnp.arange(L, dtype=jnp.float32)[:, None] * inv_freq[None, :]
        ang = jnp.concatenate([freqs, freqs], axis=-1)
        sin, cos = (jnp.sin(ang), jnp.cos(ang))
        q = _apply_rope(q.astype(jnp.float32), sin, cos).astype(x.dtype)
        k = _apply_rope(k.astype(jnp.float32), sin, cos).astype(x.dtype)
        qg = q.reshape(B, N_KV, GROUP, L, D_K)
        scores = jnp.einsum('bkgqd,bkld->bkgql', qg, k) / D_K ** 0.5
        probs = jax.nn.softmax(scores, axis=-1)
        ctx = jnp.einsum('bkgql,bkle->bkgqe', probs, v)
        ctx = ctx.reshape(B, N_HEADS, L, D_V).transpose(0, 2, 1, 3).reshape(B, L, N_HEADS * D_V)
        return ctx @ W_out + b_out

    def _L0_xattn_ref(x, y, Wq, bq, Wk, bk, Wv, bv, Wkv_dca, bkv_dca, qn_w, qn_b, kn_w, kn_b, kn_dca_w, kn_dca_b, Wo, bo):
        import jax, jax.numpy as jnp
        import numpy as np
        B, S1, S2, DCA = (2, 512, 256, 16)
        QDIM, KDIM, H = (512, 256, 16)
        HD = QDIM // H
        SCALE = HD ** (-0.5)
        EPS = 1e-06
        DCA_WEIGHT = 1.0

        def _ln(t, w, b):
            m = jnp.mean(t, axis=-1, keepdims=True)
            v = jnp.var(t, axis=-1, keepdims=True)
            return (t - m) * jax.lax.rsqrt(v + EPS) * w + b

        def _attn(q, k, v):
            s = jnp.einsum('bhqd,bhkd->bhqk', q, k) * SCALE
            p = jax.nn.softmax(s, axis=-1)
            return jnp.einsum('bhqk,bhkd->bhqd', p, v)
        b, s1, _ = x.shape
        y_dca = y[:, -DCA:, :]
        y_main = y[:, :-DCA, :]
        kv_dca = (y_dca @ Wkv_dca + bkv_dca).reshape(b, DCA, 2, H, HD)
        k_dca = _ln(kv_dca[:, :, 0], kn_dca_w, kn_dca_b)
        v_dca = kv_dca[:, :, 1]
        s2 = y_main.shape[1]
        q = _ln((x @ Wq + bq).reshape(b, s1, H, HD), qn_w, qn_b)
        kv = jnp.concatenate([y_main @ Wk + bk, y_main @ Wv + bv], axis=-1)
        kv = kv.reshape(b, s2, H, 2 * HD)
        k = _ln(kv[..., :HD], kn_w, kn_b)
        v = kv[..., HD:]
        qT = q.transpose(0, 2, 1, 3)
        ctx = _attn(qT, k.transpose(0, 2, 1, 3), v.transpose(0, 2, 1, 3))
        ctx = ctx.transpose(0, 2, 1, 3).reshape(b, s1, QDIM)
        ctx_dca = _attn(qT, k_dca.transpose(0, 2, 1, 3), v_dca.transpose(0, 2, 1, 3))
        ctx_dca = ctx_dca.transpose(0, 2, 1, 3).reshape(b, s1, QDIM)
        ctx = ctx + DCA_WEIGHT * ctx_dca
        return ctx @ Wo + bo

    def _L0_ffn_ref(hidden_states, gate_w, shared_gate_w, w13, w2, se_gate_up_w, se_down_w):
        import jax, jax.numpy as jnp
        import numpy as np
        TOP_K = 4
        orig_shape = hidden_states.shape
        E, H = gate_w.shape
        I = w2.shape[2]
        x = hidden_states.reshape(-1, H)
        M = x.shape[0]
        gu = x @ se_gate_up_w.T
        I_sh = se_down_w.shape[1]
        shared = jax.nn.silu(gu[:, :I_sh]) * gu[:, I_sh:] @ se_down_w.T
        shared = shared * jax.nn.sigmoid(x @ shared_gate_w.T)
        logits = x @ gate_w.T
        probs = jax.nn.softmax(logits.astype(jnp.float32), axis=-1)
        weights, sel = jax.lax.top_k(probs, TOP_K)
        cw = jnp.zeros((M, E), jnp.float32).at[jnp.arange(M)[:, None], sel].add(weights)

        def step(acc, ews):
            w13_e, w2_e, cw_e = ews
            gu_e = x @ w13_e.T
            h = jax.nn.silu(gu_e[:, :I]) * gu_e[:, I:]
            return (acc + cw_e[:, None] * (h @ w2_e.T), None)
        sparse, _ = jax.lax.scan(step, jnp.zeros((M, H), jnp.float32), (w13, w2, cw.T))
        return (shared + sparse).reshape(orig_shape)
    x = x + _L0_attn_ref(_layernorm(x, axis=-1), L0_attn_W_attn, L0_attn_W_out, L0_attn_b_out)
    x = x + _L0_xattn_ref(_layernorm(x, axis=-1), ctx_1024, L0_xattn_Wq, L0_xattn_bq, L0_xattn_Wk, L0_xattn_bk, L0_xattn_Wv, L0_xattn_bv, L0_xattn_Wkv_dca, L0_xattn_bkv_dca, L0_xattn_qn_w, L0_xattn_qn_b, L0_xattn_kn_w, L0_xattn_kn_b, L0_xattn_kn_dca_w, L0_xattn_kn_dca_b, L0_xattn_Wo, L0_xattn_bo)
    x = x + _L0_ffn_ref(_layernorm(x, axis=-1), L0_ffn_gate_w, L0_ffn_shared_gate_w, L0_ffn_w13, L0_ffn_w2, L0_ffn_se_gate_up_w, L0_ffn_se_down_w)
    return x

_drawn_inputs = setup_inputs


def setup_inputs(seed=0):
    import zlib

    import numpy as np

    out = dict(_drawn_inputs(seed))
    spreads = {'L0_attn_b_out': (0.0, 0.1),
     'L0_xattn_bq': (0.0, 0.697),
     'L0_xattn_bk': (0.0, 0.1),
     'L0_xattn_bv': (0.0, 0.1),
     'L0_xattn_bkv_dca': (0.0, 0.1),
     'L0_xattn_qn_w': (1.0, 0.6),
     'L0_xattn_qn_b': (0.0, 0.8),
     'L0_xattn_kn_w': (1.0, 0.6),
     'L0_xattn_kn_b': (0.0, 2.0),
     'L0_xattn_kn_dca_w': (1.0, 0.6),
     'L0_xattn_kn_dca_b': (0.0, 2.0),
     'L0_xattn_bo': (0.0, 0.1)}
    factors = {'L0_ffn_gate_w': 6.882,
     'L0_ffn_shared_gate_w': 53.576,
     'L0_ffn_w13': 5.019,
     'L0_ffn_w2': 4.991,
     'L0_ffn_se_gate_up_w': 5.256,
     'L0_ffn_se_down_w': 5.228}
    for name, (base, spread) in spreads.items():
        noise = np.random.default_rng([zlib.crc32(name.encode()), seed]).standard_normal(out[name].shape)
        drawn = base * np.exp(spread * noise) if base else spread * noise
        out[name] = jnp.asarray(drawn.astype(out[name].dtype))
    for name, factor in factors.items():
        out[name] = (out[name] * factor).astype(out[name].dtype)
    return out
```

```python
from contextlib import ExitStack

import concourse.bass as bass
from concourse import mybir

F32 = mybir.dt.float32
U32 = mybir.dt.uint32
I32 = mybir.dt.int32
ALU = mybir.AluOpType
ACT = mybir.ActivationFunctionType
AX = mybir.AxisListType.X

P = 128
B, S, D = 8, 100, 512
DC = D // P
H, KV, G = 16, 4, 4
HD = 32
VD = 128
QK = (H + KV) * HD
L, DCA = 361, 16
LM = L - DCA
LC, LN_ = 115, 3
CC = 2
E, I = 60, 352
IC = (128, 128, 96)
ISH = 1408
MC = ISH // P
TOPK = 4
LINKS = 194
T = 128
NOV = (B * S * TOPK) // (T + 1)
NG = E + 1
PAIRS = B // 2
SCALE = HD ** -0.5


class Signal:

    all = []

    def __init__(self, sem, keys):
        self.sem, self.keys = sem, list(keys)
        Signal.all.append(self)

    def at(self, i, key):
        return i * len(self.keys) + (self.keys.index(key) + 2)

    def before(self, i):
        return i * len(self.keys) + 1

    def prior(self, i, key):
        return i * len(self.keys) + (self.keys.index(key) + 1)


def attention_fills():
    out = []
    for j in range(2):
        out.append((("xT1", j), 4 + j))
    for j in range(2):
        out += [(("q", j), (0, 3)[j]), (("k", j), (1, 6)[j]), (("v", j), (2, 7)[j])]
        out += kv_fills(j, 0)
    for j in range(2):
        out += [(("qT", j), 4), (("kT", j), 5)]
        out += [(("s", j, g), g) for g in range(G)]
        out += kv_fills(j, 1)
    for j in range(2):
        out += [(("pT", j, g), 4 + g % 2) for g in range(G)]
        out += kv_fills(j, 2)
        out += [(("pv", j, k), 6 + k % 2) for k in range(KV)]
        out.append((("o", j), j))
    for j in range(2):
        out.append((("xT2", j), 4 + j))
    for j in range(2):
        out.append((("xq", j), 2 + j))
    out.append((("kxT",) + KV_UNITS[-1], 4))
    for j in range(2):
        out.append((("xqT", j), 4 + j))
    for j in range(2):
        out.append((("ds", j), 2 + j))
    for j in range(2):
        out.append((("dpT", j), 4 + j))
    for j in range(2):
        out.append((("dpv", j), 6 + j))
    for n in range(2 * H + 4):
        if n < 2 * H:
            out.append((("xs", n), n % 4))
        if 2 <= n < 2 * H + 2:
            out.append((("xpT", n - 2), 4 + n % 2))
        if n >= 4 and (n - 4) % H == H - 1:
            out.append((("ctx", (n - 4) // H), 6 + (n - 4) // H))
    for j in range(2):
        out.append((("cT", j), 4 + j))
    for j in range(2):
        out.append((("xo", j), j))
    for j in range(2):
        out.append((("xT3", j), 4 + j))
    for j in range(2):
        out.append((("gate", j), 2 + j))
    return out


KV_UNITS = [(j, c) for c in range(LN_) for j in range(2)]


def kv_fills(j, c):
    n = KV_UNITS.index((j, c))
    before = [(("kxT",) + KV_UNITS[n - 1], 4)] if n else []
    return [(("kx", j, c), 6), (("vx", j, c), 7)] + before


def decoder_kernel(nc, x, ctxT, dcaT, W_attn, W_out, b_out, Wq, bq, Wkv, bkv, Wdca, bdca, norm, Wo, bo,
                   gates, w13, w2, se_up, se_down, cos_sin, out):
    fills = attention_fills()
    bank_of = dict(fills)
    Signal.all = []

    cm = ExitStack()
    with cm:
        def sb(name, shape, dt=F32):
            return cm.enter_context(nc.sbuf_tensor(name, shape, dt))

        def sem(name):
            return cm.enter_context(nc.semaphore(name))

        xn3_d = nc.dram_tensor("xn3_d", [B, S, D], F32, kind="Internal").ap()
        x2_d = nc.dram_tensor("x2_d", [B, S, D], F32, kind="Internal").ap()
        xT3_d = nc.dram_tensor("xT3_d", [B, P, DC * S], F32, kind="Internal").ap()
        vd_d = nc.dram_tensor("vd_d", [P, D], F32, kind="Internal").ap()
        xs_d = nc.dram_tensor("xs_d", [(E + NOV) * T, D], F32, kind="Internal").ap()
        ys_d = nc.dram_tensor("ys_d", [(E + NOV) * T, D], F32, kind="Internal").ap()

        ps = cm.enter_context(nc.psum_tensor("ps", [P, 8, 512], F32))

        ident = sb("ident", [P, P])
        ones = sb("ones", [P, P])
        tri = sb("tri", [P, P])
        zero = sb("zero", [P, D])
        lg_all = sb("lg_all", [P, B, NG])

        ARENA = 50500
        arena = sb("arena", [P, ARENA])
        top = [0]

        def carve(*shape):
            n = 1
            for d in shape:
                n *= d
            a = arena[:, top[0]:top[0] + n]
            top[0] += n
            assert top[0] <= ARENA, top[0]
            if len(shape) == 2:
                return a.rearrange("p (a b) -> p a b", a=shape[0])
            if len(shape) == 3:
                return a.rearrange("p (a b c) -> p a b c", a=shape[0], b=shape[1])
            if len(shape) == 4:
                return a.rearrange("p (a b c d) -> p a b c d", a=shape[0], b=shape[1], c=shape[2])
            return a

        w_attn = carve(DC, QK + D)
        w_out = carve(H, D)
        w_q = carve(DC, D)
        w_kv = carve(CC, 2 * D)
        w_o = carve(DC, D)
        w_gate = carve(DC, NG)
        bo_bc = carve(D)
        bout_bc = carve(D)
        bq_bc = carve(D)
        bkv_bc = carve(2 * D)
        cs = carve(4, HD)
        nrm = carve(6)
        blk_k = carve(4)
        blk_v = carve(8)
        kd_all = carve(DC, P)
        vd_all = carve(B, 2, HD)
        x_in = [carve(D) for _ in range(2)]
        xr = [carve(D) for _ in range(2)]
        xn = [carve(D) for _ in range(2)]
        xT = [carve(DC, S) for _ in range(2)]
        t0 = carve(D)
        t1 = carve(D)
        stat = carve(64)
        stat_n = carve(16)
        qr = [carve(D) for _ in range(2)]
        kr = [carve(KV, G, HD) for _ in range(2)]
        v_s = [carve(D) for _ in range(2)]
        qT = [carve(KV, S) for _ in range(2)]
        kT = [carve(KV, S) for _ in range(2)]
        nmax = [carve(G, KV) for _ in range(2)]
        psum_ = [carve(G, KV) for _ in range(2)]
        prec = [carve(G, KV) for _ in range(2)]
        NP_ = 8
        preamble_at = top[0]
        pr = [carve(KV, S) for _ in range(NP_)]
        pT = carve(KV, G, S)
        cT = [carve(G, S) for _ in range(2)]
        c_in = [carve(CC, LM) for _ in range(2)]
        kn = carve(D)
        vx = [carve(LN_, D) for _ in range(2)]
        kxT = [carve(DC, LM) for _ in range(2)]
        qx = carve(D)
        xqT = [carve(DC, S) for _ in range(2)]
        kdb = [carve(DC, 4, DCA) for _ in range(2)]
        vdb = [carve(2, 8, HD) for _ in range(2)]
        dnm = carve(2, H)
        dsum = carve(2, H)
        drec = carve(2, H)
        dp = [carve(H, DCA) for _ in range(2)]
        dpT = [carve(2, S) for _ in range(2)]
        xnm = carve(2, H)
        xsum = carve(2, H)
        xrec = carve(2, H)
        NX = 3
        xp = [pr[n].rearrange("p a b -> p (a b)")[:, 0:LM] for n in range(NX)]
        pT_flat = pT.rearrange("p a b c -> p (a b c)")
        xpT = [pT_flat[:, n * LN_ * S:(n + 1) * LN_ * S].rearrange("p (a b) -> p a b", a=LN_) for n in range(NX)]
        cx, cxT = qr, cT
        vd_s = carve(D)
        print("attention", top[0])
        top[0] = preamble_at
        w_dca = carve(CC, 2 * D)
        bdca_bc = carve(2 * D)
        c_dca = carve(CC, P)

        top[0] = 0
        xT3 = carve(B, DC * S)
        se_w = [carve(DC, 2 * P) for _ in range(3)]
        hT_all = carve(MC, B * S)
        w_down = carve(MC, D)
        acc = carve(B, D)
        w13_s = [carve(DC, 2 * I) for _ in range(2)]
        w2_s = [carve(3, D) for _ in range(2)]
        xs_s = [carve(D) for _ in range(2)]
        xsT = [carve(DC, T) for _ in range(2)]
        sl = [carve(3, T) for _ in range(2)]
        hT = [carve(3, T) for _ in range(2)]
        y_s = [carve(D) for _ in range(2)]
        s_sh = [carve(400) for _ in range(2)]
        xn3 = carve(B, D)
        oh = carve(B, E)
        mask = carve(B, E)
        slot_e = carve(B, E)
        bts = carve(6, E)
        ovc = carve(NOV, E)[0:1]
        iota_e = sb("iota_e", [P, E])
        iota_n = sb("iota_n", [P, NOV])
        base_e = sb("base_e", [P, E])
        ov_i = sb("ov_i", [1, NOV + 1], I32)
        slot_u = sb("slot_u", [P, B * TOPK], U32)
        idx_u = sb("idx_u", [P, B, 8], U32)
        rsm = sb("rsm", [P, 8, B, 8])

        full = [Signal(sem(f"bank{n}_full"), [k for k, b in fills if b == n]) for n in range(8)]
        free = [Signal(sem(f"bank{n}_free"), [k for k, b in fills if b == n]) for n in range(8)]
        pre_load = sem("preamble_loaded")
        w_loaded = {n: sem(f"{n}_loaded") for n in ("w_attn", "w_out", "w_q", "w_kv", "w_o", "w_gate")}
        consts_ready = sem("consts_ready")
        weights_centred = sem("weights_centred")
        pool_pre = sem("pool_preamble")
        kd_ready = sem("kd_ready")
        vd_stored = sem("vd_stored")
        vd_loaded = sem("vd_loaded")
        dca_mm = sem("dca_projected")
        dca_n = sem("dca_normed")
        dca_t = sem("dca_transposed")
        x_loaded = [sem(f"x_loaded{j}") for j in range(2)]
        c_loaded = [sem(f"c_loaded{j}") for j in range(2)]
        xn_stored = [sem(f"xn3_stored{j}") for j in range(2)]
        x2_stored = [sem(f"x2_stored{j}") for j in range(2)]
        xT_stored = [sem(f"xT3_stored{j}") for j in range(2)]
        zeroed = sem("slots_zeroed")
        chain = sem("vector_chain")
        pairs = [0, 1]
        xn_ready = Signal(sem("xn_ready"), [(n, j) for n in (1, 2, 3) for j in pairs])
        jg = [(j, g) for j in pairs for g in range(G)]
        max_ready = Signal(sem("max_ready"), jg)
        rec_ready = Signal(sem("rec_ready"), jg)
        p_ready = Signal(sem("p_ready"), jg)
        xr_ready = Signal(sem("xr_ready"), [(n, j) for n in (0, 1) for j in pairs])
        kn_ready = Signal(sem("kn_ready"), KV_UNITS)
        qx_ready = Signal(sem("qx_ready"), pairs)
        db_ready = Signal(sem("dca_blocks_ready"), pairs)
        dexp_ready = Signal(sem("dexp_ready"), pairs)
        hh = list(range(2 * H))
        xmax_ready = Signal(sem("xmax_ready"), hh)
        xpv_done = Signal(sem("xpv_done"), [n for n in hh if n % H < H - 1])
        cx_ready = Signal(sem("cx_ready"), pairs)
        o_part = Signal(sem("o_part"), [(j, c) for j in pairs for c in (0, 1)])

        xT3_loaded = sem("xT3_loaded")
        se_loaded = [sem(f"se_loaded{r}") for r in range(3)]
        down_loaded = sem("down_loaded")
        acc_loaded = sem("acc_loaded")
        xn3_loaded = sem("xn3_loaded")
        up_full = [sem(f"up_full{r}") for r in range(2)]
        silu_ready = [sem(f"shared_silu{r}") for r in range(2)]
        hs_ready = [sem(f"shared_h{r}") for r in range(2)]
        dn_full = sem("shared_down_full")
        dn_free = sem("shared_down_free")
        router_step = sem("router_step")
        r_act = sem("router_exp")
        r_in = sem("router_in")
        r_out = sem("router_out")
        mask_ready = sem("mask_ready")
        rank_full = sem("rank_full")
        slots_ready = sem("slots_ready")
        scattered = sem("scattered")
        w13_loaded = [sem(f"w13_loaded{r}") for r in range(2)]
        w2_loaded = [sem(f"w2_loaded{r}") for r in range(2)]
        xs_loaded = [sem(f"xs_loaded{r}") for r in range(2)]
        xst_full = [sem(f"xst_full{r}") for r in range(2)]
        xst_ready = [sem(f"xst_ready{r}") for r in range(2)]
        up1_full = [sem(f"gate_up_full{r}") for r in range(2)]
        sl_ready = [sem(f"silu_ready{r}") for r in range(2)]
        h_ready = [sem(f"h_ready{r}") for r in range(2)]
        y_full = [sem(f"y_full{r}") for r in range(2)]
        y_ready = [sem(f"y_ready{r}") for r in range(2)]
        y_stored = [sem(f"y_stored{r}") for r in range(2)]
        o_w = sem("over_loaded")
        o_t = sem("over_transposed")
        o_tc = sem("over_xT")
        o_g = sem("over_gate_up")
        o_s = sem("over_silu")
        o_h = sem("over_h")
        o_y = sem("over_y")
        o_yc = sem("over_y_copied")
        o_st = sem("over_stored")
        gathered = [sem(f"gathered{r}") for r in range(4)]
        added = [sem(f"added{r}") for r in range(4)]
        out_ready = sem("out_ready")
        load_gate = sem("load_gate")
        out_stored = sem("out_stored")

        by_turns = (x2_stored + xn_stored + xT_stored + up1_full + xst_full + y_full + h_ready + y_ready + xst_ready + y_stored
                    + [o_y, o_yc, o_st])

        block = cm.enter_context(nc.Block())

        def bank(n):
            return ps[:, n, :]

        def wait_filled(eng, i, *key):
            k = bank_of[key]
            eng.wait_ge(full[k].sem, full[k].at(i, key))
            return k

        def wait_drained(eng, i, *key):
            k = bank_of[key]
            eng.wait_ge(free[k].sem, free[k].at(i, key))

        def wait_turns_filled(eng, i, *banks):
            for k in banks:
                eng.wait_ge(full[k].sem, full[k].before(i))

        @block.sync
        def _(sp):
            bc = lambda v, n: v.rearrange("(a d) -> a d", a=1).to_broadcast([P, n])
            sp.dma_start(c_dca, dcaT.rearrange("c p n -> p c n")).then_inc(pre_load, 16)
            sp.dma_start(w_dca, Wdca.rearrange("(c p) n -> p c n", p=P)).then_inc(pre_load, 16)
            sp.dma_start(bdca_bc, bc(bdca, 2 * D)).then_inc(pre_load, 16)
            sp.dma_start(bkv_bc, bc(bkv, 2 * D)).then_inc(pre_load, 16)
            sp.dma_start(bq_bc, bc(bq, D)).then_inc(pre_load, 16)
            sp.dma_start(bo_bc, bc(bo, D)).then_inc(pre_load, 16)
            sp.dma_start(bout_bc, bc(b_out, D)).then_inc(pre_load, 16)
            sp.dma_start(cs[0:S], cos_sin).then_inc(pre_load, 16)
            for g in range(4):
                sp.dma_start(nrm[g * HD:(g + 1) * HD, :], norm).then_inc(pre_load, 16)
            sp.dma_start(w_kv, Wkv.rearrange("(c p) n -> p c n", p=P)).then_inc(w_loaded["w_kv"], 16)
            sp.dma_start(w_q, Wq.rearrange("(c p) n -> p c n", p=P)).then_inc(w_loaded["w_q"], 16)
            sp.dma_start(w_attn, W_attn.rearrange("(c p) n -> p c n", p=P)).then_inc(w_loaded["w_attn"], 16)
            sp.dma_start(w_out, W_out.rearrange("(c p) n -> p c n", p=P)).then_inc(w_loaded["w_out"], 16)
            sp.dma_start(w_o, Wo.rearrange("(c p) n -> p c n", p=P)).then_inc(w_loaded["w_o"], 16)
            sp.dma_start(w_gate, gates.rearrange("(c p) n -> p c n", p=P)).then_inc(w_loaded["w_gate"], 16)
            for i in range(PAIRS):
                for j in range(2):
                    sp.wait_ge(xn_ready.sem, xn_ready.before(i))
                    sp.wait_ge(xr_ready.sem, xr_ready.before(i))
                    sp.dma_start(x_in[j][0:S, :], x[i * 2 + j, :, :]).then_inc(x_loaded[j], 16)
                for j in range(2):
                    sp.wait_ge(full[7].sem, full[7].before(i))
                    sp.dma_start(c_in[j], ctxT[i * 2 + j, :, :, :]).then_inc(c_loaded[j], 16)
                for j in range(2):
                    sp.wait_ge(xn_ready.sem, xn_ready.at(i, (3, j)))
                    sp.dma_start(xn3_d[i * 2 + j, :, :], xn[j][0:S, :]).then_inc(xn_stored[j], 16)
                    sp.dma_start(x2_d[i * 2 + j, :, :], xr[j][0:S, :]).then_inc(x2_stored[j], 16)
                for j in range(2):
                    wait_drained(sp, i, "xT3", j)
                    sp.dma_start(xT3_d[i * 2 + j, :, :], xT[j].rearrange("p a b -> p (a b)")).then_inc(xT_stored[j], 16)

            for k in range(8):
                sp.wait_ge(full[k].sem, full[k].before(PAIRS))
                sp.wait_ge(free[k].sem, free[k].before(PAIRS))
            for j in range(2):
                sp.wait_ge(xn_stored[j], 16 * PAIRS + 1)
                sp.wait_ge(x2_stored[j], 16 * PAIRS + 1)
                sp.wait_ge(xT_stored[j], 16 * PAIRS + 1)
            sp.dma_start(xT3, xT3_d.rearrange("b p n -> p b n")).then_inc(xT3_loaded, 16)

            def load_up(m):
                if m >= 3:
                    sp.wait_ge(up_full[(m - 3) % 2], 4 * ((m - 3) // 2 + 1))
                sp.dma_start(se_w[m % 3], se_up[m, :, :, :]).then_inc(se_loaded[m % 3], 16)

            for m in range(3):
                load_up(m)
            sp.dma_start(xn3[0:S], xn3_d.rearrange("b s d -> s b d")).then_inc(xn3_loaded, 16)
            sp.dma_start(acc[0:S], x2_d.rearrange("b s d -> s b d")).then_inc(acc_loaded, 16)
            sp.dma_start(w_down, se_down.rearrange("(c p) n -> p c n", p=P)).then_inc(down_loaded, 16)
            for m in range(3, MC):
                load_up(m)
            def load_13(r, turn, e):
                sp.wait_ge(up1_full[r], turn + 1)
                sp.sem_inc(load_gate, 1)
                sp.dma_start(w13_s[r], w13[e, :, :, :]).then_inc(w13_loaded[r], 16)

            def load_rows(r, turn, e):
                sp.wait_ge(xst_full[r], turn + 1)
                sp.sem_inc(load_gate, 1)
                sp.dma_start(xs_s[r], xs_d[bass.ds(e * T, T), :]).then_inc(xs_loaded[r], 16)

            def load_2(r, turn, e):
                sp.wait_ge(y_full[r], turn + 1)
                sp.sem_inc(load_gate, 1)
                sp.dma_start(w2_s[r][:, 0:2, :], w2[e, 0:256, :].rearrange("(c p) n -> p c n", p=P)).then_inc(w2_loaded[r], 16)
                sp.dma_start(w2_s[r][0:96, 2, :], w2[e, 256:I, :]).then_inc(w2_loaded[r], 16)

            load_13(0, 0, 0)
            load_13(1, 0, 1)
            load_2(0, 0, 0)
            load_2(1, 0, 1)
            sp.wait_ge(scattered, 16 * B * TOPK)
            load_rows(0, 0, 0)
            load_rows(1, 0, 1)
            load_rows(0, 1, 2)
            load_rows(1, 1, 3)
            load_13(0, 1, 2)
            with sp.Fori(0, E // 2 - 2) as i:
                load_rows(0, i + 2, i * 2 + 4)
                load_13(1, i + 1, i * 2 + 3)
                load_2(0, i + 1, i * 2 + 2)
                load_rows(1, i + 2, i * 2 + 5)
                load_13(0, i + 2, i * 2 + 4)
                load_2(1, i + 1, i * 2 + 3)
            load_13(1, E // 2 - 1, E - 1)
            load_2(0, E // 2 - 1, E - 2)
            load_2(1, E // 2 - 1, E - 1)
            sp.wait_ge(slots_ready, 1)
            sp.wait_ge(up1_full[1], E // 2 + 1)
            sp.wait_ge(y_full[0], E // 2 + 1)
            sp.wait_ge(xst_full[0], E // 2 + 1)
            count = sp.value_load(ov_i[0:1, NOV:NOV + 1], min_val=0, max_val=NOV)
            with sp.Fori(0, NOV) as t:
                with sp.If(count > t):
                    e = sp.value_load(ov_i[0:1, bass.ds(t, 1)], min_val=0, max_val=E - 1)
                    sp.wait_ge(o_y, t + 1)
                    sp.sem_inc(load_gate, 1)
                    sp.dma_start(w13_s[0], w13[e, :, :, :]).then_inc(o_w, 16)
                    sp.dma_start(xs_s[0], xs_d[bass.ds(t * T + E * T, T), :]).then_inc(o_w, 16)
                    sp.dma_start(w2_s[0][:, 0:2, :], w2[e, 0:256, :].rearrange("(c p) n -> p c n", p=P)).then_inc(o_w, 16)
                    sp.dma_start(w2_s[0][0:96, 2, :], w2[e, 256:I, :]).then_inc(o_w, 16)
            for b in range(B):
                sp.wait_ge(out_ready, b + 1)
                sp.dma_start(out[b, :, :], acc[0:S, b, :]).then_inc(out_stored, 16)
            sp.wait_ge(out_stored, 16 * B)

        @block.gpsimd
        def _(pool):
            for s in [signal.sem for signal in Signal.all] + by_turns:
                pool.sem_inc(s, 1)
            nc.gpsimd.memset(zero[:], 0.0).then_inc(pool_pre, 1)
            nc.gpsimd.memset(ones[:], 1.0).then_inc(pool_pre, 1)
            nc.gpsimd.iota(iota_e[:], pattern=[[1, E]], base=0, channel_multiplier=0,
                           allow_small_or_imprecise_dtypes=True).then_inc(consts_ready, 1)
            nc.gpsimd.iota(iota_n[:], pattern=[[1, NOV]], base=0, channel_multiplier=0,
                           allow_small_or_imprecise_dtypes=True).then_inc(consts_ready, 1)
            pool.wait_ge(pool_pre, 2)
            nc.gpsimd.affine_select(out=ident[:], in_=ones[:], compare_op=ALU.is_equal, fill=0.0, base=0,
                                    pattern=[[-1, P]], channel_multiplier=1).then_inc(consts_ready, 1)
            nc.gpsimd.affine_select(out=tri[:], in_=ones[:], compare_op=ALU.is_gt, fill=0.0, base=0,
                                    pattern=[[1, P]], channel_multiplier=-1).then_inc(consts_ready, 1)
            for width, m, n in ((HD, blk_k, 4), (DCA, blk_v, 8)):
                nc.gpsimd.affine_select(out=m, in_=ones[:, 0:n], compare_op=ALU.is_ge, fill=0.0, base=0,
                                        pattern=[[-width, n]], channel_multiplier=1).then_inc(pool_pre, 1)
            pool.wait_ge(pool_pre, 4)
            for width, m, n in ((HD, blk_k, 4), (DCA, blk_v, 8)):
                nc.gpsimd.affine_select(out=m, in_=m, compare_op=ALU.is_ge, fill=0.0, base=width - 1,
                                        pattern=[[width, n]], channel_multiplier=-1).then_inc(pool_pre, 1)
            pool.wait_ge(pool_pre, 6)
            zrow = zero[:, :].rearrange("p (a d) -> p a d", a=1).to_broadcast([P, 12, D])
            for n in range((E + NOV) // 12):
                pool.dma_start(xs_d[n * 12 * T:(n + 1) * 12 * T, :].rearrange("(a p) d -> p a d", p=P),
                               zrow).then_inc(zeroed, 16)
            for n in range(NOV // 12):
                pool.dma_start(ys_d[(E + n * 12) * T:(E + n * 12 + 12) * T, :].rearrange("(a p) d -> p a d", p=P),
                               zrow).then_inc(zeroed, 16)
            pool.wait_ge(dca_n, 2)
            pool.dma_start(vd_d, vd_s).then_inc(vd_stored, 16)
            pool.wait_ge(vd_stored, 16)
            vsrc = vd_d.rearrange("(b r) (c h e) -> r b c h e", b=B, c=2, h=8)
            for h in range(8):
                for c in range(2):
                    pool.dma_start(vd_all[h * DCA:(h + 1) * DCA, :, c, :], vsrc[:, :, c, h, :]).then_inc(vd_loaded, 16)
            pool.wait_ge(pre_load, 16 * 12)
            pool.wait_ge(vd_loaded, 16 * 16)
            pool.wait_ge(kd_ready, 1)
            with pool.Fori(0, PAIRS) as i:
                for j in range(2):
                    pool.wait_ge(x_loaded[j], i * 16 + 16)
                    pool.wait_ge(x2_stored[j], i * 16 + 1)
                    nc.gpsimd.tensor_tensor(xr[j][0:S, :], x_in[j][0:S, :], bout_bc[0:S, :], ALU.add).then_inc(xr_ready.sem, 1)
                for j in range(2):
                    pool.wait_ge(full[6].sem, full[6].before(i))
                    pool.wait_ge(full[7].sem, full[7].before(i))
                    pool.wait_ge(full[3].sem, full[3].before(i))
                    pool.wait_ge(full[2].sem, full[2].before(i))
                    kd_b = kd_all[:, :, bass.ds((i * 2 + j) * DCA, DCA)]
                    for c in range(DC):
                        nc.gpsimd.tensor_tensor(kdb[j][:, c, :, :],
                                                kd_all[:, c:c + 1, bass.ds((i * 2 + j) * DCA, DCA)].to_broadcast([P, 4, DCA]),
                                                blk_k.rearrange("p (a b) -> p a b", b=1).to_broadcast([P, 4, DCA]), ALU.mult)
                    for c in range(2):
                        last = nc.gpsimd.tensor_tensor(vdb[j][:, c, :, :],
                                                       vd_all[:, bass.ds(i * 2 + j, 1), c, :].to_broadcast([P, 8, HD]),
                                                       blk_v.rearrange("p (a b) -> p a b", b=1).to_broadcast([P, 8, HD]), ALU.mult)
                    last.then_inc(db_ready.sem, 1)
                for j in range(2):
                    for g in range(G):
                        n = j * G + g
                        pool.wait_ge(rec_ready.sem, rec_ready.at(i, (j, g)))
                        nc.gpsimd.tensor_tensor(pr[n % NP_][0:S], pr[n % NP_][0:S],
                                                prec[j][0:S, g, :].rearrange("p (a b) -> p a b", b=1).to_broadcast([S, KV, S]),
                                                ALU.mult).then_inc(p_ready.sem, 1)
                for j in range(2):
                    pool.wait_ge(xn_ready.sem, xn_ready.at(i, (2, j)))
                    nc.gpsimd.tensor_tensor(xr[j][0:S, :], xr[j][0:S, :], bo_bc[0:S, :], ALU.add).then_inc(xr_ready.sem, 1)
            pool.wait_ge(slots_ready, 1)
            pool.wait_ge(xn3_loaded, 16)
            pool.wait_ge(zeroed, 16 * ((E + 2 * NOV) // 12))
            for b in range(B):
                for k in range(TOPK):
                    n = b * TOPK + k
                    pool.indirect_dma_start(out=xs_d, out_offset=bass.IndirectOffsetOnAxis(ap=slot_u[0:S, n:n + 1], axis=0),
                                            in_=xn3[0:S, b, :], in_offset=None).then_inc(scattered, 16)
            for r in range(2):
                pool.wait_ge(y_stored[r], 16 * (E // 2) + 1)
            count = pool.value_load(ov_i[0:1, NOV:NOV + 1], min_val=0, max_val=NOV)
            with pool.Fori(0, NOV) as t:
                with pool.If(count > t):
                    pool.wait_ge(o_st, t * 16 + 17)
            for n in range(B * TOPK):
                if n >= 4:
                    pool.wait_ge(added[n % 4], n // 4)
                pool.indirect_dma_start(out=xn3[0:S, n % 4, :], out_offset=None, in_=ys_d,
                                        in_offset=bass.IndirectOffsetOnAxis(ap=slot_u[0:S, n:n + 1], axis=0)).then_inc(gathered[n % 4], 16)

        @block.tensor
        def _(pe):
            pe.wait_ge(consts_ready, 4)
            pe.wait_ge(pre_load, 16 * 12)
            pe.wait_ge(weights_centred, 3)
            for half in range(2):
                for c in range(CC):
                    last = nc.tensor.matmul(bank(half), c_dca[:, c, :], w_dca[:, c, half * D:(half + 1) * D],
                                            start=(c == 0), stop=(c == CC - 1))
            last.then_inc(dca_mm, 1)
            pe.wait_ge(dca_n, 3)
            for c in range(DC):
                last = nc.tensor.transpose(ps[:, 4, c * P:(c + 1) * P], t0[:, c * P:(c + 1) * P], ident[:])
            last.then_inc(dca_t, 1)
            pe.wait_ge(kd_ready, 1)
            for w in w_loaded.values():
                pe.wait_ge(w, 16)

            with pe.Fori(0, PAIRS) as i:
                order = iter(fills)

                def begin(*key):
                    if key != ("ctx", 0) and key != ("ctx", 1):
                        k, n = next(order)
                        assert k == key, (k, key)
                    n = bank_of[key]
                    pe.wait_ge(free[n].sem, free[n].prior(i, key))
                    return n

                def end(ins, *key):
                    ins.then_inc(full[bank_of[key]].sem, 1)

                def transpose_x(name, n, j):
                    pe.wait_ge(xn_ready.sem, xn_ready.at(i, (n, j)))
                    k = begin(name, j)
                    for c in range(DC):
                        last = nc.tensor.transpose(ps[:, k, c * S:(c + 1) * S], xn[j][0:S, c * P:(c + 1) * P], ident[0:S, 0:S])
                    end(last, name, j)

                def project(key, m, lhs, w, cols, n_c):
                    k = begin(*key)
                    for c in range(n_c):
                        last = nc.tensor.matmul(ps[0:m, k, 0:cols[1] - cols[0]], lhs(c), w[:, c, cols[0]:cols[1]],
                                                start=(c == 0), stop=(c == n_c - 1))
                    end(last, *key)

                def kv_project(j, c):
                    if c == 0:
                        pe.wait_ge(c_loaded[j], i * 16 + 16)
                    rows = lambda a: c_in[j][:, a, c * LC:(c + 1) * LC]
                    project(("kx", j, c), LC, rows, w_kv, (0, D), CC)
                    project(("vx", j, c), LC, rows, w_kv, (D, 2 * D), CC)
                    n = KV_UNITS.index((j, c))
                    if n:
                        kv_transpose(*KV_UNITS[n - 1])

                def kv_transpose(j, c):
                    pe.wait_ge(kn_ready.sem, kn_ready.at(i, (j, c)))
                    k = begin("kxT", j, c)
                    for a in range(DC):
                        last = nc.tensor.transpose(ps[:, k, a * LC:(a + 1) * LC], kn[0:LC, a * P:(a + 1) * P], ident[0:LC, 0:LC])
                    end(last, "kxT", j, c)

                for j in range(2):
                    transpose_x("xT1", 1, j)
                for j in range(2):
                    wait_drained(pe, i, "xT1", j)
                    rows = lambda a: xT[j][:, a, :]
                    project(("q", j), S, rows, w_attn, (0, D), DC)
                    project(("k", j), S, rows, w_attn, (D, QK), DC)
                    project(("v", j), S, rows, w_attn, (QK, QK + D), DC)
                    kv_project(j, 0)
                for j in range(2):
                    wait_drained(pe, i, "q", j)
                    wait_drained(pe, i, "k", j)
                    k = begin("qT", j)
                    for c in range(KV):
                        last = nc.tensor.transpose(ps[:, k, c * S:(c + 1) * S], qr[j][0:S, c * P:(c + 1) * P], ident[0:S, 0:S])
                    end(last, "qT", j)
                    k = begin("kT", j)
                    for c in range(KV):
                        last = nc.tensor.transpose(ps[:, k, c * S:(c + 1) * S], kr[j][0:S, c, :, :].rearrange("p a b -> p (a b)"), ident[0:S, 0:S])
                    end(last, "kT", j)
                    wait_drained(pe, i, "qT", j)
                    wait_drained(pe, i, "kT", j)
                    ks = [begin("s", j, g) for g in range(G)]
                    for c in range(KV):
                        for g in range(G):
                            rows_ = slice(g * HD, (g + 1) * HD)
                            last = nc.tensor.matmul(ps[0:S, ks[g], c * S:(c + 1) * S], qT[j][rows_, c, :], kT[j][rows_, c, :],
                                                    start=True, stop=True)
                            if c == KV - 1:
                                end(last, "s", j, g)
                    kv_project(j, 1)
                for j in range(2):
                    for g in range(G):
                        n = j * G + g
                        pe.wait_ge(p_ready.sem, p_ready.at(i, (j, g)))
                        k = begin("pT", j, g)
                        for c in range(KV):
                            last = nc.tensor.transpose(ps[0:S, k, c * S:(c + 1) * S], pr[n % NP_][0:S, c, :], ident[0:S, 0:S])
                        end(last, "pT", j, g)
                    kv_project(j, 2)
                    for g in range(G):
                        wait_drained(pe, i, "pT", j, g)
                    wait_drained(pe, i, "v", j)

                    def values(c):
                        k = begin("pv", j, c)
                        last = nc.tensor.matmul(ps[:, k, 0:G * S], v_s[j][0:S, c * VD:(c + 1) * VD],
                                                pT[0:S, c, :, :].rearrange("p a b -> p (a b)"), start=True, stop=True)
                        end(last, "pv", j, c)

                    def attend_out(c):
                        wait_drained(pe, i, "pv", j, c)
                        for g in range(G):
                            last = nc.tensor.matmul(ps[0:S, j, :], cT[c % 2][:, g, :], w_out[:, c * G + g, :],
                                                    start=(c == 0 and g == 0), stop=(c == KV - 1 and g == G - 1))
                        return last

                    values(0)
                    values(1)
                    pe.wait_ge(free[j].sem, free[j].prior(i, ("o", j)))
                    attend_out(0).then_inc(o_part.sem, 1)
                    values(2)
                    attend_out(1).then_inc(o_part.sem, 1)
                    values(3)
                    attend_out(2)
                    begin("o", j)
                    end(attend_out(3), "o", j)
                for j in range(2):
                    transpose_x("xT2", 2, j)
                for j in range(2):
                    wait_drained(pe, i, "xT2", j)
                    project(("xq", j), S, lambda a: xT[j][:, a, :], w_q, (0, D), DC)
                kv_transpose(*KV_UNITS[-1])
                for j in range(2):
                    pe.wait_ge(qx_ready.sem, qx_ready.at(i, j))
                    k = begin("xqT", j)
                    for c in range(DC):
                        last = nc.tensor.transpose(ps[:, k, c * S:(c + 1) * S], qx[0:S, c * P:(c + 1) * P], ident[0:S, 0:S])
                    end(last, "xqT", j)
                for j in range(2):
                    wait_drained(pe, i, "xqT", j)
                    pe.wait_ge(db_ready.sem, db_ready.at(i, j))
                    k = begin("ds", j)
                    for c in range(DC):
                        last = nc.tensor.matmul(ps[0:S, k, c * 64:(c + 1) * 64], xqT[j][:, c, :],
                                                kdb[j][:, c, :, :].rearrange("p a b -> p (a b)"), start=True, stop=True)
                    end(last, "ds", j)
                for j in range(2):
                    pe.wait_ge(dexp_ready.sem, dexp_ready.at(i, j))
                    k = begin("dpT", j)
                    for c in range(2):
                        last = nc.tensor.transpose(ps[:, k, c * S:(c + 1) * S],
                                                   dp[j][0:S, c * 8:(c + 1) * 8, :].rearrange("p a b -> p (a b)"), ident[0:S, 0:S])
                    end(last, "dpT", j)
                for j in range(2):
                    wait_drained(pe, i, "dpT", j)
                    k = begin("dpv", j)
                    for c in range(2):
                        last = nc.tensor.matmul(ps[0:S, k, c * 256:(c + 1) * 256], dpT[j][:, c, :],
                                                vdb[j][:, c, :, :].rearrange("p a b -> p (a b)"), start=True, stop=True)
                    end(last, "dpv", j)
                for j, c in KV_UNITS:
                    wait_drained(pe, i, "kxT", j, c)
                    wait_drained(pe, i, "vx", j, c)
                for n in range(2 * H + 4):
                    if n < 2 * H:
                        j, h = n // H, n % H
                        k = begin("xs", n)
                        rows_ = slice((h % 4) * HD, (h % 4 + 1) * HD)
                        end(nc.tensor.matmul(ps[0:S, k, 0:LM], xqT[j][rows_, h // 4, :], kxT[j][rows_, h // 4, :],
                                             start=True, stop=True), "xs", n)
                    if 2 <= n < 2 * H + 2:
                        m = n - 2
                        wait_drained(pe, i, "xs", m)
                        k = begin("xpT", m)
                        for c in range(LN_):
                            last = nc.tensor.transpose(ps[0:LC, k, c * S:(c + 1) * S], xp[m % NX][0:S, c * LC:(c + 1) * LC], ident[0:S, 0:S])
                        end(last, "xpT", m)
                    if n >= 4:
                        m = n - 4
                        j, h = m // H, m % H
                        wait_drained(pe, i, "xpT", m)
                        if h == 0:
                            pe.wait_ge(free[6 + j].sem, free[6 + j].prior(i, ("ctx", j)))
                        for c in range(LN_):
                            last = nc.tensor.matmul(ps[0:S, 6 + j, h * HD:(h + 1) * HD], xpT[m % NX][0:LC, c, :],
                                                    vx[j][0:LC, c, h * HD:(h + 1) * HD], start=(c == 0), stop=(c == LN_ - 1))
                        if h < H - 1:
                            last.then_inc(xpv_done.sem, 1)
                        else:
                            next(order)
                            end(last, "ctx", j)
                for j in range(2):
                    pe.wait_ge(cx_ready.sem, cx_ready.at(i, j))
                    k = begin("cT", j)
                    for c in range(DC):
                        last = nc.tensor.transpose(ps[:, k, c * S:(c + 1) * S], cx[j][0:S, c * P:(c + 1) * P], ident[0:S, 0:S])
                    end(last, "cT", j)
                for j in range(2):
                    wait_drained(pe, i, "cT", j)
                    project(("xo", j), S, lambda a: cxT[j][:, a, :], w_o, (0, D), DC)
                for j in range(2):
                    transpose_x("xT3", 3, j)
                for j in range(2):
                    wait_drained(pe, i, "xT3", j)
                    project(("gate", j), S, lambda a: xT[j][:, a, :], w_gate, (0, NG), DC)

            for n in range(8):
                pe.wait_ge(free[n].sem, free[n].before(PAIRS))
            pe.wait_ge(xT3_loaded, 16)
            for m in range(MC):
                pe.wait_ge(se_loaded[m % 3], 16 * (m // 3 + 1))
                for half in range(2):
                    if m >= 2:
                        pe.wait_ge(hs_ready[m % 2], 2 * ((m - 2) // 2) + half + 1)
                    for gu in range(2):
                        for c in range(DC):
                            tok = xT3[:, half * 4:(half + 1) * 4, c * S:(c + 1) * S]
                            last = nc.tensor.matmul(ps[:, (m % 2) * 4 + half * 2 + gu, 0:400].rearrange("p (a b) -> p a b", a=4),
                                                    se_w[m % 3][:, c, gu * P:(gu + 1) * P], tok,
                                                    start=(c == 0), stop=(c == DC - 1))
                        last.then_inc(up_full[m % 2], 1)
            pe.wait_ge(mask_ready, 1)
            pe.wait_ge(hs_ready[0], 2 * ((MC + 1) // 2))
            pe.wait_ge(hs_ready[1], 2 * (MC // 2))
            for b in range(B):
                for a in range(b + 1):
                    nc.tensor.matmul(ps[0:S, 0, b * E:(b + 1) * E], (tri if a == b else ones)[0:S, 0:S], mask[0:S, a, :],
                                     start=(a == 0), stop=(a == b))
            for b in range(B):
                last = nc.tensor.matmul(ps[:, 1, 0:E], ones[0:S, :], mask[0:S, b, :], start=(b == 0), stop=(b == B - 1))
            last.then_inc(rank_full, 1)
            pe.wait_ge(down_loaded, 16)
            for b in range(B):
                if b >= 2:
                    pe.wait_ge(dn_free, b - 1)
                for m in range(MC):
                    last = nc.tensor.matmul(ps[0:S, 2 + b % 2, :], hT_all[:, m, b * S:(b + 1) * S], w_down[:, m, :],
                                            start=(m == 0), stop=(m == MC - 1))
                last.then_inc(dn_full, 1)
            pe.wait_ge(slots_ready, 1)
            pe.wait_ge(dn_free, B)

            def rows_T(r, turn):
                pe.wait_ge(xs_loaded[r], turn * 16 + 16)
                pe.wait_ge(xst_ready[r], turn + 1)
                for c in range(DC):
                    last = nc.tensor.transpose(ps[:, r, c * T:(c + 1) * T], xs_s[r][:, c * P:(c + 1) * P], ident[:])
                last.then_inc(xst_full[r], 1)

            def gate_up(r, turn):
                pe.wait_ge(w13_loaded[r], turn * 16 + 16)
                pe.wait_ge(xst_ready[r], turn + 2)
                pe.wait_ge(h_ready[r], turn + 1)
                gate_up_products(r)[-1].then_inc(up1_full[r], 1)

            def gate_up_products(r):
                done = []
                for gu in range(2):
                    for n, w in enumerate(IC):
                        at = gu * I + n * P
                        for c in range(DC):
                            done.append(nc.tensor.matmul(ps[0:w, 2 + 2 * gu + r, n * T:(n + 1) * T], w13_s[r][:, c, at:at + w],
                                                         xsT[r][:, c, :], start=(c == 0), stop=(c == DC - 1)))
                return done

            def down_products(r):
                for n, w in enumerate(IC):
                    last = nc.tensor.matmul(ps[:, 6 + r, :], hT[r][0:w, n, :], w2_s[r][0:w, n, :],
                                            start=(n == 0), stop=(n == len(IC) - 1))
                return last

            def down(r, turn):
                pe.wait_ge(w2_loaded[r], turn * 32 + 32)
                pe.wait_ge(h_ready[r], turn + 2)
                pe.wait_ge(y_ready[r], turn + 1)
                down_products(r).then_inc(y_full[r], 1)

            rows_T(0, 0)
            rows_T(1, 0)
            gate_up(0, 0)
            with pe.Fori(0, E // 2 - 1) as i:
                rows_T(0, i + 1)
                gate_up(1, i)
                down(0, i)
                rows_T(1, i + 1)
                gate_up(0, i + 1)
                down(1, i)
            gate_up(1, E // 2 - 1)
            down(0, E // 2 - 1)
            down(1, E // 2 - 1)
            pe.wait_ge(y_ready[0], E // 2 + 1)
            count = pe.value_load(ov_i[0:1, NOV:NOV + 1], min_val=0, max_val=NOV)
            with pe.Fori(0, NOV) as t:
                with pe.If(count > t):
                    pe.wait_ge(o_w, t * 64 + 64)
                    pe.wait_ge(o_yc, t + 1)
                    for c in range(DC):
                        last = nc.tensor.transpose(ps[:, 0, c * T:(c + 1) * T], xs_s[0][:, c * P:(c + 1) * P], ident[:])
                    last.then_inc(o_t, 1)
                    pe.wait_ge(o_tc, t + 1)
                    gate_up_products(0)[-1].then_inc(o_g, 1)
                    pe.wait_ge(o_h, t + 1)
                    down_products(0).then_inc(o_y, 1)

        @block.scalar
        def _(act):
            act.wait_ge(dca_t, 1)
            act.wait_ge(weights_centred, 4)
            for c in range(DC):
                last = nc.scalar.activation(kd_all[:, c, :], ps[:, 4, c * P:(c + 1) * P], ACT.Identity, bias=nrm[:, 5:6], scale=nrm[:, 4:5])
            last.then_inc(kd_ready, 1)

            with act.Fori(0, PAIRS) as i:
                def filled(*key):
                    return wait_filled(act, i, *key)

                def x_T(name, j):
                    k = filled(name, j)
                    nc.scalar.activation(xT[j].rearrange("p a b -> p (a b)"), ps[:, k, 0:DC * S], ACT.Copy).then_inc(free[k].sem, 1)

                def kv(n):
                    if n < 0:
                        return
                    j, c = KV_UNITS[n]
                    k = filled("kxT", j, c)
                    nc.scalar.activation(kxT[j][:, :, c * LC:(c + 1) * LC], ps[:, k, 0:DC * LC].rearrange("p (a b) -> p a b", a=DC),
                                         ACT.Identity, bias=nrm[:, 3:4], scale=nrm[:, 2:3]).then_inc(free[k].sem, 1)

                for j in range(2):
                    act.wait_ge(full[2 + j].sem, full[2 + j].before(i))
                    act.wait_ge(xT_stored[j], i * 16 + 1)
                    x_T("xT1", j)
                for j in range(2):
                    k = filled("v", j)
                    act.wait_ge(full[6].sem, full[6].before(i))
                    act.wait_ge(full[7].sem, full[7].before(i))
                    nc.scalar.activation(v_s[j][0:S, :], ps[0:S, k, :], ACT.Copy).then_inc(free[k].sem, 1)
                    act.wait_ge(xpv_done.sem, xpv_done.before(i))
                    kv(j - 1)
                for j in range(2):
                    k = filled("qT", j)
                    nc.scalar.activation(qT[j].rearrange("p a b -> p (a b)"), ps[:, k, 0:DC * S], ACT.Copy).then_inc(free[k].sem, 1)
                    for g in range(G):
                        n = j * G + g
                        k = filled("s", j, g)
                        act.wait_ge(max_ready.sem, max_ready.at(i, (j, g)))
                        for c in range(KV):
                            last = nc.scalar.activation(pr[n % NP_][0:S, c, :], ps[0:S, k, c * S:(c + 1) * S], ACT.Exp,
                                                        bias=nmax[j][0:S, g, c:c + 1], scale=1.0, accum_out=psum_[j][0:S, g, c:c + 1])
                        last.then_inc(free[k].sem, 1)
                    kv(2 + j - 1)
                for j in range(2):
                    for g in (1, 3):
                        k = filled("pT", j, g)
                        if j:
                            act.wait_ge(full[7].sem, full[7].at(i, ("pv", 0, 3)))
                        nc.scalar.activation(pT[0:S, :, g, :], ps[0:S, k, 0:KV * S].rearrange("p (a b) -> p a b", a=KV),
                                             ACT.Copy).then_inc(free[k].sem, 1)
                    kv(4 + j - 1)
                    for c in (1, 3):
                        k = filled("pv", j, c)
                        if c == 3:
                            act.wait_ge(o_part.sem, o_part.at(i, (j, 1)))
                        elif j:
                            act.wait_ge(full[0].sem, full[0].at(i, ("o", 0)))
                        nc.scalar.activation(cT[1].rearrange("p a b -> p (a b)"), ps[:, k, 0:G * S], ACT.Copy).then_inc(free[k].sem, 1)
                for j in range(2):
                    x_T("xT2", j)
                kv(5)
                for j in range(2):
                    k = filled("xqT", j)
                    act.wait_ge(xpv_done.sem, xpv_done.before(i))
                    nc.scalar.activation(xqT[j].rearrange("p a b -> p (a b)"), ps[:, k, 0:DC * S], ACT.Identity, bias=nrm[:, 1:2],
                                         scale=nrm[:, 0:1]).then_inc(free[k].sem, 1)
                for j in range(2):
                    wait_drained(act, i, "ds", j)
                    nc.scalar.activation(dp[j][0:S].rearrange("p a b -> p (a b)"), dp[j][0:S].rearrange("p a b -> p (a b)"), ACT.Exp).then_inc(dexp_ready.sem, 1)
                for j in range(2):
                    k = filled("dpT", j)
                    nc.scalar.activation(dpT[j].rearrange("p a b -> p (a b)"), ps[:, k, 0:2 * S], ACT.Copy).then_inc(free[k].sem, 1)
                for n in range(2 * H):
                    j, h = n // H, n % H
                    k = filled("xs", n)
                    act.wait_ge(xmax_ready.sem, xmax_ready.at(i, n))
                    if n >= NX:
                        kk = bank_of[("xpT", n - NX)]
                        act.wait_ge(full[kk].sem, full[kk].at(i, ("xpT", n - NX)))
                    nc.scalar.activation(xp[n % NX][0:S, :], ps[0:S, k, 0:LM], ACT.Exp, bias=xnm[0:S, j, h:h + 1], scale=1.0,
                                         accum_out=xsum[0:S, j, h:h + 1]).then_inc(free[k].sem, 1)
                for j in range(2):
                    k = filled("cT", j)
                    nc.scalar.activation(cxT[j].rearrange("p a b -> p (a b)"), ps[:, k, 0:DC * S], ACT.Copy).then_inc(free[k].sem, 1)
                for j in range(2):
                    x_T("xT3", j)
                for j in range(2):
                    k = filled("gate", j)
                    nc.scalar.activation(lg_all[0:S, bass.ds(i * 2 + j, 1), :], ps[0:S, k:k + 1, 0:NG], ACT.Copy).then_inc(free[k].sem, 1)

            act.wait_ge(r_in, 1)
            for b in range(B):
                nc.scalar.activation(rsm[0:S, 1, b, 0:TOPK], rsm[0:S, 0, b, 0:TOPK], ACT.Exp, bias=rsm[0:S, 2, b, 0:1])
                nc.scalar.activation(oh[0:S, b, :], lg_all[0:S, b, 0:E], ACT.Exp, bias=rsm[0:S, 2, b, 0:1],
                                            accum_out=rsm[0:S, 3, b, 0:1])
            nc.scalar.activation(rsm[0:S, 6, :, 2:3], lg_all[0:S, :, E:NG], ACT.Sigmoid).then_inc(r_act, 1)
            for m in range(MC):
                for half in range(2):
                    act.wait_ge(up_full[m % 2], 4 * (m // 2) + 2 * half + 1)
                    if m:
                        act.wait_ge(hs_ready[(m - 1) % 2], 2 * ((m - 1) // 2) + half + 1)
                    nc.scalar.activation(s_sh[half], ps[:, (m % 2) * 4 + half * 2, 0:400], ACT.Silu).then_inc(silu_ready[m % 2], 1)

            def silu(r, turn):
                act.wait_ge(up1_full[r], turn + 2)
                act.wait_ge(h_ready[r], turn + 1)
                silu_parts(r).then_inc(sl_ready[r], 1)

            def silu_parts(r):
                nc.scalar.activation(sl[r][:, 0:2, :].rearrange("p a b -> p (a b)"), ps[:, 2 + r, 0:2 * T], ACT.Silu)
                return nc.scalar.activation(sl[r][0:96, 2, :], ps[0:96, 2 + r, 2 * T:3 * T], ACT.Silu)

            def store(r, turn, e):
                act.wait_ge(y_full[r], turn + 2)
                act.wait_ge(y_stored[r], turn * 16 + 1)
                nc.scalar.activation(y_s[r], ps[:, 6 + r, :], ACT.Copy).then_inc(y_ready[r], 1)
                act.wait_ge(y_ready[r], turn + 2)
                act.dma_start(ys_d[bass.ds(e * T, T), :], y_s[r]).then_inc(y_stored[r], 16)

            silu(0, 0)
            with act.Fori(0, E // 2 - 1) as i:
                silu(1, i)
                store(0, i, i * 2)
                silu(0, i + 1)
                store(1, i, i * 2 + 1)
            silu(1, E // 2 - 1)
            store(0, E // 2 - 1, E - 2)
            store(1, E // 2 - 1, E - 1)
            for r in range(2):
                act.wait_ge(y_stored[r], 16 * (E // 2) + 1)
            act.wait_ge(slots_ready, 1)
            count = act.value_load(ov_i[0:1, NOV:NOV + 1], min_val=0, max_val=NOV)
            with act.Fori(0, NOV) as t:
                with act.If(count > t):
                    act.wait_ge(o_g, t + 1)
                    silu_parts(0).then_inc(o_s, 1)
                    act.wait_ge(o_y, t + 2)
                    act.wait_ge(o_st, t * 16 + 1)
                    nc.scalar.activation(y_s[0], ps[:, 6, :], ACT.Copy).then_inc(o_yc, 1)
                    act.wait_ge(o_yc, t + 2)
                    act.dma_start(ys_d[bass.ds(t * T + E * T, T), :], y_s[0]).then_inc(o_st, 16)

        @block.vector
        def _(dve):
            count_ = [0, None, 0]

            def link(ins):
                ins.then_inc(chain, 1)
                count_[0] += 1
                if count_[1] is None:
                    dve.wait_ge(chain, count_[2] + count_[0])
                else:
                    dve.wait_ge(chain, count_[1] * LINKS + (count_[2] + count_[0]))

            def centre(view, n):
                m = stat[:, 0:n]
                link(nc.vector.tensor_reduce(m, view, AX, ALU.add))
                link(nc.vector.tensor_scalar(m, m, 1.0 / HD, None, ALU.mult))
                return nc.vector.tensor_tensor(view, view, m.rearrange("p (a b) -> p a b", b=1).to_broadcast([P, n, HD]), ALU.subtract)

            def head(v):
                return v.rearrange("p (a b) -> p a b", b=HD)

            dve.wait_ge(pre_load, 16 * 12)
            for c in range(CC):
                last = centre(head(w_dca[:, c, 0:D]), H)
                link(last)
            link(centre(head(bdca_bc[:, 0:D]), H))
            nc.vector.tensor_scalar(nrm[:, 0:2], nrm[:, 0:2], SCALE, None, ALU.mult).then_inc(weights_centred, 3)
            link(centre(head(bkv_bc[:, 0:D]), H))
            link(centre(head(bq_bc), H))
            dve.wait_ge(dca_mm, 1)
            dve.wait_ge(weights_centred, 3)
            link(nc.vector.tensor_tensor(kn, ps[:, 0, :], bdca_bc[:, 0:D], ALU.add))
            nc.vector.tensor_tensor(vd_s, ps[:, 1, :], bdca_bc[:, D:2 * D], ALU.add).then_inc(dca_n, 2)

            def inverse_root(v, work):
                y, minus_half, a = work
                nc.vector.tensor_scalar(y.bitcast(I32), v.bitcast(I32), -0.5, float(0x5f3759df), ALU.mult, ALU.add)
                link(nc.vector.tensor_scalar(minus_half, v, -0.5, None, ALU.mult))
                for n in range(3):
                    link(nc.vector.tensor_tensor(a, y, minus_half, ALU.mult))
                    link(nc.vector.tensor_tensor(a, a, y, ALU.mult))
                    link(nc.vector.scalar_tensor_tensor(out=y if n < 2 else v, in0=a, scalar=1.5, in1=y, op0=ALU.add, op1=ALU.mult))

            def head_norm(src, dst, m):
                link(nc.vector.tensor_tensor(t1[0:m, :], src, src, ALU.mult))
                ss = stat[0:m, 0:H]
                link(nc.vector.tensor_reduce(ss, head(t1[0:m, :]), AX, ALU.add))
                link(nc.vector.tensor_scalar(ss, ss, HD * 1e-6, None, ALU.add))
                inverse_root(ss, [stat[0:m, n * H:(n + 1) * H] for n in (1, 2, 3)])
                return nc.vector.scalar_tensor_tensor(out=head(dst), in0=head(src), scalar=float(HD) ** 0.5,
                                                      in1=ss.rearrange("p (a b) -> p a b", b=1).to_broadcast([m, H, HD]),
                                                      op0=ALU.mult, op1=ALU.mult)

            head_norm(kn[:, :], t0[:, :], P).then_inc(dca_n, 1)
            dve.wait_ge(dca_n, 3)
            for name, view, cc in (("w_kv", w_kv, CC), ("w_q", w_q, DC)):
                dve.wait_ge(w_loaded[name], 16)
                for c in range(cc):
                    last = centre(head(view[:, c, 0:D]), H)
                    link(last)
            dve.sem_inc(weights_centred, 1)
            dve.wait_ge(kd_ready, 1)

            count_[2] = count_[0]
            count_[0] = 0
            with dve.Fori(0, PAIRS) as i:
                count_[1] = i

                def filled(*key):
                    return wait_filled(dve, i, *key)

                last_use = [cx_ready, None]

                def claim(signal, key):
                    sig, k = last_use
                    dve.wait_ge(sig.sem, sig.before(i) if k is None else sig.at(i, k))
                    last_use[:] = [signal, key]

                def layer_norm(src, dst):
                    link(nc.vector.bn_stats(stat_n[0:S, 0:6], src))
                    nc.vector.memset(stat_n[0:S, 15:16], 0.0)
                    link(nc.vector.bn_aggr(stat_n[0:S, 8:10], stat_n[0:S, 0:6]))
                    link(nc.vector.tensor_scalar(stat_n[0:S, 10:11], stat_n[0:S, 9:10], 1e-5, None, ALU.add))
                    inverse_root(stat_n[0:S, 10:11], [stat_n[0:S, n:n + 1] for n in (12, 13, 14)])
                    return nc.vector.tensor_scalar(dst, src, stat_n[0:S, 8:9], stat_n[0:S, 10:11], ALU.subtract, ALU.mult)

                def rope(src, n, table, dst):
                    s3 = src.rearrange("p (a b) -> p a b", b=HD)
                    a3 = t0[0:S, 0:n * HD].rearrange("p (a b) -> p a b", b=HD)
                    b3 = t1[0:S, 0:n * HD].rearrange("p (a b) -> p a b", b=HD)
                    half = HD // 2
                    tab = lambda r, lo, hi: cs[0:S, r:r + 1, lo:hi].to_broadcast([S, n, hi - lo])
                    nc.vector.tensor_tensor(a3, s3, tab(table, 0, HD), ALU.mult)
                    nc.vector.tensor_tensor(b3[:, :, 0:half], s3[:, :, half:HD], tab(table + 1, 0, half), ALU.mult)
                    link(nc.vector.tensor_tensor(b3[:, :, half:HD], s3[:, :, 0:half], tab(table + 1, half, HD), ALU.mult))
                    return dst(a3, b3)

                def kv(j, c):
                    k = filled("kx", j, c)
                    claim(kn_ready, (j, c))
                    nc.vector.tensor_tensor(t0[0:LC, :], ps[0:LC, k, :], bkv_bc[0:LC, 0:D], ALU.add).then_inc(free[k].sem, 1)
                    dve.wait_ge(free[k].sem, free[k].at(i, ("kx", j, c)))
                    prev = KV_UNITS.index((j, c))
                    if prev:
                        pj, pc = KV_UNITS[prev - 1]
                        dve.wait_ge(full[4].sem, full[4].at(i, ("kxT", pj, pc)))
                    head_norm(t0[0:LC, :], kn[0:LC, :], LC).then_inc(kn_ready.sem, 1)
                    k = filled("vx", j, c)
                    nc.vector.tensor_tensor(vx[j][0:LC, c, :], ps[0:LC, k, :], bkv_bc[0:LC, D:2 * D], ALU.add).then_inc(free[k].sem, 1)

                for j in range(2):
                    dve.wait_ge(x_loaded[j], i * 16 + 16)
                    dve.wait_ge(full[4].sem, full[4].before(i))
                    dve.wait_ge(full[5].sem, full[5].before(i))
                    dve.wait_ge(xn_stored[j], i * 16 + 1)
                    dve.wait_ge(xn_ready.sem, xn_ready.prior(i, (1, j)))
                    layer_norm(x_in[j][0:S, :], xn[j][0:S, :]).then_inc(xn_ready.sem, 1)
                for j in range(2):
                    k = filled("q", j)
                    claim(free[bank_of["k", j]], ("k", j))
                    rope(ps[0:S, k, :], H, 0, lambda a, b: nc.vector.tensor_tensor(qr[j][0:S, :].rearrange("p (a b) -> p a b", b=HD), a, b, ALU.add)).then_inc(free[k].sem, 1)
                    k2 = filled("k", j)
                    dve.wait_ge(free[k].sem, free[k].at(i, ("q", j)))

                    def spread(a, b):
                        full_ = lambda v: v.rearrange("p (k g) e -> p k g e", g=1).to_broadcast([S, KV, G, HD])
                        return nc.vector.tensor_tensor(kr[j][0:S], full_(a), full_(b), ALU.add)
                    rope(ps[0:S, k2, 0:KV * HD], KV, 2, spread).then_inc(free[k2].sem, 1)
                    kv(j, 0)
                for j in range(2):
                    k = filled("kT", j)
                    nc.vector.tensor_copy(kT[j].rearrange("p a b -> p (a b)"), ps[:, k, 0:DC * S]).then_inc(free[k].sem, 1)
                    for g in range(G):
                        k = filled("s", j, g)
                        nc.vector.tensor_reduce(nmax[j][0:S, g, :], ps[0:S, k, 0:KV * S].rearrange("p (a b) -> p a b", a=KV), AX, ALU.max,
                                                negate=True).then_inc(max_ready.sem, 1)
                    for g in range(G):
                        wait_drained(dve, i, "s", j, g)
                        nc.vector.reciprocal(prec[j][0:S, g, :], psum_[j][0:S, g, :]).then_inc(rec_ready.sem, 1)
                    kv(j, 1)
                for j in range(2):
                    for g in (0, 2):
                        k = filled("pT", j, g)
                        if j:
                            dve.wait_ge(full[7].sem, full[7].at(i, ("pv", 0, 3)))
                        nc.vector.tensor_copy(pT[0:S, :, g, :], ps[0:S, k, 0:KV * S].rearrange("p (a b) -> p a b", a=KV)).then_inc(free[k].sem, 1)
                    kv(j, 2)
                    for c in (0, 2):
                        k = filled("pv", j, c)
                        if c == 2:
                            dve.wait_ge(o_part.sem, o_part.at(i, (j, 0)))
                        elif j:
                            dve.wait_ge(full[0].sem, full[0].at(i, ("o", 0)))
                        nc.vector.tensor_copy(cT[0].rearrange("p a b -> p (a b)"), ps[:, k, 0:G * S]).then_inc(free[k].sem, 1)
                    k = filled("o", j)
                    dve.wait_ge(xr_ready.sem, xr_ready.at(i, (0, j)))
                    nc.vector.tensor_tensor(xr[j][0:S, :], xr[j][0:S, :], ps[0:S, k, :], ALU.add).then_inc(free[k].sem, 1)
                    dve.wait_ge(free[k].sem, free[k].at(i, ("o", j)))
                    dve.wait_ge(xn_ready.sem, xn_ready.prior(i, (2, j)))
                    layer_norm(xr[j][0:S, :], xn[j][0:S, :]).then_inc(xn_ready.sem, 1)
                for j in range(2):
                    k = filled("xq", j)
                    claim(qx_ready, j)
                    nc.vector.tensor_tensor(t0[0:S, :], ps[0:S, k, :], bq_bc[0:S, :], ALU.add).then_inc(free[k].sem, 1)
                    dve.wait_ge(free[k].sem, free[k].at(i, ("xq", j)))
                    if j:
                        dve.wait_ge(full[4].sem, full[4].at(i, ("xqT", 0)))
                    head_norm(t0[0:S, :], qx[0:S, :], S).then_inc(qx_ready.sem, 1)
                for j in range(2):
                    k = filled("ds", j)
                    d3 = ps[0:S, k, 0:H * DCA].rearrange("p (a b) -> p a b", a=H)
                    link(nc.vector.tensor_reduce(dnm[0:S, j, :], d3, AX, ALU.max, negate=True))
                    nc.vector.tensor_tensor(dp[j][0:S], d3, dnm[0:S, j, :].rearrange("p (a b) -> p a b", b=1).to_broadcast([S, H, DCA]),
                                            ALU.add).then_inc(free[k].sem, 1)
                for j in range(2):
                    dve.wait_ge(dexp_ready.sem, dexp_ready.at(i, j))
                    link(nc.vector.tensor_reduce(dsum[0:S, j, :], dp[j][0:S], AX, ALU.add))
                    link(nc.vector.reciprocal(drec[0:S, j, :], dsum[0:S, j, :]))
                for j in range(2):
                    k = filled("dpv", j)
                    nc.vector.tensor_tensor(head(cx[j][0:S, :]), head(ps[0:S, k, :]),
                                            drec[0:S, j, :].rearrange("p (a b) -> p a b", b=1).to_broadcast([S, H, HD]), ALU.mult).then_inc(free[k].sem, 1)
                for n in range(2 * H + 2):
                    if n < 2 * H:
                        j, h = n // H, n % H
                        k = filled("xs", n)
                        nc.vector.tensor_reduce(xnm[0:S, j, h:h + 1], ps[0:S, k, 0:LM], AX, ALU.max, negate=True).then_inc(xmax_ready.sem, 1)
                    if n >= 2:
                        m = n - 2
                        k = filled("xpT", m)
                        if m >= NX and (m - NX) % H == H - 1:
                            wait_filled(dve, i, "ctx", 0)
                        elif m >= NX:
                            dve.wait_ge(xpv_done.sem, xpv_done.at(i, m - NX))
                        nc.vector.tensor_copy(xpT[m % NX][0:LC].rearrange("p a b -> p (a b)"), ps[0:LC, k, 0:LN_ * S]).then_inc(free[k].sem, 1)
                for j in range(2):
                    wait_drained(dve, i, "xs", j * H + H - 1)
                    link(nc.vector.reciprocal(xrec[0:S, j, :], xsum[0:S, j, :]))
                    wait_filled(dve, i, "ctx", j)
                    dve.wait_ge(free[6 + j].sem, free[6 + j].at(i, ("dpv", j)))
                    t3 = head(t0[0:S, :])
                    claim(cx_ready, j)
                    nc.vector.tensor_tensor(t3, head(ps[0:S, 6 + j, :]),
                                            xrec[0:S, j, :].rearrange("p (a b) -> p a b", b=1).to_broadcast([S, H, HD]), ALU.mult).then_inc(free[6 + j].sem, 1)
                    dve.wait_ge(free[6 + j].sem, free[6 + j].at(i, ("ctx", j)))
                    nc.vector.tensor_tensor(cx[j][0:S, :], cx[j][0:S, :], t0[0:S, :], ALU.add).then_inc(cx_ready.sem, 1)
                for j in range(2):
                    k = filled("xo", j)
                    dve.wait_ge(xr_ready.sem, xr_ready.at(i, (1, j)))
                    nc.vector.tensor_tensor(xr[j][0:S, :], xr[j][0:S, :], ps[0:S, k, :], ALU.add).then_inc(free[k].sem, 1)
                    dve.wait_ge(free[k].sem, free[k].at(i, ("xo", j)))
                    dve.wait_ge(xn_ready.sem, xn_ready.prior(i, (3, j)))
                    layer_norm(xr[j][0:S, :], xn[j][0:S, :]).then_inc(xn_ready.sem, 1)
                assert count_[0] == LINKS, f"LINKS = {count_[0]}"
            count_[2] += LINKS * PAIRS
            count_[0] = 0
            count_[1] = None

            for k in (2, 3):
                dve.wait_ge(free[k].sem, free[k].before(PAIRS))
            for b in range(B):
                link(nc.vector.max(rsm[0:S, 0, b, :], lg_all[0:S, b, 0:E]))
                link(nc.vector.max_index(idx_u[0:S, b, :], rsm[0:S, 0, b, :], lg_all[0:S, b, 0:E]))
            link(nc.vector.tensor_copy(rsm[0:S, 4], idx_u[0:S]))
            nc.vector.tensor_scalar(rsm[0:S, 2, :, 0:1], rsm[0:S, 0, :, 0:1], -1.0, None, ALU.mult).then_inc(r_in, 1)
            for b in range(B):
                link(nc.vector.tensor_scalar(mask[0:S, b, :], iota_e[0:S, :], rsm[0:S, 4, b, 0:1], None, ALU.is_equal))
                for k in range(1, TOPK):
                    link(nc.vector.scalar_tensor_tensor(out=mask[0:S, b, :], in0=iota_e[0:S, :], scalar=rsm[0:S, 4, b, k:k + 1],
                                                        in1=mask[0:S, b, :], op0=ALU.is_equal, op1=ALU.add))
            dve.sem_inc(mask_ready, 1)
            dve.wait_ge(r_act, 1)
            link(nc.vector.reciprocal(rsm[0:S, 3, :, 1:2], rsm[0:S, 3, :, 0:1]))
            link(nc.vector.tensor_tensor(rsm[0:S, 5, :, 0:TOPK], rsm[0:S, 1, :, 0:TOPK],
                                         rsm[0:S, 3, :, 1:2].to_broadcast([S, B, TOPK]), ALU.mult))

            for m in range(MC):
                for half in range(2):
                    dve.wait_ge(silu_ready[m % 2], 2 * (m // 2) + half + 1)
                    dve.wait_ge(up_full[m % 2], 4 * (m // 2) + 2 * half + 2)
                    nc.vector.tensor_tensor(hT_all[:, m, half * 400:(half + 1) * 400], s_sh[half],
                                            ps[:, (m % 2) * 4 + half * 2 + 1, 0:400], ALU.mult).then_inc(hs_ready[m % 2], 1)

            dve.wait_ge(rank_full, 1)
            cnt, tiles, incl, obase = bts[:, 0, :], bts[:, 1, :], bts[:, 2, :], bts[:, 3, :]
            link(nc.vector.tensor_copy(cnt, ps[:, 1, 0:E]))
            link(nc.vector.tensor_scalar(tiles, cnt, float(T), None, ALU.is_gt))
            for n in range(2, (B * S + T - 1) // T):
                link(nc.vector.scalar_tensor_tensor(out=tiles, in0=cnt, scalar=float(n * T), in1=tiles, op0=ALU.is_gt, op1=ALU.add))
            link(nc.vector.memset(bts[:, 4, :], 1.0))
            link(nc.vector.tensor_tensor_scan(incl, bts[:, 4, :], tiles, 0.0, ALU.mult, ALU.add))
            link(nc.vector.tensor_tensor(obase, incl, tiles, ALU.subtract))
            link(nc.vector.tensor_scalar(obase, obase, float(T), float((E - 1) * T), ALU.mult, ALU.add))
            link(nc.vector.tensor_scalar(base_e[:], iota_e[:], float(T), None, ALU.mult))
            link(nc.vector.tensor_tensor(obase, obase, base_e[:], ALU.subtract))
            rank = ps[0:S, 0, 0:B * E].rearrange("p (a b) -> p a b", a=B)
            over = lambda v: v.rearrange("p (a b) -> p a b", a=1).to_broadcast([S, B, E])
            link(nc.vector.tensor_scalar(slot_e[0:S], rank, float(T), None, ALU.is_ge))
            link(nc.vector.tensor_tensor(slot_e[0:S], slot_e[0:S], over(obase[0:S]), ALU.mult))
            link(nc.vector.tensor_tensor(slot_e[0:S], slot_e[0:S], rank, ALU.add))
            link(nc.vector.tensor_tensor(slot_e[0:S], slot_e[0:S], over(base_e[0:S, :]), ALU.add))
            for k in range(TOPK):
                link(nc.vector.tensor_tensor(oh[0:S], over(iota_e[0:S, :]), rsm[0:S, 4, :, k:k + 1].to_broadcast([S, B, E]), ALU.is_equal))
                link(nc.vector.tensor_tensor(oh[0:S], oh[0:S], slot_e[0:S], ALU.mult))
                link(nc.vector.tensor_reduce(rsm[0:S, 7, :, k:k + 1], oh[0:S], AX, ALU.add))
            link(nc.vector.tensor_copy(slot_u[0:S, :].rearrange("p (a b) -> p a b", a=B), rsm[0:S, 7, :, 0:TOPK]))
            link(nc.vector.tensor_tensor(ovc, incl[0:1, :].rearrange("p (a b) -> p a b", a=1).to_broadcast([1, NOV, E]),
                                         iota_n[0:1, :].rearrange("p (a b) -> p a b", b=1).to_broadcast([1, NOV, E]), ALU.is_le))
            link(nc.vector.tensor_reduce(bts[0:1, 5, 0:NOV], ovc, AX, ALU.add))
            link(nc.vector.tensor_scalar(bts[0:1, 5, 0:NOV], bts[0:1, 5, 0:NOV], float(E - 1), None, ALU.min))
            link(nc.vector.tensor_copy(ov_i[0:1, 0:NOV], bts[0:1, 5, 0:NOV]))
            nc.vector.tensor_copy(ov_i[0:1, NOV:NOV + 1], incl[0:1, E - 1:E]).then_inc(slots_ready, 1)

            dve.wait_ge(acc_loaded, 16)
            for b in range(B):
                dve.wait_ge(dn_full, b + 1)
                nc.vector.scalar_tensor_tensor(out=acc[0:S, b, :], in0=ps[0:S, 2 + b % 2, :], scalar=rsm[0:S, 6, b, 2:3],
                                               in1=acc[0:S, b, :], op0=ALU.mult, op1=ALU.add).then_inc(dn_free, 1)

            def rows_T(r, turn):
                dve.wait_ge(xst_full[r], turn + 2)
                dve.wait_ge(up1_full[r], turn + 1)
                nc.vector.tensor_copy(xsT[r].rearrange("p a b -> p (a b)"), ps[:, r, :]).then_inc(xst_ready[r], 1)

            def hidden_parts(r):
                nc.vector.tensor_tensor(hT[r][:, 0:2, :].rearrange("p a b -> p (a b)"), sl[r][:, 0:2, :].rearrange("p a b -> p (a b)"),
                                        ps[:, 4 + r, 0:2 * T], ALU.mult)
                return nc.vector.tensor_tensor(hT[r][0:96, 2, :], sl[r][0:96, 2, :], ps[0:96, 4 + r, 2 * T:3 * T], ALU.mult)

            def hidden(r, turn):
                dve.wait_ge(sl_ready[r], turn + 1)
                dve.wait_ge(y_full[r], turn + 1)
                hidden_parts(r).then_inc(h_ready[r], 1)

            rows_T(0, 0)
            rows_T(1, 0)
            hidden(0, 0)
            with dve.Fori(0, E // 2 - 1) as i:
                rows_T(0, i + 1)
                hidden(1, i)
                rows_T(1, i + 1)
                hidden(0, i + 1)
            hidden(1, E // 2 - 1)
            dve.wait_ge(slots_ready, 1)
            count = dve.value_load(ov_i[0:1, NOV:NOV + 1], min_val=0, max_val=NOV)
            with dve.Fori(0, NOV) as t:
                with dve.If(count > t):
                    dve.wait_ge(o_t, t + 1)
                    nc.vector.tensor_copy(xsT[0].rearrange("p a b -> p (a b)"), ps[:, 0, :]).then_inc(o_tc, 1)
                    dve.wait_ge(o_s, t + 1)
                    hidden_parts(0).then_inc(o_h, 1)
            dve.wait_ge(dn_free, B)
            for b in range(B):
                for k in range(TOPK):
                    n = b * TOPK + k
                    dve.wait_ge(gathered[n % 4], 16 * (n // 4 + 1))
                    ins = nc.vector.scalar_tensor_tensor(out=acc[0:S, b, :], in0=xn3[0:S, n % 4, :], scalar=rsm[0:S, 5, b, k:k + 1],
                                                         in1=acc[0:S, b, :], op0=ALU.mult, op1=ALU.add)
                    ins.then_inc(added[n % 4], 1)
                    dve.wait_ge(added[n % 4], n // 4 + 1)
                dve.sem_inc(out_ready, 1)


def kernel(x, ctx_1024, L0_attn_W_attn, L0_attn_W_out, L0_attn_b_out, L0_xattn_Wq, L0_xattn_bq, L0_xattn_Wk, L0_xattn_bk,
           L0_xattn_Wv, L0_xattn_bv, L0_xattn_Wkv_dca, L0_xattn_bkv_dca, L0_xattn_qn_w, L0_xattn_qn_b, L0_xattn_kn_w,
           L0_xattn_kn_b, L0_xattn_kn_dca_w, L0_xattn_kn_dca_b, L0_xattn_Wo, L0_xattn_bo, L0_ffn_gate_w,
           L0_ffn_shared_gate_w, L0_ffn_w13, L0_ffn_w2, L0_ffn_se_gate_up_w, L0_ffn_se_down_w):
    import numpy as np
    import concourse.bacc as bacc
    from concourse.bass_utils import run_bass_kernel_spmd

    a = np.asarray
    ctx = a(ctx_1024)
    by_kind = lambda w: w.reshape(w.shape[:-1] + (H, 2, HD)).swapaxes(-3, -2).reshape(w.shape)
    inv = (1.0 / np.float32(10000.0) ** (np.arange(0, HD, 2, dtype=np.float32) / np.float32(HD))).astype(np.float32)
    ang = np.arange(S, dtype=np.float32)[:, None] * inv[None, :]
    cos, sin = np.cos(ang), np.sin(ang)
    table = np.stack([np.concatenate([cos, cos], 1), np.concatenate([-sin, sin], 1)], 1)
    cos_sin = np.concatenate([table * np.float32(SCALE), table], 1).astype(np.float32)
    se_up = a(L0_ffn_se_gate_up_w).T.reshape(DC, P, 2, MC, P).transpose(3, 1, 0, 2, 4).reshape(MC, P, DC, 2 * P)
    arrays = {
        "x": a(x),
        "ctxT": ctx[:, :LM, :].transpose(0, 2, 1).reshape(B, CC, P, LM).transpose(0, 2, 1, 3),
        "dcaT": ctx[:, LM:, :].reshape(B * DCA, CC * P).T.reshape(CC, P, B * DCA),
        "W_attn": a(L0_attn_W_attn), "W_out": a(L0_attn_W_out), "b_out": a(L0_attn_b_out),
        "Wq": a(L0_xattn_Wq), "bq": a(L0_xattn_bq),
        "Wkv": by_kind(np.concatenate([a(L0_xattn_Wk), a(L0_xattn_Wv)], 1)),
        "bkv": by_kind(np.concatenate([a(L0_xattn_bk), a(L0_xattn_bv)])),
        "Wdca": a(L0_xattn_Wkv_dca), "bdca": a(L0_xattn_bkv_dca),
        "norm": np.stack([a(v) for v in (L0_xattn_qn_w, L0_xattn_qn_b, L0_xattn_kn_w, L0_xattn_kn_b,
                                         L0_xattn_kn_dca_w, L0_xattn_kn_dca_b)], 1),
        "Wo": a(L0_xattn_Wo), "bo": a(L0_xattn_bo),
        "gates": np.concatenate([a(L0_ffn_gate_w).T, a(L0_ffn_shared_gate_w).T], 1),
        "w13": a(L0_ffn_w13).transpose(0, 2, 1).reshape(E, DC, P, 2 * I).transpose(0, 2, 1, 3),
        "w2": a(L0_ffn_w2).transpose(0, 2, 1),
        "se_up": se_up, "se_down": a(L0_ffn_se_down_w).T, "cos_sin": cos_sin,
    }
    nc = bacc.Bacc("TRN2", target_bir_lowering=False, num_devices=1)
    sent, args = {}, []
    for name, v in arrays.items():
        v = np.ascontiguousarray(v)
        sent[f"in_{name}"] = v
        args.append(nc.dram_tensor(f"in_{name}", v.shape, mybir.dt.from_np(v.dtype), kind="ExternalInput").ap())
    result = nc.dram_tensor("result", (B, S, D), F32, kind="ExternalOutput").ap()
    decoder_kernel(nc, *args, result)
    return run_bass_kernel_spmd(nc, [sent], core_ids=[0]).results[0]["result"]
```

```python
from contextlib import ExitStack

import concourse.bass as bass
from concourse import mybir

F32 = mybir.dt.float32
U32 = mybir.dt.uint32
I32 = mybir.dt.int32
ALU = mybir.AluOpType
ACT = mybir.ActivationFunctionType
AX = mybir.AxisListType.X

P = 128
B, S, D = 8, 100, 512
DC = D // P
H, KV, G = 16, 4, 4
HD = 32
VD = 128
QK = (H + KV) * HD
L, DCA = 361, 16
LM = L - DCA
LC, LN_ = 115, 3
CC = 2
E, I = 60, 352
IC = (128, 128, 96)
ISH = 1408
MC = ISH // P
TOPK = 4
NORM_STEPS = 20
LINKS = 88
T = 128
NOV = (B * S * TOPK) // (T + 1)
NG = E + 1
PAIRS = B // 2
SCALE = HD ** -0.5


class Signal:

    all = []

    def __init__(self, sem, keys):
        self.sem, self.keys = sem, list(keys)
        Signal.all.append(self)

    def at(self, i, key):
        return i * len(self.keys) + (self.keys.index(key) + 2)

    def before(self, i):
        return i * len(self.keys) + 1

    def prior(self, i, key):
        return i * len(self.keys) + (self.keys.index(key) + 1)


KV_UNITS = [(j, c) for c in range(LN_) for j in range(2)]
XS_LAG, PV_LAG = 3, 5

DCA_EXP_1 = 16


def attention_fills():
    u = KV_UNITS
    unit = lambda n: [(("kx",) + u[n], 6), (("vx",) + u[n], 7)]
    kxT = lambda n, b: [(("kxT",) + u[n], b)]
    out = [(("xT1", 0), 4), (("xT1", 1), 5)]
    out += [(("q", 0), 0), (("k", 0), 1), (("v", 0), 2)] + unit(0)
    out += [(("q", 1), 3), (("k", 1), 4), (("v", 1), 5)] + unit(1)
    out += [(("qT", 0), 0), (("kT", 0), 1)] + unit(2) + kxT(0, 2)
    out += [(("qT", 1), 0), (("kT", 1), 1)]
    out += [(("s", 0, g), 2 + g) for g in range(G)]
    out += unit(3) + kxT(1, 0)
    out += [(("s", 1, g), 2 + g) for g in range(G)]
    out += unit(4)
    out += [(("pT", 0, g), g % 2) for g in range(G)]
    out += [(("pv", 0, 0), 6), (("pv", 0, 1), 7)] + kxT(2, 2) + [(("pv", 0, 2), 6), (("pv", 0, 3), 7)]
    out += [(("pT", 1, g), 2 + g) for g in range(G)]
    out += [(("pv", 1, 0), 6), (("o", 0), 0), (("pv", 1, 1), 7), (("pv", 1, 2), 6)]
    out += [(("xT2", 0), 4)] + kxT(3, 5) + [(("pv", 1, 3), 7), (("xq", 0), 3), (("o", 1), 1)]
    out += unit(5) + kxT(4, 5)
    out += [(("xqT", 0), 2), (("xT2", 1), 4), (("ds", 0), 3), (("xq", 1), 0)]
    for n in range(2 * H + PV_LAG):
        out += [(key, 3) for key in HEAD_HOOKS.get(n, [])]
        if n < 2 * H:
            out.append((("xs", n), (n + 1) % 3))
        if XS_LAG <= n < 2 * H + XS_LAG:
            out.append((("xpT", n - XS_LAG), 4 + n % 2))
        if n >= PV_LAG and (n - PV_LAG) % H == H - 1:
            out.append((("ctx", (n - PV_LAG) // H), 6 + (n - PV_LAG) // H))
    out += [(("xo", 1), 0), (("xT3", 1), 4), (("gate", 1), 5)]
    return out


HEAD_HOOKS = {4: [("dpT", 0)], 8: [("kxT", 1, 2)], 12: [("xqT", 1)], 14: [("ds", 1)], 20: [("dpT", 1)],
              H + PV_LAG + 1: [("xo", 0)], H + PV_LAG + 8: [("xT3", 0)], H + PV_LAG + 9: [("gate", 0)]}


def decoder_kernel(nc, x, ctxT, dcaT, W_attn, W_out, b_out, Wq, bq, Wkv, bkv, Wdca, bdca, norm, Wo, bo,
                   gates, w13, w2, se_up, se_down, cos_sin, out):
    fills = attention_fills()
    bank_of = dict(fills)
    Signal.all = []

    cm = ExitStack()
    with cm:
        def sb(name, shape, dt=F32):
            return cm.enter_context(nc.sbuf_tensor(name, shape, dt))

        def sem(name):
            return cm.enter_context(nc.semaphore(name))

        xn3_d = nc.dram_tensor("xn3_d", [B, S, D], F32, kind="Internal").ap()
        x2_d = nc.dram_tensor("x2_d", [B, S, D], F32, kind="Internal").ap()
        xT3_d = nc.dram_tensor("xT3_d", [B, P, DC * S], F32, kind="Internal").ap()
        vd_d = nc.dram_tensor("vd_d", [P, D], F32, kind="Internal").ap()
        xs_d = nc.dram_tensor("xs_d", [(E + NOV) * T, D], F32, kind="Internal").ap()
        ys_d = nc.dram_tensor("ys_d", [(E + NOV) * T, D], F32, kind="Internal").ap()

        ps = cm.enter_context(nc.psum_tensor("ps", [P, 8, 512], F32))

        ident = sb("ident", [P, P])
        ones = sb("ones", [P, P])
        tri = sb("tri", [P, P])
        zero = sb("zero", [P, D])
        lg_all = sb("lg_all", [P, B, NG])

        ARENA = 51250
        arena = sb("arena", [P, ARENA])
        top = [0]

        def carve(*shape):
            n = 1
            for d in shape:
                n *= d
            a = arena[:, top[0]:top[0] + n]
            top[0] += n
            assert top[0] <= ARENA, top[0]
            if len(shape) == 2:
                return a.rearrange("p (a b) -> p a b", a=shape[0])
            if len(shape) == 3:
                return a.rearrange("p (a b c) -> p a b c", a=shape[0], b=shape[1])
            if len(shape) == 4:
                return a.rearrange("p (a b c d) -> p a b c d", a=shape[0], b=shape[1], c=shape[2])
            return a

        w_attn = carve(DC, QK + D)
        w_out = carve(H, D)
        w_q = carve(DC, D)
        w_kv = carve(CC, 2 * D)
        w_o = carve(DC, D)
        w_gate = carve(DC, NG)
        bo_bc = carve(D)
        bout_bc = carve(D)
        bq_bc = carve(D)
        bkv_bc = carve(2 * D)
        cs = carve(4, HD)
        nrm = carve(6)
        blk_k = carve(4)
        blk_v = carve(8)
        kd_all = carve(DC, P)
        vd_all = carve(B, 2, HD)
        x_in = [carve(D) for _ in range(2)]
        xr = [carve(D) for _ in range(2)]
        xn = [carve(D) for _ in range(2)]
        xT = [carve(DC, S) for _ in range(2)]
        t0 = carve(D)
        t1 = carve(D)
        stat = carve(64)
        stat_n = carve(16)
        qr = [carve(D) for _ in range(2)]
        kr = [carve(KV, G, HD) for _ in range(2)]
        v_s = [carve(D) for _ in range(2)]
        qT = [carve(KV, S) for _ in range(2)]
        kT = [carve(KV, S) for _ in range(2)]
        nmax = [carve(G, KV) for _ in range(2)]
        psum_ = [carve(G, KV) for _ in range(2)]
        prec = [carve(G, KV) for _ in range(2)]
        NP_ = 8
        preamble_at = top[0]
        pr = [carve(KV, S) for _ in range(NP_)]
        pT = carve(KV, G, S)
        cT = [carve(G, S) for _ in range(2)]
        c_in = [carve(CC, LM) for _ in range(2)]
        hn = [carve(D) for _ in range(3)]
        sq = carve(D)
        root = [carve(H) for _ in range(3)]
        vx = [carve(LN_, D) for _ in range(2)]
        kxT = [carve(DC, LM) for _ in range(2)]
        xqT = [carve(DC, S) for _ in range(2)]
        kdb = [carve(DC, 4, DCA) for _ in range(2)]
        vdb = [carve(2, 8, HD) for _ in range(2)]
        dnm = carve(2, H)
        dsum = carve(2, H)
        drec = carve(2, H)
        dp = [carve(H, DCA) for _ in range(2)]
        dpT = [carve(2, S) for _ in range(2)]
        xnm = carve(2, H)
        xsum = carve(2, H)
        xrec = carve(2, H)
        NX = 4
        xp = [pr[n].rearrange("p a b -> p (a b)")[:, 0:LM] for n in range(NX)]
        pT_flat = pT.rearrange("p a b c -> p (a b c)")
        xpT = [pT_flat[:, n * LN_ * S:(n + 1) * LN_ * S].rearrange("p (a b) -> p a b", a=LN_) for n in range(NX)]
        cxT = cT
        kn = hn[0]
        vd_s = sq
        print("attention", top[0])
        top[0] = preamble_at
        w_dca = carve(CC, 2 * D)
        bdca_bc = carve(2 * D)
        c_dca = carve(CC, P)

        top[0] = 0
        xT3 = carve(B, DC * S)
        se_w = [carve(DC, 2 * P) for _ in range(3)]
        hT_all = carve(MC, B * S)
        w_down = carve(MC, D)
        acc = carve(B, D)
        w13_s = [carve(DC, 2 * I) for _ in range(2)]
        w2_s = [carve(3, D) for _ in range(2)]
        xs_s = [carve(D) for _ in range(2)]
        xsT = [carve(DC, T) for _ in range(2)]
        sl = [carve(3, T) for _ in range(2)]
        hT = [carve(3, T) for _ in range(2)]
        y_s = [carve(D) for _ in range(2)]
        s_sh = [carve(400) for _ in range(2)]
        xn3 = carve(B, D)
        oh = carve(B, E)
        mask = carve(B, E)
        slot_e = carve(B, E)
        bts = carve(6, E)
        ovc = carve(NOV, E)[0:1]
        rsm = carve(8, B, 8)
        half3 = sb("three_halves", [P, H])
        iota_e = sb("iota_e", [P, E])
        iota_n = sb("iota_n", [P, NOV])
        base_e = sb("base_e", [P, E])
        ov_i = sb("ov_i", [1, NOV + 1], I32)
        slot_u = sb("slot_u", [P, B * TOPK], U32)
        idx_u = sb("idx_u", [P, B, 8], U32)

        full = [Signal(sem(f"bank{n}_full"), [k for k, b in fills if b == n and k[0] != "ctx"]) for n in range(8)]
        free = [Signal(sem(f"bank{n}_free"), [k for k, b in fills if b == n]) for n in range(8)]
        pre_load = sem("preamble_loaded")
        w_loaded = {n: sem(f"{n}_loaded") for n in ("w_attn", "w_out", "w_q", "w_kv", "w_o", "w_gate")}
        consts_ready = sem("consts_ready")
        weights_centred = sem("weights_centred")
        pool_pre = sem("pool_preamble")
        kd_ready = sem("kd_ready")
        vd_stored = sem("vd_stored")
        vd_loaded = sem("vd_loaded")
        dca_mm = sem("dca_projected")
        dca_n = sem("dca_normed")
        dca_t = sem("dca_transposed")
        x_loaded = [sem(f"x_loaded{j}") for j in range(2)]
        c_loaded = [sem(f"c_loaded{j}") for j in range(2)]
        xn_stored = [sem(f"xn3_stored{j}") for j in range(2)]
        x2_stored = [sem(f"x2_stored{j}") for j in range(2)]
        xT_stored = [sem(f"xT3_stored{j}") for j in range(2)]
        zeroed = sem("slots_zeroed")
        chain = sem("vector_chain")
        pairs = [0, 1]
        xn_ready = Signal(sem("xn_ready"), [(n, j) for n in (1, 2, 3) for j in pairs])
        jg = [(j, g) for j in pairs for g in range(G)]
        max_ready = Signal(sem("max_ready"), jg)
        rec_ready = Signal(sem("rec_ready"), jg)
        p_ready = Signal(sem("p_ready"), jg)
        xr_ready = Signal(sem("xr_ready"), [(n, j) for n in (0, 1) for j in pairs])
        u = KV_UNITS
        NORMS = u[:5] + [("q", 0), u[5], ("q", 1)]
        hn_ready = Signal(sem("heads_normed"), NORMS)
        pool_step = Signal(sem("pool_chain"), [(k, n) for k in NORMS for n in range(NORM_STEPS)])
        dp_ready = Signal(sem("dca_probs_ready"), pairs)
        db_ready = Signal(sem("dca_blocks_ready"), pairs)
        dexp_ready = Signal(sem("dexp_ready"), pairs)
        hh = list(range(2 * H))
        xmax_ready = Signal(sem("xmax_ready"), hh)
        xrec_ready = Signal(sem("xrec_ready"), hh)
        xp_ready = Signal(sem("xp_ready"), hh)
        xpv_done = Signal(sem("xpv_done"), hh)
        o_part = Signal(sem("o_part"), [(0, 0), (0, 1), (0, 2), (1, 0), (1, 1), (1, 2)])

        xT3_loaded = sem("xT3_loaded")
        se_loaded = [sem(f"se_loaded{r}") for r in range(3)]
        down_loaded = sem("down_loaded")
        acc_loaded = sem("acc_loaded")
        xn3_loaded = sem("xn3_loaded")
        up_full = [sem(f"up_full{r}") for r in range(2)]
        silu_ready = [sem(f"shared_silu{r}") for r in range(2)]
        hs_ready = [sem(f"shared_h{r}") for r in range(2)]
        dn_full = sem("shared_down_full")
        dn_free = sem("shared_down_free")
        router_step = sem("router_step")
        r_act = sem("router_exp")
        r_in = sem("router_in")
        r_out = sem("router_out")
        mask_ready = sem("mask_ready")
        rank_full = sem("rank_full")
        slots_ready = sem("slots_ready")
        scattered = sem("scattered")
        w13_loaded = [sem(f"w13_loaded{r}") for r in range(2)]
        w2_loaded = [sem(f"w2_loaded{r}") for r in range(2)]
        xs_loaded = [sem(f"xs_loaded{r}") for r in range(2)]
        xst_full = [sem(f"xst_full{r}") for r in range(2)]
        xst_ready = [sem(f"xst_ready{r}") for r in range(2)]
        up1_full = [sem(f"gate_up_full{r}") for r in range(2)]
        sl_ready = [sem(f"silu_ready{r}") for r in range(2)]
        h_ready = [sem(f"h_ready{r}") for r in range(2)]
        y_full = [sem(f"y_full{r}") for r in range(2)]
        y_ready = [sem(f"y_ready{r}") for r in range(2)]
        y_stored = [sem(f"y_stored{r}") for r in range(2)]
        o_w = sem("over_loaded")
        o_t = sem("over_transposed")
        o_tc = sem("over_xT")
        o_g = sem("over_gate_up")
        o_s = sem("over_silu")
        o_h = sem("over_h")
        o_y = sem("over_y")
        o_yc = sem("over_y_copied")
        o_st = sem("over_stored")
        gathered = [sem(f"gathered{r}") for r in range(4)]
        added = [sem(f"added{r}") for r in range(4)]
        out_ready = sem("out_ready")
        load_gate = sem("load_gate")
        out_stored = sem("out_stored")

        by_turns = (x2_stored + xn_stored + xT_stored + up1_full + xst_full + y_full + h_ready + y_ready + xst_ready + y_stored
                    + [o_y, o_yc, o_st])

        block = cm.enter_context(nc.Block())

        def bank(n):
            return ps[:, n, :]

        def wait_filled(eng, i, *key):
            k = bank_of[key]
            eng.wait_ge(full[k].sem, full[k].at(i, key))
            return k

        def wait_drained(eng, i, *key):
            k = bank_of[key]
            eng.wait_ge(free[k].sem, free[k].at(i, key))

        def wait_turns_filled(eng, i, *banks):
            for k in banks:
                eng.wait_ge(full[k].sem, full[k].before(i))

        @block.sync
        def _(sp):
            bc = lambda v, n: v.rearrange("(a d) -> a d", a=1).to_broadcast([P, n])
            sp.dma_start(c_dca, dcaT.rearrange("c p n -> p c n")).then_inc(pre_load, 16)
            sp.dma_start(w_dca, Wdca.rearrange("(c p) n -> p c n", p=P)).then_inc(pre_load, 16)
            sp.dma_start(bdca_bc, bc(bdca, 2 * D)).then_inc(pre_load, 16)
            sp.dma_start(bkv_bc, bc(bkv, 2 * D)).then_inc(pre_load, 16)
            sp.dma_start(bq_bc, bc(bq, D)).then_inc(pre_load, 16)
            sp.dma_start(bo_bc, bc(bo, D)).then_inc(pre_load, 16)
            sp.dma_start(bout_bc, bc(b_out, D)).then_inc(pre_load, 16)
            sp.dma_start(cs[0:S], cos_sin).then_inc(pre_load, 16)
            for g in range(4):
                sp.dma_start(nrm[g * HD:(g + 1) * HD, :], norm).then_inc(pre_load, 16)
            sp.dma_start(w_kv, Wkv.rearrange("(c p) n -> p c n", p=P)).then_inc(w_loaded["w_kv"], 16)
            sp.dma_start(w_q, Wq.rearrange("(c p) n -> p c n", p=P)).then_inc(w_loaded["w_q"], 16)
            sp.dma_start(w_attn, W_attn.rearrange("(c p) n -> p c n", p=P)).then_inc(w_loaded["w_attn"], 16)
            sp.dma_start(w_out, W_out.rearrange("(c p) n -> p c n", p=P)).then_inc(w_loaded["w_out"], 16)
            sp.dma_start(w_o, Wo.rearrange("(c p) n -> p c n", p=P)).then_inc(w_loaded["w_o"], 16)
            sp.dma_start(w_gate, gates.rearrange("(c p) n -> p c n", p=P)).then_inc(w_loaded["w_gate"], 16)
            for i in range(PAIRS):
                for j in range(2):
                    sp.wait_ge(xn_ready.sem, xn_ready.before(i))
                    sp.wait_ge(xr_ready.sem, xr_ready.before(i))
                    sp.dma_start(x_in[j][0:S, :], x[i * 2 + j, :, :]).then_inc(x_loaded[j], 16)
                for j in range(2):
                    wait_turns_filled(sp, i, 7)
                    sp.dma_start(c_in[j], ctxT[i * 2 + j, :, :, :]).then_inc(c_loaded[j], 16)
                for j in range(2):
                    sp.wait_ge(xn_ready.sem, xn_ready.at(i, (3, j)))
                    sp.dma_start(xn3_d[i * 2 + j, :, :], xn[j][0:S, :]).then_inc(xn_stored[j], 16)
                    sp.dma_start(x2_d[i * 2 + j, :, :], xr[j][0:S, :]).then_inc(x2_stored[j], 16)
                for j in range(2):
                    wait_drained(sp, i, "xT3", j)
                    sp.dma_start(xT3_d[i * 2 + j, :, :], xT[j].rearrange("p a b -> p (a b)")).then_inc(xT_stored[j], 16)

            for k in range(8):
                sp.wait_ge(full[k].sem, full[k].before(PAIRS))
                sp.wait_ge(free[k].sem, free[k].before(PAIRS))
            for j in range(2):
                sp.wait_ge(xn_stored[j], 16 * PAIRS + 1)
                sp.wait_ge(x2_stored[j], 16 * PAIRS + 1)
                sp.wait_ge(xT_stored[j], 16 * PAIRS + 1)
            sp.dma_start(xT3, xT3_d.rearrange("b p n -> p b n")).then_inc(xT3_loaded, 16)

            def load_up(m):
                if m >= 3:
                    sp.wait_ge(up_full[(m - 3) % 2], 4 * ((m - 3) // 2 + 1))
                sp.dma_start(se_w[m % 3], se_up[m, :, :, :]).then_inc(se_loaded[m % 3], 16)

            for m in range(3):
                load_up(m)
            sp.dma_start(xn3[0:S], xn3_d.rearrange("b s d -> s b d")).then_inc(xn3_loaded, 16)
            sp.dma_start(acc[0:S], x2_d.rearrange("b s d -> s b d")).then_inc(acc_loaded, 16)
            sp.dma_start(w_down, se_down.rearrange("(c p) n -> p c n", p=P)).then_inc(down_loaded, 16)
            for m in range(3, MC):
                load_up(m)
            def load_13(r, turn, e):
                sp.wait_ge(up1_full[r], turn + 1)
                sp.sem_inc(load_gate, 1)
                sp.dma_start(w13_s[r], w13[e, :, :, :]).then_inc(w13_loaded[r], 16)

            def load_rows(r, turn, e):
                sp.wait_ge(xst_full[r], turn + 1)
                sp.sem_inc(load_gate, 1)
                sp.dma_start(xs_s[r], xs_d[bass.ds(e * T, T), :]).then_inc(xs_loaded[r], 16)

            def load_2(r, turn, e):
                sp.wait_ge(y_full[r], turn + 1)
                sp.sem_inc(load_gate, 1)
                sp.dma_start(w2_s[r][:, 0:2, :], w2[e, 0:256, :].rearrange("(c p) n -> p c n", p=P)).then_inc(w2_loaded[r], 16)
                sp.dma_start(w2_s[r][0:96, 2, :], w2[e, 256:I, :]).then_inc(w2_loaded[r], 16)

            load_13(0, 0, 0)
            load_13(1, 0, 1)
            load_2(0, 0, 0)
            load_2(1, 0, 1)
            sp.wait_ge(scattered, 16 * B * TOPK)
            load_rows(0, 0, 0)
            load_rows(1, 0, 1)
            load_rows(0, 1, 2)
            load_rows(1, 1, 3)
            load_13(0, 1, 2)
            with sp.Fori(0, E // 2 - 2) as i:
                load_rows(0, i + 2, i * 2 + 4)
                load_13(1, i + 1, i * 2 + 3)
                load_2(0, i + 1, i * 2 + 2)
                load_rows(1, i + 2, i * 2 + 5)
                load_13(0, i + 2, i * 2 + 4)
                load_2(1, i + 1, i * 2 + 3)
            load_13(1, E // 2 - 1, E - 1)
            load_2(0, E // 2 - 1, E - 2)
            load_2(1, E // 2 - 1, E - 1)
            sp.wait_ge(slots_ready, 1)
            sp.wait_ge(up1_full[1], E // 2 + 1)
            sp.wait_ge(y_full[0], E // 2 + 1)
            sp.wait_ge(xst_full[0], E // 2 + 1)
            count = sp.value_load(ov_i[0:1, NOV:NOV + 1], min_val=0, max_val=NOV)
            with sp.Fori(0, NOV) as t:
                with sp.If(count > t):
                    e = sp.value_load(ov_i[0:1, bass.ds(t, 1)], min_val=0, max_val=E - 1)
                    sp.wait_ge(o_y, t + 1)
                    sp.sem_inc(load_gate, 1)
                    sp.dma_start(w13_s[0], w13[e, :, :, :]).then_inc(o_w, 16)
                    sp.dma_start(xs_s[0], xs_d[bass.ds(t * T + E * T, T), :]).then_inc(o_w, 16)
                    sp.dma_start(w2_s[0][:, 0:2, :], w2[e, 0:256, :].rearrange("(c p) n -> p c n", p=P)).then_inc(o_w, 16)
                    sp.dma_start(w2_s[0][0:96, 2, :], w2[e, 256:I, :]).then_inc(o_w, 16)
            for b in range(B):
                sp.wait_ge(out_ready, b + 1)
                sp.dma_start(out[b, :, :], acc[0:S, b, :]).then_inc(out_stored, 16)
            sp.wait_ge(out_stored, 16 * B)

        @block.gpsimd
        def _(pool):
            for s in [signal.sem for signal in Signal.all] + by_turns:
                pool.sem_inc(s, 1)
            nc.gpsimd.memset(zero[:], 0.0).then_inc(pool_pre, 1)
            nc.gpsimd.memset(ones[:], 1.0).then_inc(pool_pre, 1)
            nc.gpsimd.memset(half3[:], 1.5).then_inc(pool_pre, 1)
            nc.gpsimd.iota(iota_e[:], pattern=[[1, E]], base=0, channel_multiplier=0,
                           allow_small_or_imprecise_dtypes=True).then_inc(consts_ready, 1)
            nc.gpsimd.iota(iota_n[:], pattern=[[1, NOV]], base=0, channel_multiplier=0,
                           allow_small_or_imprecise_dtypes=True).then_inc(consts_ready, 1)
            pool.wait_ge(pool_pre, 3)
            nc.gpsimd.affine_select(out=ident[:], in_=ones[:], compare_op=ALU.is_equal, fill=0.0, base=0,
                                    pattern=[[-1, P]], channel_multiplier=1).then_inc(consts_ready, 1)
            nc.gpsimd.affine_select(out=tri[:], in_=ones[:], compare_op=ALU.is_gt, fill=0.0, base=0,
                                    pattern=[[1, P]], channel_multiplier=-1).then_inc(consts_ready, 1)
            for width, m, n in ((HD, blk_k, 4), (DCA, blk_v, 8)):
                nc.gpsimd.affine_select(out=m, in_=ones[:, 0:n], compare_op=ALU.is_ge, fill=0.0, base=0,
                                        pattern=[[-width, n]], channel_multiplier=1).then_inc(pool_pre, 1)
            pool.wait_ge(pool_pre, 5)
            for width, m, n in ((HD, blk_k, 4), (DCA, blk_v, 8)):
                nc.gpsimd.affine_select(out=m, in_=m, compare_op=ALU.is_ge, fill=0.0, base=width - 1,
                                        pattern=[[width, n]], channel_multiplier=-1).then_inc(pool_pre, 1)
            pool.wait_ge(pool_pre, 7)
            zrow = zero[:, :].rearrange("p (a d) -> p a d", a=1).to_broadcast([P, 12, D])
            for n in range((E + NOV) // 12):
                pool.dma_start(xs_d[n * 12 * T:(n + 1) * 12 * T, :].rearrange("(a p) d -> p a d", p=P),
                               zrow).then_inc(zeroed, 16)
            for n in range(NOV // 12):
                pool.dma_start(ys_d[(E + n * 12) * T:(E + n * 12 + 12) * T, :].rearrange("(a p) d -> p a d", p=P),
                               zrow).then_inc(zeroed, 16)
            pool.wait_ge(dca_n, 2)
            pool.dma_start(vd_d, vd_s).then_inc(vd_stored, 16)
            pool.wait_ge(vd_stored, 16)
            vsrc = vd_d.rearrange("(b r) (c h e) -> r b c h e", b=B, c=2, h=8)
            for h in range(8):
                for c in range(2):
                    pool.dma_start(vd_all[h * DCA:(h + 1) * DCA, :, c, :], vsrc[:, :, c, h, :]).then_inc(vd_loaded, 16)
            pool.wait_ge(pre_load, 16 * 12)
            pool.wait_ge(vd_loaded, 16 * 16)
            pool.wait_ge(kd_ready, 1)
            with pool.Fori(0, PAIRS) as i:
                for j in range(2):
                    pool.wait_ge(x_loaded[j], i * 16 + 16)
                    pool.wait_ge(x2_stored[j], i * 16 + 1)
                    nc.gpsimd.tensor_tensor(xr[j][0:S, :], x_in[j][0:S, :], bout_bc[0:S, :], ALU.add).then_inc(xr_ready.sem, 1)
                for j in range(2):
                    pool.wait_ge(xpv_done.sem, xpv_done.before(i))
                    kd_b = kd_all[:, :, bass.ds((i * 2 + j) * DCA, DCA)]
                    for c in range(DC):
                        nc.gpsimd.tensor_tensor(kdb[j][:, c, :, :],
                                                kd_all[:, c:c + 1, bass.ds((i * 2 + j) * DCA, DCA)].to_broadcast([P, 4, DCA]),
                                                blk_k.rearrange("p (a b) -> p a b", b=1).to_broadcast([P, 4, DCA]), ALU.mult)
                    for c in range(2):
                        last = nc.gpsimd.tensor_tensor(vdb[j][:, c, :, :],
                                                       vd_all[:, bass.ds(i * 2 + j, 1), c, :].to_broadcast([P, 8, HD]),
                                                       blk_v.rearrange("p (a b) -> p a b", b=1).to_broadcast([P, 8, HD]), ALU.mult)
                    last.then_inc(db_ready.sem, 1)

                def head_norm(key):
                    slot, m = NORMS.index(key) % 3, S if key[0] == "q" else LC
                    v = hn[slot][0:m, :]
                    step = [0]

                    def then(ins, carrier=False):
                        ins.then_inc(pool_step.sem, 1)
                        pool.wait_ge(pool_step.sem, pool_step.at(i, (key, step[0])))
                        step[0] += 1
                        if carrier:
                            pool.sem_inc(load_gate, 1)
                    wait_drained(pool, i, *(("xq", key[1]) if key[0] == "q" else ("kx",) + key))
                    s3 = sq[0:m, :].rearrange("p (a b) -> p a b", b=HD)
                    then(nc.gpsimd.tensor_tensor(sq[0:m, :], v, v, ALU.mult))
                    w = HD // 2
                    while w > 1:
                        then(nc.gpsimd.tensor_tensor(s3[:, :, 0:w], s3[:, :, 0:w], s3[:, :, w:2 * w], ALU.add))
                        w //= 2
                    ss, y, minus_half = [r[0:m, :] for r in root]
                    col = lambda a: a.rearrange("p (a b) -> p a b", b=1)
                    then(nc.gpsimd.tensor_tensor(col(ss), s3[:, :, 0:1], s3[:, :, 1:2], ALU.add), carrier=True)
                    then(nc.gpsimd.tensor_scalar(ss, ss, HD * 1e-6, None, ALU.add), carrier=True)
                    nc.gpsimd.tensor_scalar(y.bitcast(I32), ss.bitcast(I32), -0.5, float(0x5f3759df), ALU.mult, ALU.add)
                    then(nc.gpsimd.tensor_scalar(minus_half, ss, -0.5, None, ALU.mult))
                    for _ in range(3):
                        then(nc.gpsimd.tensor_tensor(ss, y, y, ALU.mult))
                        then(nc.gpsimd.tensor_tensor(ss, ss, minus_half, ALU.mult))
                        then(nc.gpsimd.tensor_tensor(ss, ss, half3[0:m, :], ALU.add))
                        then(nc.gpsimd.tensor_tensor(y, y, ss, ALU.mult))
                    nc.gpsimd.tensor_tensor(v.rearrange("p (a b) -> p a b", b=HD), v.rearrange("p (a b) -> p a b", b=HD),
                                            col(y).to_broadcast([m, H, HD]), ALU.mult).then_inc(hn_ready.sem, 1)
                    assert step[0] == NORM_STEPS, f"NORM_STEPS = {step[0]}"

                def normalise(j):
                    for g in range(G):
                        n = j * G + g
                        pool.wait_ge(rec_ready.sem, rec_ready.at(i, (j, g)))
                        nc.gpsimd.tensor_tensor(pr[n % NP_][0:S], pr[n % NP_][0:S],
                                                prec[j][0:S, g, :].rearrange("p (a b) -> p a b", b=1).to_broadcast([S, KV, S]),
                                                ALU.mult).then_inc(p_ready.sem, 1)

                def add_bias(j):
                    pool.wait_ge(xn_ready.sem, xn_ready.at(i, (2, j)))
                    nc.gpsimd.tensor_tensor(xr[j][0:S, :], xr[j][0:S, :], bo_bc[0:S, :], ALU.add).then_inc(xr_ready.sem, 1)

                for n in range(3):
                    head_norm(NORMS[n])
                normalise(0)
                normalise(1)
                for n in range(3, 6):
                    head_norm(NORMS[n])
                add_bias(0)
                head_norm(NORMS[6])
                head_norm(NORMS[7])
                add_bias(1)
            pool.wait_ge(slots_ready, 1)
            pool.wait_ge(xn3_loaded, 16)
            pool.wait_ge(zeroed, 16 * ((E + 2 * NOV) // 12))
            for b in range(B):
                for k in range(TOPK):
                    n = b * TOPK + k
                    pool.indirect_dma_start(out=xs_d, out_offset=bass.IndirectOffsetOnAxis(ap=slot_u[0:S, n:n + 1], axis=0),
                                            in_=xn3[0:S, b, :], in_offset=None).then_inc(scattered, 16)
            for r in range(2):
                pool.wait_ge(y_stored[r], 16 * (E // 2) + 1)
            count = pool.value_load(ov_i[0:1, NOV:NOV + 1], min_val=0, max_val=NOV)
            with pool.Fori(0, NOV) as t:
                with pool.If(count > t):
                    pool.wait_ge(o_st, t * 16 + 17)
            for n in range(B * TOPK):
                if n >= 4:
                    pool.wait_ge(added[n % 4], n // 4)
                pool.indirect_dma_start(out=xn3[0:S, n % 4, :], out_offset=None, in_=ys_d,
                                        in_offset=bass.IndirectOffsetOnAxis(ap=slot_u[0:S, n:n + 1], axis=0)).then_inc(gathered[n % 4], 16)

        @block.tensor
        def _(pe):
            pe.wait_ge(consts_ready, 4)
            pe.wait_ge(pre_load, 16 * 12)
            pe.wait_ge(weights_centred, 3)
            for half in range(2):
                for c in range(CC):
                    last = nc.tensor.matmul(bank(half), c_dca[:, c, :], w_dca[:, c, half * D:(half + 1) * D],
                                            start=(c == 0), stop=(c == CC - 1))
            last.then_inc(dca_mm, 1)
            pe.wait_ge(dca_n, 3)
            for c in range(DC):
                last = nc.tensor.transpose(ps[:, 4, c * P:(c + 1) * P], t0[:, c * P:(c + 1) * P], ident[:])
            last.then_inc(dca_t, 1)
            pe.wait_ge(kd_ready, 1)
            for w in w_loaded.values():
                pe.wait_ge(w, 16)

            with pe.Fori(0, PAIRS) as i:
                order = iter(fills)

                def begin(*key):
                    k, n = next(order)
                    assert k == key, (k, key)
                    n = bank_of[key]
                    pe.wait_ge(free[n].sem, free[n].prior(i, key))
                    return n

                def end(ins, *key):
                    ins.then_inc(full[bank_of[key]].sem, 1)

                def transpose_x(name, n, j):
                    pe.wait_ge(xn_ready.sem, xn_ready.at(i, (n, j)))
                    k = begin(name, j)
                    for c in range(DC):
                        last = nc.tensor.transpose(ps[:, k, c * S:(c + 1) * S], xn[j][0:S, c * P:(c + 1) * P], ident[0:S, 0:S])
                    end(last, name, j)

                def project(key, m, lhs, w, cols, n_c):
                    k = begin(*key)
                    for c in range(n_c):
                        last = nc.tensor.matmul(ps[0:m, k, 0:cols[1] - cols[0]], lhs(c), w[:, c, cols[0]:cols[1]],
                                                start=(c == 0), stop=(c == n_c - 1))
                    end(last, *key)

                def kv_project(n):
                    j, c = KV_UNITS[n]
                    if c == 0:
                        pe.wait_ge(c_loaded[j], i * 16 + 16)
                    rows = lambda a: c_in[j][:, a, c * LC:(c + 1) * LC]
                    project(("kx", j, c), LC, rows, w_kv, (0, D), CC)
                    project(("vx", j, c), LC, rows, w_kv, (D, 2 * D), CC)

                def transpose_normed(key, fill, m):
                    pe.wait_ge(hn_ready.sem, hn_ready.at(i, key))
                    k = begin(*fill)
                    for a in range(DC):
                        last = nc.tensor.transpose(ps[:, k, a * m:(a + 1) * m], hn[NORMS.index(key) % 3][0:m, a * P:(a + 1) * P],
                                                   ident[0:m, 0:m])
                    end(last, *fill)

                def kv_transpose(n):
                    transpose_normed(KV_UNITS[n], ("kxT",) + KV_UNITS[n], LC)

                def self_project(j):
                    wait_drained(pe, i, "xT1", j)
                    rows = lambda a: xT[j][:, a, :]
                    project(("q", j), S, rows, w_attn, (0, D), DC)
                    project(("k", j), S, rows, w_attn, (D, QK), DC)
                    project(("v", j), S, rows, w_attn, (QK, QK + D), DC)

                def transpose_qk(j):
                    wait_drained(pe, i, "k", j)
                    k = begin("qT", j)
                    for c in range(KV):
                        last = nc.tensor.transpose(ps[:, k, c * S:(c + 1) * S], qr[j][0:S, c * P:(c + 1) * P], ident[0:S, 0:S])
                    end(last, "qT", j)
                    k = begin("kT", j)
                    for c in range(KV):
                        last = nc.tensor.transpose(ps[:, k, c * S:(c + 1) * S], kr[j][0:S, c, :, :].rearrange("p a b -> p (a b)"), ident[0:S, 0:S])
                    end(last, "kT", j)

                def scores(j):
                    wait_drained(pe, i, "qT", j)
                    wait_drained(pe, i, "kT", j)
                    ks = [begin("s", j, g) for g in range(G)]
                    for c in range(KV):
                        for g in range(G):
                            rows_ = slice(g * HD, (g + 1) * HD)
                            last = nc.tensor.matmul(ps[0:S, ks[g], c * S:(c + 1) * S], qT[j][rows_, c, :], kT[j][rows_, c, :],
                                                    start=True, stop=True)
                            if c == KV - 1:
                                end(last, "s", j, g)

                def transpose_probs(j):
                    for g in range(G):
                        n = j * G + g
                        pe.wait_ge(p_ready.sem, p_ready.at(i, (j, g)))
                        k = begin("pT", j, g)
                        for c in range(KV):
                            last = nc.tensor.transpose(ps[0:S, k, c * S:(c + 1) * S], pr[n % NP_][0:S, c, :], ident[0:S, 0:S])
                        end(last, "pT", j, g)

                def values(j, c):
                    if c == 0:
                        for g in range(G):
                            wait_drained(pe, i, "pT", j, g)
                        wait_drained(pe, i, "v", j)
                    k = begin("pv", j, c)
                    last = nc.tensor.matmul(ps[:, k, 0:G * S], v_s[j][0:S, c * VD:(c + 1) * VD],
                                            pT[0:S, c, :, :].rearrange("p a b -> p (a b)"), start=True, stop=True)
                    end(last, "pv", j, c)

                def attend_out(j, c):
                    wait_drained(pe, i, "pv", j, c)
                    if c == 0:
                        pe.wait_ge(free[j].sem, free[j].prior(i, ("o", j)))
                    for g in range(G):
                        last = nc.tensor.matmul(ps[0:S, j, :], cT[c % 2][:, g, :], w_out[:, c * G + g, :],
                                                start=(c == 0 and g == 0), stop=(c == KV - 1 and g == G - 1))
                    if c < KV - 1:
                        last.then_inc(o_part.sem, 1)
                    return last

                def x_project(name, j, lhs, w, cols):
                    project((name, j), S, lhs, w, cols, DC)

                def dca_scores(j):
                    wait_drained(pe, i, "xqT", j)
                    pe.wait_ge(db_ready.sem, db_ready.at(i, j))
                    k = begin("ds", j)
                    for c in range(DC):
                        last = nc.tensor.matmul(ps[0:S, k, c * 64:(c + 1) * 64], xqT[j][:, c, :],
                                                kdb[j][:, c, :, :].rearrange("p a b -> p (a b)"), start=True, stop=True)
                    end(last, "ds", j)

                def dca_transpose(j):
                    pe.wait_ge(dp_ready.sem, dp_ready.at(i, j))
                    k = begin("dpT", j)
                    for c in range(2):
                        last = nc.tensor.transpose(ps[:, k, c * S:(c + 1) * S],
                                                   dp[j][0:S, c * 8:(c + 1) * 8, :].rearrange("p a b -> p (a b)"), ident[0:S, 0:S])
                    end(last, "dpT", j)

                def dca_values(j, a):
                    if a == 0:
                        wait_drained(pe, i, "dpT", j)
                        pe.wait_ge(free[6 + j].sem, free[6 + j].prior(i, ("ctx", j)))
                    four = vdb[j][:, a // 2, (a % 2) * 4:(a % 2) * 4 + 4, :].rearrange("p a b -> p (a b)")
                    nc.tensor.matmul(ps[:, 6 + j, a * S:(a + 1) * S], four, dpT[j][:, a // 2, :], start=True, stop=False)

                def query_project(j):
                    wait_drained(pe, i, "xT2", j)
                    x_project("xq", j, lambda a: xT[j][:, a, :], w_q, (0, D))

                def context_out(j):
                    wait_drained(pe, i, "ctx", j)
                    x_project("xo", j, lambda a: cxT[j][:, a, :], w_o, (0, D))

                def gate(j):
                    wait_drained(pe, i, "xT3", j)
                    x_project("gate", j, lambda a: xT[j][:, a, :], w_gate, (0, NG))

                transpose_x("xT1", 1, 0)
                transpose_x("xT1", 1, 1)
                self_project(0)
                kv_project(0)
                self_project(1)
                kv_project(1)
                transpose_qk(0)
                kv_project(2)
                kv_transpose(0)
                transpose_qk(1)
                scores(0)
                kv_project(3)
                kv_transpose(1)
                scores(1)
                kv_project(4)
                transpose_probs(0)
                values(0, 0)
                values(0, 1)
                kv_transpose(2)
                attend_out(0, 0)
                values(0, 2)
                attend_out(0, 1)
                values(0, 3)
                transpose_probs(1)
                attend_out(0, 2)
                values(1, 0)
                begin("o", 0)
                end(attend_out(0, 3), "o", 0)
                values(1, 1)
                attend_out(1, 0)
                values(1, 2)
                attend_out(1, 1)
                transpose_x("xT2", 2, 0)
                kv_transpose(3)
                values(1, 3)
                attend_out(1, 2)
                query_project(0)
                begin("o", 1)
                end(attend_out(1, 3), "o", 1)
                kv_project(5)
                kv_transpose(4)
                transpose_normed(("q", 0), ("xqT", 0), S)
                transpose_x("xT2", 2, 1)
                dca_scores(0)
                query_project(1)

                hooks = {"dpT": dca_transpose, "kxT": lambda j, c: kv_transpose(KV_UNITS.index((j, c))),
                         "xqT": lambda j: transpose_normed(("q", j), ("xqT", j), S), "ds": dca_scores, "xo": context_out,
                         "xT3": lambda j: transpose_x("xT3", 3, j), "gate": gate}
                for n in range(2 * H + PV_LAG):
                    for key in HEAD_HOOKS.get(n, []):
                        hooks[key[0]](*key[1:])
                    if n < 2 * H:
                        j, h = n // H, n % H
                        if h == 0:
                            wait_drained(pe, i, "xqT", j)
                            for c in range(LN_):
                                wait_drained(pe, i, "kxT", j, c)
                                wait_drained(pe, i, "vx", j, c)
                        k = begin("xs", n)
                        rows_ = slice((h % 4) * HD, (h % 4 + 1) * HD)
                        end(nc.tensor.matmul(ps[0:S, k, 0:LM], xqT[j][rows_, h // 4, :], kxT[j][rows_, h // 4, :],
                                             start=True, stop=True), "xs", n)
                    if XS_LAG <= n < 2 * H + XS_LAG:
                        m = n - XS_LAG
                        pe.wait_ge(xp_ready.sem, xp_ready.at(i, m))
                        k = begin("xpT", m)
                        for c in range(LN_):
                            last = nc.tensor.transpose(ps[0:LC, k, c * S:(c + 1) * S], xp[m % NX][0:S, c * LC:(c + 1) * LC], ident[0:S, 0:S])
                        end(last, "xpT", m)
                    if n >= PV_LAG:
                        m = n - PV_LAG
                        j, h = m // H, m % H
                        wait_drained(pe, i, "xpT", m)
                        if h % 4 == 0:
                            dca_values(j, h // 4)
                        for c in range(LN_):
                            last = nc.tensor.matmul(ps[(h % 4) * HD:(h % 4 + 1) * HD, 6 + j, (h // 4) * S:(h // 4 + 1) * S],
                                                    vx[j][0:LC, c, h * HD:(h + 1) * HD], xpT[m % NX][0:LC, c, :],
                                                    start=False, stop=(c == LN_ - 1))
                        last.then_inc(xpv_done.sem, 1)
                        if h == H - 1:
                            assert next(order)[0] == ("ctx", j)
                context_out(1)
                transpose_x("xT3", 3, 1)
                gate(1)

            for n in range(8):
                pe.wait_ge(free[n].sem, free[n].before(PAIRS))
            pe.wait_ge(xT3_loaded, 16)
            for m in range(MC):
                pe.wait_ge(se_loaded[m % 3], 16 * (m // 3 + 1))
                for half in range(2):
                    if m >= 2:
                        pe.wait_ge(hs_ready[m % 2], 2 * ((m - 2) // 2) + half + 1)
                    for gu in range(2):
                        for c in range(DC):
                            tok = xT3[:, half * 4:(half + 1) * 4, c * S:(c + 1) * S]
                            last = nc.tensor.matmul(ps[:, (m % 2) * 4 + half * 2 + gu, 0:400].rearrange("p (a b) -> p a b", a=4),
                                                    se_w[m % 3][:, c, gu * P:(gu + 1) * P], tok,
                                                    start=(c == 0), stop=(c == DC - 1))
                        last.then_inc(up_full[m % 2], 1)
            pe.wait_ge(mask_ready, 1)
            pe.wait_ge(hs_ready[0], 2 * ((MC + 1) // 2))
            pe.wait_ge(hs_ready[1], 2 * (MC // 2))
            for b in range(B):
                for a in range(b + 1):
                    nc.tensor.matmul(ps[0:S, 0, b * E:(b + 1) * E], (tri if a == b else ones)[0:S, 0:S], mask[0:S, a, :],
                                     start=(a == 0), stop=(a == b))
            for b in range(B):
                last = nc.tensor.matmul(ps[:, 1, 0:E], ones[0:S, :], mask[0:S, b, :], start=(b == 0), stop=(b == B - 1))
            last.then_inc(rank_full, 1)
            pe.wait_ge(down_loaded, 16)
            for b in range(B):
                if b >= 2:
                    pe.wait_ge(dn_free, b - 1)
                for m in range(MC):
                    last = nc.tensor.matmul(ps[0:S, 2 + b % 2, :], hT_all[:, m, b * S:(b + 1) * S], w_down[:, m, :],
                                            start=(m == 0), stop=(m == MC - 1))
                last.then_inc(dn_full, 1)
            pe.wait_ge(slots_ready, 1)
            pe.wait_ge(dn_free, B)

            def rows_T(r, turn):
                pe.wait_ge(xs_loaded[r], turn * 16 + 16)
                pe.wait_ge(xst_ready[r], turn + 1)
                for c in range(DC):
                    last = nc.tensor.transpose(ps[:, r, c * T:(c + 1) * T], xs_s[r][:, c * P:(c + 1) * P], ident[:])
                last.then_inc(xst_full[r], 1)

            def gate_up(r, turn):
                pe.wait_ge(w13_loaded[r], turn * 16 + 16)
                pe.wait_ge(xst_ready[r], turn + 2)
                pe.wait_ge(h_ready[r], turn + 1)
                gate_up_products(r)[-1].then_inc(up1_full[r], 1)

            def gate_up_products(r):
                done = []
                for gu in range(2):
                    for n, w in enumerate(IC):
                        at = gu * I + n * P
                        for c in range(DC):
                            done.append(nc.tensor.matmul(ps[0:w, 2 + 2 * gu + r, n * T:(n + 1) * T], w13_s[r][:, c, at:at + w],
                                                         xsT[r][:, c, :], start=(c == 0), stop=(c == DC - 1)))
                return done

            def down_products(r):
                for n, w in enumerate(IC):
                    last = nc.tensor.matmul(ps[:, 6 + r, :], hT[r][0:w, n, :], w2_s[r][0:w, n, :],
                                            start=(n == 0), stop=(n == len(IC) - 1))
                return last

            def down(r, turn):
                pe.wait_ge(w2_loaded[r], turn * 32 + 32)
                pe.wait_ge(h_ready[r], turn + 2)
                pe.wait_ge(y_ready[r], turn + 1)
                down_products(r).then_inc(y_full[r], 1)

            rows_T(0, 0)
            rows_T(1, 0)
            gate_up(0, 0)
            with pe.Fori(0, E // 2 - 1) as i:
                rows_T(0, i + 1)
                gate_up(1, i)
                down(0, i)
                rows_T(1, i + 1)
                gate_up(0, i + 1)
                down(1, i)
            gate_up(1, E // 2 - 1)
            down(0, E // 2 - 1)
            down(1, E // 2 - 1)
            pe.wait_ge(y_ready[0], E // 2 + 1)
            count = pe.value_load(ov_i[0:1, NOV:NOV + 1], min_val=0, max_val=NOV)
            with pe.Fori(0, NOV) as t:
                with pe.If(count > t):
                    pe.wait_ge(o_w, t * 64 + 64)
                    pe.wait_ge(o_yc, t + 1)
                    for c in range(DC):
                        last = nc.tensor.transpose(ps[:, 0, c * T:(c + 1) * T], xs_s[0][:, c * P:(c + 1) * P], ident[:])
                    last.then_inc(o_t, 1)
                    pe.wait_ge(o_tc, t + 1)
                    gate_up_products(0)[-1].then_inc(o_g, 1)
                    pe.wait_ge(o_h, t + 1)
                    down_products(0).then_inc(o_y, 1)

        @block.scalar
        def _(act):
            act.wait_ge(dca_t, 1)
            act.wait_ge(weights_centred, 4)
            for c in range(DC):
                last = nc.scalar.activation(kd_all[:, c, :], ps[:, 4, c * P:(c + 1) * P], ACT.Identity, bias=nrm[:, 5:6], scale=nrm[:, 4:5])
            last.then_inc(kd_ready, 1)

            with act.Fori(0, PAIRS) as i:
                def filled(*key):
                    return wait_filled(act, i, *key)

                def x_T(name, j):
                    k = filled(name, j)
                    nc.scalar.activation(xT[j].rearrange("p a b -> p (a b)"), ps[:, k, 0:DC * S], ACT.Copy).then_inc(free[k].sem, 1)

                def kv(n):
                    j, c = KV_UNITS[n]
                    k = filled("kxT", j, c)
                    nc.scalar.activation(kxT[j][:, :, c * LC:(c + 1) * LC], ps[:, k, 0:DC * LC].rearrange("p (a b) -> p a b", a=DC),
                                         ACT.Identity, bias=nrm[:, 3:4], scale=nrm[:, 2:3]).then_inc(free[k].sem, 1)

                def q_T(j):
                    k = filled("xqT", j)
                    nc.scalar.activation(xqT[j].rearrange("p a b -> p (a b)"), ps[:, k, 0:DC * S], ACT.Identity, bias=nrm[:, 1:2],
                                         scale=nrm[:, 0:1]).then_inc(free[k].sem, 1)

                def context_T(j):
                    act.wait_ge(xpv_done.sem, xpv_done.at(i, j * H + H - 1))
                    nc.scalar.activation(cxT[j].rearrange("p a b -> p (a b)"), ps[:, 6 + j, 0:DC * S], ACT.Copy).then_inc(free[6 + j].sem, 1)

                def copy(name, j, dst, cols):
                    k = filled(name, j)
                    nc.scalar.activation(dst, ps[0:dst.shape[0], k, 0:cols], ACT.Copy).then_inc(free[k].sem, 1)

                def exps(j):
                    for g in range(G):
                        n = j * G + g
                        k = filled("s", j, g)
                        act.wait_ge(max_ready.sem, max_ready.at(i, (j, g)))
                        for c in range(KV):
                            last = nc.scalar.activation(pr[n % NP_][0:S, c, :], ps[0:S, k, c * S:(c + 1) * S], ACT.Exp,
                                                        bias=nmax[j][0:S, g, c:c + 1], scale=1.0, accum_out=psum_[j][0:S, g, c:c + 1])
                        last.then_inc(free[k].sem, 1)

                def context(j, c):
                    k = filled("pv", j, c)
                    before = 4 * j + c - 2
                    if before >= 0:
                        jj, cc = before // KV, before % KV
                        if cc == KV - 1:
                            act.wait_ge(full[jj].sem, full[jj].at(i, ("o", jj)))
                        else:
                            act.wait_ge(o_part.sem, o_part.at(i, (jj, cc)))
                    nc.scalar.activation(cT[c % 2].rearrange("p a b -> p (a b)"), ps[:, k, 0:G * S], ACT.Copy).then_inc(free[k].sem, 1)

                def dca_exp(j):
                    wait_drained(act, i, "ds", j)
                    nc.scalar.activation(dp[j][0:S].rearrange("p a b -> p (a b)"), dp[j][0:S].rearrange("p a b -> p (a b)"), ACT.Exp).then_inc(dexp_ready.sem, 1)

                def gate_out(j):
                    k = filled("gate", j)
                    nc.scalar.activation(lg_all[0:S, bass.ds(i * 2 + j, 1), :], ps[0:S, k:k + 1, 0:NG], ACT.Copy).then_inc(free[k].sem, 1)

                def scale_probs(n):
                    act.wait_ge(xrec_ready.sem, xrec_ready.at(i, n))
                    nc.scalar.activation(xp[n % NX][0:S, :], xp[n % NX][0:S, :], ACT.Copy,
                                         scale=xrec[0:S, n // H, n % H:n % H + 1]).then_inc(xp_ready.sem, 1)

                for j in range(2):
                    act.wait_ge(xT_stored[j], i * 16 + 1)
                    x_T("xT1", j)
                copy("v", 0, v_s[0][0:S, :], D)
                copy("v", 1, v_s[1][0:S, :], D)
                copy("qT", 0, qT[0].rearrange("p a b -> p (a b)"), DC * S)
                kv(0)
                copy("qT", 1, qT[1].rearrange("p a b -> p (a b)"), DC * S)
                exps(0)
                kv(1)
                exps(1)
                context(0, 0)
                context(0, 1)
                kv(2)
                context(0, 2)
                context(0, 3)
                for c in range(KV - 1):
                    context(1, c)
                x_T("xT2", 0)
                kv(3)
                context(1, 3)
                kv(4)
                q_T(0)
                x_T("xT2", 1)
                dca_exp(0)
                for n in range(2 * H + 1):
                    for key in HEAD_HOOKS.get(n, []):
                        if key[0] == "dpT":
                            copy("dpT", key[1], dpT[key[1]].rearrange("p a b -> p (a b)"), 2 * S)
                        elif key[0] == "kxT":
                            kv(KV_UNITS.index(key[1:]))
                        elif key[0] == "xqT":
                            q_T(key[1])
                        elif key[0] == "xT3":
                            x_T("xT3", key[1])
                        elif key[0] == "gate":
                            gate_out(key[1])
                    if n == DCA_EXP_1:
                        dca_exp(1)
                    if n < 2 * H:
                        j, h = n // H, n % H
                        k = filled("xs", n)
                        act.wait_ge(xmax_ready.sem, xmax_ready.at(i, n))
                        if n >= NX:
                            kk = bank_of[("xpT", n - NX)]
                            act.wait_ge(full[kk].sem, full[kk].at(i, ("xpT", n - NX)))
                        nc.scalar.activation(xp[n % NX][0:S, :], ps[0:S, k, 0:LM], ACT.Exp, bias=xnm[0:S, j, h:h + 1], scale=1.0,
                                             accum_out=xsum[0:S, j, h:h + 1]).then_inc(free[k].sem, 1)
                    if 1 <= n < 2 * H + 1:
                        scale_probs(n - 1)
                    if n == H + PV_LAG - 1:
                        context_T(0)
                context_T(1)
                x_T("xT3", 1)
                gate_out(1)

            act.wait_ge(r_in, 1)
            for b in range(B):
                nc.scalar.activation(rsm[0:S, 1, b, 0:TOPK], rsm[0:S, 0, b, 0:TOPK], ACT.Exp, bias=rsm[0:S, 2, b, 0:1])
                nc.scalar.activation(oh[0:S, b, :], lg_all[0:S, b, 0:E], ACT.Exp, bias=rsm[0:S, 2, b, 0:1],
                                            accum_out=rsm[0:S, 3, b, 0:1])
            nc.scalar.activation(rsm[0:S, 6, :, 2:3], lg_all[0:S, :, E:NG], ACT.Sigmoid).then_inc(r_act, 1)
            for m in range(MC):
                for half in range(2):
                    act.wait_ge(up_full[m % 2], 4 * (m // 2) + 2 * half + 1)
                    if m:
                        act.wait_ge(hs_ready[(m - 1) % 2], 2 * ((m - 1) // 2) + half + 1)
                    nc.scalar.activation(s_sh[half], ps[:, (m % 2) * 4 + half * 2, 0:400], ACT.Silu).then_inc(silu_ready[m % 2], 1)

            def silu(r, turn):
                act.wait_ge(up1_full[r], turn + 2)
                act.wait_ge(h_ready[r], turn + 1)
                silu_parts(r).then_inc(sl_ready[r], 1)

            def silu_parts(r):
                nc.scalar.activation(sl[r][:, 0:2, :].rearrange("p a b -> p (a b)"), ps[:, 2 + r, 0:2 * T], ACT.Silu)
                return nc.scalar.activation(sl[r][0:96, 2, :], ps[0:96, 2 + r, 2 * T:3 * T], ACT.Silu)

            def store(r, turn, e):
                act.wait_ge(y_full[r], turn + 2)
                act.wait_ge(y_stored[r], turn * 16 + 1)
                nc.scalar.activation(y_s[r], ps[:, 6 + r, :], ACT.Copy).then_inc(y_ready[r], 1)
                act.wait_ge(y_ready[r], turn + 2)
                act.dma_start(ys_d[bass.ds(e * T, T), :], y_s[r]).then_inc(y_stored[r], 16)

            silu(0, 0)
            with act.Fori(0, E // 2 - 1) as i:
                silu(1, i)
                store(0, i, i * 2)
                silu(0, i + 1)
                store(1, i, i * 2 + 1)
            silu(1, E // 2 - 1)
            store(0, E // 2 - 1, E - 2)
            store(1, E // 2 - 1, E - 1)
            for r in range(2):
                act.wait_ge(y_stored[r], 16 * (E // 2) + 1)
            act.wait_ge(slots_ready, 1)
            count = act.value_load(ov_i[0:1, NOV:NOV + 1], min_val=0, max_val=NOV)
            with act.Fori(0, NOV) as t:
                with act.If(count > t):
                    act.wait_ge(o_g, t + 1)
                    silu_parts(0).then_inc(o_s, 1)
                    act.wait_ge(o_y, t + 2)
                    act.wait_ge(o_st, t * 16 + 1)
                    nc.scalar.activation(y_s[0], ps[:, 6, :], ACT.Copy).then_inc(o_yc, 1)
                    act.wait_ge(o_yc, t + 2)
                    act.dma_start(ys_d[bass.ds(t * T + E * T, T), :], y_s[0]).then_inc(o_st, 16)

        @block.vector
        def _(dve):
            count_ = [0, None, 0]

            def link(ins):
                ins.then_inc(chain, 1)
                count_[0] += 1
                if count_[1] is None:
                    dve.wait_ge(chain, count_[2] + count_[0])
                else:
                    dve.wait_ge(chain, count_[1] * LINKS + (count_[2] + count_[0]))

            def centre(view, n):
                m = stat[:, 0:n]
                link(nc.vector.tensor_reduce(m, view, AX, ALU.add))
                link(nc.vector.tensor_scalar(m, m, 1.0 / HD, None, ALU.mult))
                return nc.vector.tensor_tensor(view, view, m.rearrange("p (a b) -> p a b", b=1).to_broadcast([P, n, HD]), ALU.subtract)

            def head(v):
                return v.rearrange("p (a b) -> p a b", b=HD)

            dve.wait_ge(pre_load, 16 * 12)
            for c in range(CC):
                last = centre(head(w_dca[:, c, 0:D]), H)
                link(last)
            link(centre(head(bdca_bc[:, 0:D]), H))
            link(nc.vector.tensor_scalar(nrm[:, 0:2], nrm[:, 0:2], SCALE, None, ALU.mult))
            for c in (0, 2):
                link(nc.vector.tensor_scalar(nrm[:, c:c + 1], nrm[:, c:c + 1], float(HD) ** 0.5, None, ALU.mult))
            dve.sem_inc(weights_centred, 3)
            link(centre(head(bkv_bc[:, 0:D]), H))
            link(centre(head(bq_bc), H))
            dve.wait_ge(dca_mm, 1)
            dve.wait_ge(weights_centred, 3)
            link(nc.vector.tensor_tensor(kn, ps[:, 0, :], bdca_bc[:, 0:D], ALU.add))
            nc.vector.tensor_tensor(vd_s, ps[:, 1, :], bdca_bc[:, D:2 * D], ALU.add).then_inc(dca_n, 2)

            def inverse_root(v, work):
                y, minus_half, a = work
                nc.vector.tensor_scalar(y.bitcast(I32), v.bitcast(I32), -0.5, float(0x5f3759df), ALU.mult, ALU.add)
                link(nc.vector.tensor_scalar(minus_half, v, -0.5, None, ALU.mult))
                for n in range(3):
                    link(nc.vector.tensor_tensor(a, y, minus_half, ALU.mult))
                    link(nc.vector.tensor_tensor(a, a, y, ALU.mult))
                    link(nc.vector.scalar_tensor_tensor(out=y if n < 2 else v, in0=a, scalar=1.5, in1=y, op0=ALU.add, op1=ALU.mult))
                    yield

            def head_norm(src, dst, m):
                link(nc.vector.tensor_tensor(t1[0:m, :], src, src, ALU.mult))
                ss = stat[0:m, 0:H]
                link(nc.vector.tensor_reduce(ss, head(t1[0:m, :]), AX, ALU.add))
                link(nc.vector.tensor_scalar(ss, ss, HD * 1e-6, None, ALU.add))
                for _ in inverse_root(ss, [stat[0:m, n * H:(n + 1) * H] for n in (1, 2, 3)]):
                    pass
                return nc.vector.scalar_tensor_tensor(out=head(dst), in0=head(src), scalar=float(HD) ** 0.5,
                                                      in1=ss.rearrange("p (a b) -> p a b", b=1).to_broadcast([m, H, HD]),
                                                      op0=ALU.mult, op1=ALU.mult)

            head_norm(kn[:, :], t0[:, :], P).then_inc(dca_n, 1)
            dve.wait_ge(dca_n, 3)
            for name, view, cc in (("w_kv", w_kv, CC), ("w_q", w_q, DC)):
                dve.wait_ge(w_loaded[name], 16)
                for c in range(cc):
                    last = centre(head(view[:, c, 0:D]), H)
                    link(last)
            dve.sem_inc(weights_centred, 1)
            dve.wait_ge(kd_ready, 1)

            count_[2] = count_[0]
            count_[0] = 0
            with dve.Fori(0, PAIRS) as i:
                count_[1] = i

                def filled(*key):
                    return wait_filled(dve, i, *key)

                def layer_norm(src, dst, signal):
                    link(nc.vector.bn_stats(stat_n[0:S, 0:6], src))
                    nc.vector.memset(stat_n[0:S, 15:16], 0.0)
                    link(nc.vector.bn_aggr(stat_n[0:S, 8:10], stat_n[0:S, 0:6]))
                    link(nc.vector.tensor_scalar(stat_n[0:S, 10:11], stat_n[0:S, 9:10], 1e-5, None, ALU.add))
                    yield
                    yield from inverse_root(stat_n[0:S, 10:11], [stat_n[0:S, n:n + 1] for n in (12, 13, 14)])
                    nc.vector.tensor_scalar(dst, src, stat_n[0:S, 8:9], stat_n[0:S, 10:11], ALU.subtract, ALU.mult).then_inc(signal.sem, 1)

                def norm_x(n, j):
                    src = x_in[j] if n == 1 else xr[j]
                    return layer_norm(src[0:S, :], xn[j][0:S, :], xn_ready)

                def wait_normed(k):
                    dve.wait_ge(xn_ready.sem, xn_ready.prior(i, k))

                def rope(src, n, table, dst, before):
                    s3 = src.rearrange("p (a b) -> p a b", b=HD)
                    a3 = t0[0:S, 0:n * HD].rearrange("p (a b) -> p a b", b=HD)
                    b3 = t1[0:S, 0:n * HD].rearrange("p (a b) -> p a b", b=HD)
                    half = HD // 2
                    tab = lambda r, lo, hi: cs[0:S, r:r + 1, lo:hi].to_broadcast([S, n, hi - lo])
                    sig, value = before
                    dve.wait_ge(sig.sem, value)
                    nc.vector.tensor_tensor(a3, s3, tab(table, 0, HD), ALU.mult)
                    nc.vector.tensor_tensor(b3[:, :, 0:half], s3[:, :, half:HD], tab(table + 1, 0, half), ALU.mult)
                    link(nc.vector.tensor_tensor(b3[:, :, half:HD], s3[:, :, 0:half], tab(table + 1, half, HD), ALU.mult))
                    return dst(a3, b3)

                def rotate(j):
                    k, k2 = filled("q", j), bank_of["k", j]
                    last_k = bank_of["k", 1 - j]
                    before = free[last_k].at(i, ("k", 0)) if j else free[last_k].before(i)
                    rope(ps[0:S, k, :], H, 0, lambda a, b: nc.vector.tensor_tensor(qr[j][0:S, :].rearrange("p (a b) -> p a b", b=HD), a, b, ALU.add),
                         (free[last_k], before)).then_inc(free[k].sem, 1)
                    filled("k", j)

                    def spread(a, b):
                        full_ = lambda v: v.rearrange("p (k g) e -> p k g e", g=1).to_broadcast([S, KV, G, HD])
                        return nc.vector.tensor_tensor(kr[j][0:S], full_(a), full_(b), ALU.add)
                    rope(ps[0:S, k2, 0:KV * HD], KV, 2, spread, (free[k], free[k].at(i, ("q", j)))).then_inc(free[k2].sem, 1)

                def kv(n):
                    key = KV_UNITS[n]
                    j, c = key
                    slot = claim_slot(key)
                    k = filled("kx", j, c)
                    nc.vector.tensor_tensor(hn[slot][0:LC, :], ps[0:LC, k, :], bkv_bc[0:LC, 0:D], ALU.add).then_inc(free[k].sem, 1)
                    k = filled("vx", j, c)
                    nc.vector.tensor_tensor(vx[j][0:LC, c, :], ps[0:LC, k, :], bkv_bc[0:LC, D:2 * D], ALU.add).then_inc(free[k].sem, 1)

                def query(j):
                    slot = claim_slot(("q", j))
                    k = filled("xq", j)
                    nc.vector.tensor_tensor(hn[slot][0:S, :], ps[0:S, k, :], bq_bc[0:S, :], ALU.add).then_inc(free[k].sem, 1)

                def claim_slot(key):
                    n = NORMS.index(key)
                    if n >= 3:
                        past = NORMS[n - 3]
                        past = ("xqT", past[1]) if past[0] == "q" else ("kxT",) + past
                        k = bank_of[past]
                        dve.wait_ge(full[k].sem, full[k].at(i, past))
                    return n % 3

                def key_T(j):
                    k = filled("kT", j)
                    nc.vector.tensor_copy(kT[j].rearrange("p a b -> p (a b)"), ps[:, k, 0:DC * S]).then_inc(free[k].sem, 1)

                def maxima(j):
                    for g in range(G):
                        k = filled("s", j, g)
                        nc.vector.tensor_reduce(nmax[j][0:S, g, :], ps[0:S, k, 0:KV * S].rearrange("p (a b) -> p a b", a=KV), AX, ALU.max,
                                                negate=True).then_inc(max_ready.sem, 1)

                def reciprocals(j):
                    for g in range(G):
                        wait_drained(dve, i, "s", j, g)
                        nc.vector.reciprocal(prec[j][0:S, g, :], psum_[j][0:S, g, :]).then_inc(rec_ready.sem, 1)

                def probs_T(j):
                    for g in range(G):
                        k = filled("pT", j, g)
                        if j:
                            dve.wait_ge(full[7].sem, full[7].at(i, ("pv", 0, 3)))
                        nc.vector.tensor_copy(pT[0:S, :, g, :], ps[0:S, k, 0:KV * S].rearrange("p (a b) -> p a b", a=KV)).then_inc(free[k].sem, 1)

                def residual(name, j):
                    k = filled(name, j)
                    dve.wait_ge(xr_ready.sem, xr_ready.at(i, (0 if name == "o" else 1, j)))
                    nc.vector.tensor_tensor(xr[j][0:S, :], xr[j][0:S, :], ps[0:S, k, :], ALU.add).then_inc(free[k].sem, 1)
                    dve.wait_ge(free[k].sem, free[k].at(i, (name, j)))

                def dca_softmax(j):
                    k = filled("ds", j)
                    d3 = ps[0:S, k, 0:H * DCA].rearrange("p (a b) -> p a b", a=H)
                    per_head = lambda v: v.rearrange("p (a b) -> p a b", b=1).to_broadcast([S, H, DCA])
                    link(nc.vector.tensor_reduce(dnm[0:S, j, :], d3, AX, ALU.max, negate=True))
                    nc.vector.tensor_tensor(dp[j][0:S], d3, per_head(dnm[0:S, j, :]), ALU.add).then_inc(free[k].sem, 1)
                    yield
                    dve.wait_ge(dexp_ready.sem, dexp_ready.at(i, j))
                    link(nc.vector.tensor_reduce(dsum[0:S, j, :], dp[j][0:S], AX, ALU.add))
                    yield
                    link(nc.vector.reciprocal(drec[0:S, j, :], dsum[0:S, j, :]))
                    nc.vector.tensor_tensor(dp[j][0:S], dp[j][0:S], per_head(drec[0:S, j, :]), ALU.mult).then_inc(dp_ready.sem, 1)

                def run(pieces):
                    for _ in pieces:
                        pass

                for j in range(2):
                    dve.wait_ge(x_loaded[j], i * 16 + 16)
                    wait_turns_filled(dve, i, 3, 4)
                    dve.wait_ge(xn_stored[j], i * 16 + 1)
                    wait_normed((1, j))
                    run(norm_x(1, j))
                rotate(0)
                kv(0)
                rotate(1)
                kv(1)
                key_T(0)
                kv(2)
                key_T(1)
                maxima(0)
                reciprocals(0)
                kv(3)
                maxima(1)
                reciprocals(1)
                kv(4)
                probs_T(0)
                probs_T(1)
                residual("o", 0)
                wait_normed((2, 0))
                run(norm_x(2, 0))
                query(0)
                residual("o", 1)
                wait_normed((2, 1))
                run(norm_x(2, 1))
                kv(5)
                dca0, dca1 = dca_softmax(0), dca_softmax(1)
                next(dca0)
                query(1)
                pieces = []
                for n in range(2 * H + XS_LAG):
                    if n < 2 * H:
                        j, h = n // H, n % H
                        k = filled("xs", n)
                        nc.vector.tensor_reduce(xnm[0:S, j, h:h + 1], ps[0:S, k, 0:LM], AX, ALU.max, negate=True).then_inc(xmax_ready.sem, 1)
                    if 1 <= n < 2 * H + 1:
                        m = n - 1
                        wait_drained(dve, i, "xs", m)
                        nc.vector.reciprocal(xrec[0:S, m // H, m % H:m % H + 1], xsum[0:S, m // H, m % H:m % H + 1]).then_inc(xrec_ready.sem, 1)
                    if n >= XS_LAG:
                        m = n - XS_LAG
                        k = filled("xpT", m)
                        if m >= NX:
                            dve.wait_ge(xpv_done.sem, xpv_done.at(i, m - NX))
                        nc.vector.tensor_copy(xpT[m % NX][0:LC].rearrange("p a b -> p (a b)"), ps[0:LC, k, 0:LN_ * S]).then_inc(free[k].sem, 1)
                    if n in (1, 2):
                        next(dca0, None)
                    if n in (DCA_EXP_1 - 1, DCA_EXP_1 + 1, DCA_EXP_1 + 2):
                        next(dca1, None)
                    if n == H + PV_LAG + 2:
                        residual("xo", 0)
                        wait_normed((3, 0))
                        norm3 = norm_x(3, 0)
                    if n > H + PV_LAG + 2:
                        next(norm3, None)
                run(norm3)
                residual("xo", 1)
                wait_normed((3, 1))
                run(norm_x(3, 1))
                assert count_[0] == LINKS, f"LINKS = {count_[0]}"
            count_[2] += LINKS * PAIRS
            count_[0] = 0
            count_[1] = None

            for k in {bank_of["gate", j] for j in range(2)}:
                dve.wait_ge(free[k].sem, free[k].before(PAIRS))
            for b in range(B):
                link(nc.vector.max(rsm[0:S, 0, b, :], lg_all[0:S, b, 0:E]))
                link(nc.vector.max_index(idx_u[0:S, b, :], rsm[0:S, 0, b, :], lg_all[0:S, b, 0:E]))
            link(nc.vector.tensor_copy(rsm[0:S, 4], idx_u[0:S]))
            nc.vector.tensor_scalar(rsm[0:S, 2, :, 0:1], rsm[0:S, 0, :, 0:1], -1.0, None, ALU.mult).then_inc(r_in, 1)
            for b in range(B):
                link(nc.vector.tensor_scalar(mask[0:S, b, :], iota_e[0:S, :], rsm[0:S, 4, b, 0:1], None, ALU.is_equal))
                for k in range(1, TOPK):
                    link(nc.vector.scalar_tensor_tensor(out=mask[0:S, b, :], in0=iota_e[0:S, :], scalar=rsm[0:S, 4, b, k:k + 1],
                                                        in1=mask[0:S, b, :], op0=ALU.is_equal, op1=ALU.add))
            dve.sem_inc(mask_ready, 1)
            dve.wait_ge(r_act, 1)
            link(nc.vector.reciprocal(rsm[0:S, 3, :, 1:2], rsm[0:S, 3, :, 0:1]))
            link(nc.vector.tensor_tensor(rsm[0:S, 5, :, 0:TOPK], rsm[0:S, 1, :, 0:TOPK],
                                         rsm[0:S, 3, :, 1:2].to_broadcast([S, B, TOPK]), ALU.mult))

            for m in range(MC):
                for half in range(2):
                    dve.wait_ge(silu_ready[m % 2], 2 * (m // 2) + half + 1)
                    dve.wait_ge(up_full[m % 2], 4 * (m // 2) + 2 * half + 2)
                    nc.vector.tensor_tensor(hT_all[:, m, half * 400:(half + 1) * 400], s_sh[half],
                                            ps[:, (m % 2) * 4 + half * 2 + 1, 0:400], ALU.mult).then_inc(hs_ready[m % 2], 1)

            dve.wait_ge(rank_full, 1)
            cnt, tiles, incl, obase = bts[:, 0, :], bts[:, 1, :], bts[:, 2, :], bts[:, 3, :]
            link(nc.vector.tensor_copy(cnt, ps[:, 1, 0:E]))
            link(nc.vector.tensor_scalar(tiles, cnt, float(T), None, ALU.is_gt))
            for n in range(2, (B * S + T - 1) // T):
                link(nc.vector.scalar_tensor_tensor(out=tiles, in0=cnt, scalar=float(n * T), in1=tiles, op0=ALU.is_gt, op1=ALU.add))
            link(nc.vector.memset(bts[:, 4, :], 1.0))
            link(nc.vector.tensor_tensor_scan(incl, bts[:, 4, :], tiles, 0.0, ALU.mult, ALU.add))
            link(nc.vector.tensor_tensor(obase, incl, tiles, ALU.subtract))
            link(nc.vector.tensor_scalar(obase, obase, float(T), float((E - 1) * T), ALU.mult, ALU.add))
            link(nc.vector.tensor_scalar(base_e[:], iota_e[:], float(T), None, ALU.mult))
            link(nc.vector.tensor_tensor(obase, obase, base_e[:], ALU.subtract))
            rank = ps[0:S, 0, 0:B * E].rearrange("p (a b) -> p a b", a=B)
            over = lambda v: v.rearrange("p (a b) -> p a b", a=1).to_broadcast([S, B, E])
            link(nc.vector.tensor_scalar(slot_e[0:S], rank, float(T), None, ALU.is_ge))
            link(nc.vector.tensor_tensor(slot_e[0:S], slot_e[0:S], over(obase[0:S]), ALU.mult))
            link(nc.vector.tensor_tensor(slot_e[0:S], slot_e[0:S], rank, ALU.add))
            link(nc.vector.tensor_tensor(slot_e[0:S], slot_e[0:S], over(base_e[0:S, :]), ALU.add))
            for k in range(TOPK):
                link(nc.vector.tensor_tensor(oh[0:S], over(iota_e[0:S, :]), rsm[0:S, 4, :, k:k + 1].to_broadcast([S, B, E]), ALU.is_equal))
                link(nc.vector.tensor_tensor(oh[0:S], oh[0:S], slot_e[0:S], ALU.mult))
                link(nc.vector.tensor_reduce(rsm[0:S, 7, :, k:k + 1], oh[0:S], AX, ALU.add))
            link(nc.vector.tensor_copy(slot_u[0:S, :].rearrange("p (a b) -> p a b", a=B), rsm[0:S, 7, :, 0:TOPK]))
            link(nc.vector.tensor_tensor(ovc, incl[0:1, :].rearrange("p (a b) -> p a b", a=1).to_broadcast([1, NOV, E]),
                                         iota_n[0:1, :].rearrange("p (a b) -> p a b", b=1).to_broadcast([1, NOV, E]), ALU.is_le))
            link(nc.vector.tensor_reduce(bts[0:1, 5, 0:NOV], ovc, AX, ALU.add))
            link(nc.vector.tensor_scalar(bts[0:1, 5, 0:NOV], bts[0:1, 5, 0:NOV], float(E - 1), None, ALU.min))
            link(nc.vector.tensor_copy(ov_i[0:1, 0:NOV], bts[0:1, 5, 0:NOV]))
            nc.vector.tensor_copy(ov_i[0:1, NOV:NOV + 1], incl[0:1, E - 1:E]).then_inc(slots_ready, 1)

            dve.wait_ge(acc_loaded, 16)
            for b in range(B):
                dve.wait_ge(dn_full, b + 1)
                nc.vector.scalar_tensor_tensor(out=acc[0:S, b, :], in0=ps[0:S, 2 + b % 2, :], scalar=rsm[0:S, 6, b, 2:3],
                                               in1=acc[0:S, b, :], op0=ALU.mult, op1=ALU.add).then_inc(dn_free, 1)

            def rows_T(r, turn):
                dve.wait_ge(xst_full[r], turn + 2)
                dve.wait_ge(up1_full[r], turn + 1)
                nc.vector.tensor_copy(xsT[r].rearrange("p a b -> p (a b)"), ps[:, r, :]).then_inc(xst_ready[r], 1)

            def hidden_parts(r):
                nc.vector.tensor_tensor(hT[r][:, 0:2, :].rearrange("p a b -> p (a b)"), sl[r][:, 0:2, :].rearrange("p a b -> p (a b)"),
                                        ps[:, 4 + r, 0:2 * T], ALU.mult)
                return nc.vector.tensor_tensor(hT[r][0:96, 2, :], sl[r][0:96, 2, :], ps[0:96, 4 + r, 2 * T:3 * T], ALU.mult)

            def hidden(r, turn):
                dve.wait_ge(sl_ready[r], turn + 1)
                dve.wait_ge(y_full[r], turn + 1)
                hidden_parts(r).then_inc(h_ready[r], 1)

            rows_T(0, 0)
            rows_T(1, 0)
            hidden(0, 0)
            with dve.Fori(0, E // 2 - 1) as i:
                rows_T(0, i + 1)
                hidden(1, i)
                rows_T(1, i + 1)
                hidden(0, i + 1)
            hidden(1, E // 2 - 1)
            dve.wait_ge(slots_ready, 1)
            count = dve.value_load(ov_i[0:1, NOV:NOV + 1], min_val=0, max_val=NOV)
            with dve.Fori(0, NOV) as t:
                with dve.If(count > t):
                    dve.wait_ge(o_t, t + 1)
                    nc.vector.tensor_copy(xsT[0].rearrange("p a b -> p (a b)"), ps[:, 0, :]).then_inc(o_tc, 1)
                    dve.wait_ge(o_s, t + 1)
                    hidden_parts(0).then_inc(o_h, 1)
            dve.wait_ge(dn_free, B)
            for b in range(B):
                for k in range(TOPK):
                    n = b * TOPK + k
                    dve.wait_ge(gathered[n % 4], 16 * (n // 4 + 1))
                    ins = nc.vector.scalar_tensor_tensor(out=acc[0:S, b, :], in0=xn3[0:S, n % 4, :], scalar=rsm[0:S, 5, b, k:k + 1],
                                                         in1=acc[0:S, b, :], op0=ALU.mult, op1=ALU.add)
                    ins.then_inc(added[n % 4], 1)
                    dve.wait_ge(added[n % 4], n // 4 + 1)
                dve.sem_inc(out_ready, 1)


def kernel(x, ctx_1024, L0_attn_W_attn, L0_attn_W_out, L0_attn_b_out, L0_xattn_Wq, L0_xattn_bq, L0_xattn_Wk, L0_xattn_bk,
           L0_xattn_Wv, L0_xattn_bv, L0_xattn_Wkv_dca, L0_xattn_bkv_dca, L0_xattn_qn_w, L0_xattn_qn_b, L0_xattn_kn_w,
           L0_xattn_kn_b, L0_xattn_kn_dca_w, L0_xattn_kn_dca_b, L0_xattn_Wo, L0_xattn_bo, L0_ffn_gate_w,
           L0_ffn_shared_gate_w, L0_ffn_w13, L0_ffn_w2, L0_ffn_se_gate_up_w, L0_ffn_se_down_w):
    import numpy as np
    import concourse.bacc as bacc
    from concourse.bass_utils import run_bass_kernel_spmd

    a = np.asarray
    ctx = a(ctx_1024)
    by_kind = lambda w: w.reshape(w.shape[:-1] + (H, 2, HD)).swapaxes(-3, -2).reshape(w.shape)
    inv = (1.0 / np.float32(10000.0) ** (np.arange(0, HD, 2, dtype=np.float32) / np.float32(HD))).astype(np.float32)
    ang = np.arange(S, dtype=np.float32)[:, None] * inv[None, :]
    cos, sin = np.cos(ang), np.sin(ang)
    table = np.stack([np.concatenate([cos, cos], 1), np.concatenate([-sin, sin], 1)], 1)
    cos_sin = np.concatenate([table * np.float32(SCALE), table], 1).astype(np.float32)
    se_up = a(L0_ffn_se_gate_up_w).T.reshape(DC, P, 2, MC, P).transpose(3, 1, 0, 2, 4).reshape(MC, P, DC, 2 * P)
    arrays = {
        "x": a(x),
        "ctxT": ctx[:, :LM, :].transpose(0, 2, 1).reshape(B, CC, P, LM).transpose(0, 2, 1, 3),
        "dcaT": ctx[:, LM:, :].reshape(B * DCA, CC * P).T.reshape(CC, P, B * DCA),
        "W_attn": a(L0_attn_W_attn), "W_out": a(L0_attn_W_out), "b_out": a(L0_attn_b_out),
        "Wq": a(L0_xattn_Wq), "bq": a(L0_xattn_bq),
        "Wkv": by_kind(np.concatenate([a(L0_xattn_Wk), a(L0_xattn_Wv)], 1)),
        "bkv": by_kind(np.concatenate([a(L0_xattn_bk), a(L0_xattn_bv)])),
        "Wdca": a(L0_xattn_Wkv_dca), "bdca": a(L0_xattn_bkv_dca),
        "norm": np.stack([a(v) for v in (L0_xattn_qn_w, L0_xattn_qn_b, L0_xattn_kn_w, L0_xattn_kn_b,
                                         L0_xattn_kn_dca_w, L0_xattn_kn_dca_b)], 1),
        "Wo": a(L0_xattn_Wo), "bo": a(L0_xattn_bo),
        "gates": np.concatenate([a(L0_ffn_gate_w).T, a(L0_ffn_shared_gate_w).T], 1),
        "w13": a(L0_ffn_w13).transpose(0, 2, 1).reshape(E, DC, P, 2 * I).transpose(0, 2, 1, 3),
        "w2": a(L0_ffn_w2).transpose(0, 2, 1),
        "se_up": se_up, "se_down": a(L0_ffn_se_down_w).T, "cos_sin": cos_sin,
    }
    nc = bacc.Bacc("TRN2", target_bir_lowering=False, num_devices=1)
    sent, args = {}, []
    for name, v in arrays.items():
        v = np.ascontiguousarray(v)
        sent[f"in_{name}"] = v
        args.append(nc.dram_tensor(f"in_{name}", v.shape, mybir.dt.from_np(v.dtype), kind="ExternalInput").ap())
    result = nc.dram_tensor("result", (B, S, D), F32, kind="ExternalOutput").ap()
    decoder_kernel(nc, *args, result)
    return run_bass_kernel_spmd(nc, [sent], core_ids=[0]).results[0]["result"]
```

```python
from contextlib import ExitStack

import concourse.bass as bass
from concourse import mybir

F32 = mybir.dt.float32
U32 = mybir.dt.uint32
I32 = mybir.dt.int32
ALU = mybir.AluOpType
ACT = mybir.ActivationFunctionType
AX = mybir.AxisListType.X

P = 128
B, S, D = 8, 100, 512
DC = D // P
H, KV, G = 16, 4, 4
HD = 32
VD = 128
QK = (H + KV) * HD
L, DCA = 361, 16
LM = L - DCA
LC, LN_ = 115, 3
CC = 2
E, I = 60, 352
IC = (128, 128, 96)
ISH = 1408
MC = ISH // P
TOPK = 4
NORM_STEPS = 20
LINKS = 88
T = 116
NOV = (B * S * TOPK - 1) // T
ZERO_FILLS = 10
NG = E + 1
PAIRS = B // 2
SCALE = HD ** -0.5


class Signal:

    all = []

    def __init__(self, sem, keys):
        self.sem, self.keys = sem, list(keys)
        Signal.all.append(self)

    def at(self, i, key):
        return i * len(self.keys) + (self.keys.index(key) + 2)

    def before(self, i):
        return i * len(self.keys) + 1

    def prior(self, i, key):
        return i * len(self.keys) + (self.keys.index(key) + 1)


KV_UNITS = [(j, c) for c in range(LN_) for j in range(2)]
XS_LAG, PV_LAG = 3, 5

def scalar_copies(head):
    return head >= H and head % 2 == 1


DCA_EXP_1 = 16


def attention_fills():
    u = KV_UNITS
    unit = lambda n: [(("kx",) + u[n], 6), (("vx",) + u[n], 7)]
    kxT = lambda n, b: [(("kxT",) + u[n], b)]
    out = [(("xT1", 0), 4), (("xT1", 1), 5)]
    out += [(("q", 0), 0), (("k", 0), 1), (("v", 0), 2), (("xT3", 1), 4)] + unit(0)[:1] + [(("gate", 1), 5)] + unit(0)[1:]
    out += [(("q", 1), 3), (("k", 1), 4), (("v", 1), 5)] + unit(1)
    out += [(("qT", 0), 0), (("kT", 0), 1)] + unit(2) + kxT(0, 2)
    out += [(("qT", 1), 0), (("kT", 1), 1)]
    out += [(("s", 0, g), 2 + g) for g in range(G)]
    out += unit(3) + kxT(1, 0)
    out += [(("s", 1, g), 2 + g) for g in range(G)]
    out += unit(4)
    out += [(("pT", 0, g), g % 2) for g in range(G)]
    out += [(("pv", 0, 0), 6), (("pv", 0, 1), 7)] + kxT(2, 2) + [(("pv", 0, 2), 6), (("pv", 0, 3), 7)]
    out += [(("pT", 1, g), 2 + g) for g in range(G)]
    out += [(("pv", 1, 0), 6), (("o", 0), 0), (("pv", 1, 1), 7), (("pv", 1, 2), 6)]
    out += [(("xT2", 0), 4), (("xq", 0), 3)] + kxT(3, 5) + [(("pv", 1, 3), 7), (("o", 1), 1)]
    out += unit(5) + kxT(4, 5)
    out += [(("xqT", 0), 2), (("ds", 0), 3)]
    for n in range(2 * H + PV_LAG):
        out += [(key, 3) for key in HEAD_HOOKS.get(n, [])]
        if n < 2 * H:
            out.append((("xs", n), n % 3))
        if XS_LAG <= n < 2 * H + XS_LAG:
            out.append((("xpT", n - XS_LAG), 4 + n % 2))
        if n >= PV_LAG and (n - PV_LAG) % H == H - 1:
            out.append((("ctx", (n - PV_LAG) // H), 6 + (n - PV_LAG) // H))
    out += [(("xo", 1), 0)]
    return out


HEAD_HOOKS = {2: [("xT2", 1)], 3: [("xq", 1)], 4: [("dpT", 0)], 9: [("kxT", 1, 2)], 14: [("xqT", 1)], 15: [("ds", 1)],
              20: [("dpT", 1)],
              H + PV_LAG + 1: [("xo", 0)], H + PV_LAG + 10: [("xT3", 0)], H + PV_LAG + 11: [("gate", 0)]}


def decoder_kernel(nc, x, ctxT, dcaT, W_attn, W_out, b_out, Wq, bq, Wkv, bkv, Wdca, bdca, norm, Wo, bo,
                   gates, w13, w2, se_up, se_down, cos_sin, out):
    fills = attention_fills()
    bank_of = dict(fills)
    Signal.all = []

    cm = ExitStack()
    with cm:
        def sb(name, shape, dt=F32):
            return cm.enter_context(nc.sbuf_tensor(name, shape, dt))

        def sem(name):
            return cm.enter_context(nc.semaphore(name))

        xn3_d = nc.dram_tensor("xn3_d", [B, S, D], F32, kind="Internal").ap()
        x2_d = nc.dram_tensor("x2_d", [B, S, D], F32, kind="Internal").ap()
        xT3_d = nc.dram_tensor("xT3_d", [B, P, DC * S], F32, kind="Internal").ap()
        vd_d = nc.dram_tensor("vd_d", [P, D], F32, kind="Internal").ap()
        xs_d = nc.dram_tensor("xs_d", [(E + NOV) * T, D], F32, kind="Internal").ap()
        ys_d = nc.dram_tensor("ys_d", [(E + NOV) * T, D], F32, kind="Internal").ap()

        ps = cm.enter_context(nc.psum_tensor("ps", [P, 8, 512], F32))

        ident = sb("ident", [P, P])
        ones = sb("ones", [P, P])
        tri = sb("tri", [P, P])
        zero = sb("zero", [P, D])
        lg_late = sb("lg_late", [P, B + 2, NG])
        lg_all = lg_late[:, 2:B + 2, :]

        ARENA = 51250
        arena = sb("arena", [P, ARENA])
        top = [0]

        def carve(*shape):
            n = 1
            for d in shape:
                n *= d
            a = arena[:, top[0]:top[0] + n]
            top[0] += n
            assert top[0] <= ARENA, top[0]
            if len(shape) == 2:
                return a.rearrange("p (a b) -> p a b", a=shape[0])
            if len(shape) == 3:
                return a.rearrange("p (a b c) -> p a b c", a=shape[0], b=shape[1])
            if len(shape) == 4:
                return a.rearrange("p (a b c d) -> p a b c d", a=shape[0], b=shape[1], c=shape[2])
            return a

        w_attn = carve(DC, QK + D)
        w_out = carve(H, D)
        w_q = carve(DC, D)
        w_kv = carve(CC, 2 * D)
        w_o = carve(DC, D)
        w_gate = carve(DC, NG)
        bo_bc = carve(D)
        bout_bc = carve(D)
        bq_bc = carve(D)
        bkv_bc = carve(2 * D)
        cs = carve(4, HD)
        nrm = carve(6)
        blk_k = carve(4)
        blk_v = carve(8)
        kd_all = carve(DC, P)
        vd_all = carve(B, 2, HD)
        x_in = [carve(D) for _ in range(2)]
        xr = [carve(D) for _ in range(2)]
        xn = [carve(D) for _ in range(2)]
        xT = [carve(DC, S) for _ in range(2)]
        t0 = carve(D)
        t1 = carve(D)
        stat = carve(64)
        stat_n = carve(16)
        qr = [carve(D) for _ in range(2)]
        kr = [carve(KV, G, HD) for _ in range(2)]
        v_s = [carve(D) for _ in range(2)]
        qT = [carve(KV, S) for _ in range(2)]
        kT = [carve(KV, S) for _ in range(2)]
        nmax = [carve(G, KV) for _ in range(2)]
        psum_ = [carve(G, KV) for _ in range(2)]
        prec = [carve(G, KV) for _ in range(2)]
        NP_ = 8
        preamble_at = top[0]
        pr = [carve(KV, S) for _ in range(NP_)]
        pT = carve(KV, G, S)
        cT = [carve(G, S) for _ in range(2)]
        c_in = [carve(CC, LM) for _ in range(2)]
        hn = [carve(D) for _ in range(3)]
        sq = carve(D)
        root = [carve(H) for _ in range(3)]
        vx = [carve(LN_, D) for _ in range(2)]
        kxT = [carve(DC, LM) for _ in range(2)]
        xqT = [carve(DC, S) for _ in range(2)]
        kdb = [carve(DC, 4, DCA) for _ in range(2)]
        vdb = [carve(2, 8, HD) for _ in range(2)]
        dnm = carve(2, H)
        dsum = carve(2, H)
        drec = carve(2, H)
        dp = [carve(H, DCA) for _ in range(2)]
        dpT = [carve(2, S) for _ in range(2)]
        xnm = carve(2, H)
        xsum = carve(2, H)
        xrec = carve(2, H)
        NX = 4
        xp = [pr[n].rearrange("p a b -> p (a b)")[:, 0:LM] for n in range(NX)]
        pT_flat = pT.rearrange("p a b c -> p (a b c)")
        xpT = [pT_flat[:, n * LN_ * S:(n + 1) * LN_ * S].rearrange("p (a b) -> p a b", a=LN_) for n in range(NX)]
        cxT = cT
        x1 = qr
        kn = hn[0]
        vd_s = sq
        top[0] = preamble_at
        w_dca = carve(CC, 2 * D)
        bdca_bc = carve(2 * D)
        c_dca = carve(CC, P)

        top[0] = 0
        xT3 = carve(B, DC * S)
        se_w = [carve(DC, 2 * P) for _ in range(3)]
        hT_all = carve(MC, B * S)
        w_down = carve(MC, D)
        acc = carve(B, D)
        w13_s = [carve(DC, 2 * I) for _ in range(2)]
        w2_s = [carve(3, D) for _ in range(2)]
        xs_s = [carve(D) for _ in range(2)]
        xsT = [carve(DC, T) for _ in range(2)]
        sl = [carve(3, T) for _ in range(2)]
        hT = [carve(3, T) for _ in range(2)]
        y_s = [carve(D) for _ in range(2)]
        s_sh = [carve(400) for _ in range(2)]
        xn3 = carve(B, D)
        oh = carve(B, E)
        mask = carve(B, E)
        mask_sum = carve(B, E)
        slot_e = carve(B, E)
        bts = carve(6, E)
        ovc = carve(NOV, E)[0:1]
        rsm = carve(8, B, 8)
        half3 = sb("three_halves", [P, H])
        iota_e = sb("iota_e", [P, E])
        iota_n = sb("iota_n", [P, NOV])
        base_e = sb("base_e", [P, E])
        ov_i = sb("ov_i", [1, NOV + 1], I32)
        slot_u = sb("slot_u", [P, B * TOPK], U32)
        idx_u = sb("idx_u", [P, B, 8], U32)

        full = [Signal(sem(f"bank{n}_full"), [k for k, b in fills if b == n and k[0] != "ctx"]) for n in range(8)]
        free = [Signal(sem(f"bank{n}_free"), [k for k, b in fills if b == n]) for n in range(8)]
        pre_load = sem("preamble_loaded")
        dca_load = sem("dca_loaded")
        w_loaded = {n: sem(f"{n}_loaded") for n in ("w_attn", "w_out", "w_q", "w_kv", "w_o", "w_gate")}
        consts_ready = sem("consts_ready")
        weights_centred = sem("weights_centred")
        kv_centred = sem("kv_weights_centred")
        q_centred = sem("q_weights_centred")
        pool_pre = sem("pool_preamble")
        kd_ready = sem("kd_ready")
        vd_stored = sem("vd_stored")
        vd_loaded = sem("vd_loaded")
        dca_mm = sem("dca_projected")
        dca_n = sem("dca_normed")
        dca_t = sem("dca_transposed")
        x_loaded = [sem(f"x_loaded{j}") for j in range(2)]
        c_loaded = [sem(f"c_loaded{j}") for j in range(2)]
        xn_stored = [sem(f"xn3_stored{j}") for j in range(2)]
        x2_stored = [sem(f"x2_stored{j}") for j in range(2)]
        xT_stored = [sem(f"xT3_stored{j}") for j in range(2)]
        zeroed = sem("slots_zeroed")
        chain = sem("vector_chain")
        pairs = [0, 1]
        late_full = sem("last_gate_full")
        late_free = sem("last_gate_free")
        xn_ready = Signal(sem("xn_ready"), [(n, j) for n in (2, 3) for j in pairs])
        x1_ready = sem("x1_ready")
        jg = [(j, g) for j in pairs for g in range(G)]
        max_ready = Signal(sem("max_ready"), jg)
        rec_ready = Signal(sem("rec_ready"), jg)
        p_ready = Signal(sem("p_ready"), jg)
        xr_ready = Signal(sem("xr_ready"), [(n, j) for n in (0, 1) for j in pairs])
        u = KV_UNITS
        NORMS = u[:5] + [("q", 0), u[5], ("q", 1)]
        hn_ready = Signal(sem("heads_normed"), NORMS)
        pool_step = Signal(sem("pool_chain"), [(k, n) for k in NORMS for n in range(NORM_STEPS)])
        dp_ready = Signal(sem("dca_probs_ready"), pairs)
        db_ready = Signal(sem("dca_blocks_ready"), pairs)
        dexp_ready = Signal(sem("dexp_ready"), pairs)
        hh = list(range(2 * H))
        xmax_ready = Signal(sem("xmax_ready"), hh)
        xrec_ready = Signal(sem("xrec_ready"), hh)
        xp_ready = [Signal(sem(f"xp_ready{j}"), range(H)) for j in range(2)]
        xpv_done = Signal(sem("xpv_done"), hh)
        cT_used = Signal(sem("context_part_used"), [(0, 0), (0, 1), (0, 2), (1, 0), (1, 1), (1, 2)])

        xT3_early = sem("xT3_first_loaded")
        xT3_loaded = sem("xT3_loaded")
        se_loaded = [sem(f"se_loaded{r}") for r in range(3)]
        down_loaded = sem("down_loaded")
        acc_loaded = sem("acc_loaded")
        xn3_loaded = sem("xn3_loaded")
        up_full = [sem(f"up_full{r}") for r in range(2)]
        silu_ready = [sem(f"shared_silu{r}") for r in range(2)]
        hs_ready = [sem(f"shared_h{r}") for r in range(2)]
        dn_full = sem("shared_down_full")
        dn_free = sem("shared_down_free")
        r_act = sem("router_exp")
        r_in = sem("router_in")
        mask_ready = sem("mask_ready")
        rank_full = sem("rank_full")
        slots_ready = sem("slots_ready")
        scattered = sem("scattered")
        w13_loaded = [sem(f"w13_loaded{r}") for r in range(2)]
        w2_loaded = [sem(f"w2_loaded{r}") for r in range(2)]
        xs_loaded = [sem(f"xs_loaded{r}") for r in range(2)]
        xst_full = [sem(f"xst_full{r}") for r in range(2)]
        xst_ready = [sem(f"xst_ready{r}") for r in range(2)]
        up1_full = [sem(f"gate_up_full{r}") for r in range(2)]
        sl_ready = [sem(f"silu_ready{r}") for r in range(2)]
        h_ready = [sem(f"h_ready{r}") for r in range(2)]
        y_full = [sem(f"y_full{r}") for r in range(2)]
        y_ready = [sem(f"y_ready{r}") for r in range(2)]
        y_stored = [sem(f"y_stored{r}") for r in range(2)]
        o_w = sem("over_loaded")
        o_t = sem("over_transposed")
        o_tc = sem("over_xT")
        o_g = sem("over_gate_up")
        o_s = sem("over_silu")
        o_h = sem("over_h")
        o_y = sem("over_y")
        o_yc = sem("over_y_copied")
        o_st = sem("over_stored")
        gathered = [sem(f"gathered{r}") for r in range(4)]
        added = [sem(f"added{r}") for r in range(4)]
        out_ready = sem("out_ready")
        load_gate = sem("load_gate")
        out_stored = sem("out_stored")

        by_turns = (x2_stored + xn_stored + xT_stored + up1_full + xst_full + y_full + h_ready + y_ready + xst_ready + y_stored
                    + [o_y, o_yc, o_st])

        block = cm.enter_context(nc.Block())

        def bank(n):
            return ps[:, n, :]

        def wait_filled(eng, i, *key):
            k = bank_of[key]
            eng.wait_ge(full[k].sem, full[k].at(i, key))
            return k

        def wait_drained(eng, i, *key):
            k = bank_of[key]
            eng.wait_ge(free[k].sem, free[k].at(i, key))

        @block.sync
        def _(sp):
            bc = lambda v, n: v.rearrange("(a d) -> a d", a=1).to_broadcast([P, n])
            def load_x(i):
                for j in range(2):
                    sp.dma_start(x_in[j][0:S, :], x[i * 2 + j, :, :]).then_inc(x_loaded[j], 16)

            def load_context(i):
                for j in range(2):
                    sp.dma_start(c_in[j], ctxT[i * 2 + j, :, :, :]).then_inc(c_loaded[j], 16)

            load_x(0)
            sp.dma_start(c_dca, dcaT.rearrange("c p n -> p c n")).then_inc(dca_load, 16)
            sp.dma_start(w_dca, Wdca.rearrange("(c p) n -> p c n", p=P)).then_inc(dca_load, 16)
            sp.dma_start(bdca_bc, bc(bdca, 2 * D)).then_inc(dca_load, 16)
            for g in range(4):
                sp.dma_start(nrm[g * HD:(g + 1) * HD, :], norm).then_inc(pre_load, 16)
            sp.dma_start(cs[0:S], cos_sin).then_inc(pre_load, 16)
            sp.dma_start(bkv_bc, bc(bkv, 2 * D)).then_inc(pre_load, 16)
            sp.dma_start(bq_bc, bc(bq, D)).then_inc(pre_load, 16)
            sp.dma_start(bout_bc, bc(b_out, D)).then_inc(pre_load, 16)
            sp.dma_start(bo_bc, bc(bo, D)).then_inc(pre_load, 16)
            sp.dma_start(w_kv, Wkv.rearrange("(c p) n -> p c n", p=P)).then_inc(w_loaded["w_kv"], 16)
            sp.dma_start(w_q, Wq.rearrange("(c p) n -> p c n", p=P)).then_inc(w_loaded["w_q"], 16)
            sp.dma_start(w_attn, W_attn.rearrange("(c p) n -> p c n", p=P)).then_inc(w_loaded["w_attn"], 16)
            load_context(0)
            sp.wait_ge(dca_n, 2)
            sp.dma_start(vd_d, vd_s).then_inc(vd_stored, 16)
            sp.dma_start(w_out, W_out.rearrange("(c p) n -> p c n", p=P)).then_inc(w_loaded["w_out"], 16)
            sp.wait_ge(vd_stored, 16)
            vsrc = vd_d.rearrange("(b r) (c h e) -> r b c h e", b=B, c=2, h=8)
            for h in range(8):
                for c in range(2):
                    sp.dma_start(vd_all[h * DCA:(h + 1) * DCA, :, c, :], vsrc[:, :, c, h, :]).then_inc(vd_loaded, 16)
            sp.dma_start(w_o, Wo.rearrange("(c p) n -> p c n", p=P)).then_inc(w_loaded["w_o"], 16)
            sp.dma_start(w_gate, gates.rearrange("(c p) n -> p c n", p=P)).then_inc(w_loaded["w_gate"], 16)
            sp.wait_ge(pool_pre, 7)
            def fill_zeros(rows, first, last):
                for n in range(first, last, 13):
                    m = min(13, last - n)
                    sp.dma_start(rows[n * T:(n + m) * T, :].rearrange("(a p) d -> p a d", p=T),
                                 zero[0:T, :].rearrange("p (a d) -> p a d", a=1).to_broadcast([T, m, D])).then_inc(zeroed, 16)
                return -(-(last - first) // 13)

            fills_started = fill_zeros(xs_d, 0, E + NOV)
            fills_started += fill_zeros(ys_d, E, E + NOV)
            assert fills_started == ZERO_FILLS

            def load_up(m):
                if m >= 3:
                    sp.wait_ge(up_full[(m - 3) % 2], 4 * ((m - 3) // 2 + 1))
                sp.dma_start(se_w[m % 3], se_up[m, :, :, :]).then_inc(se_loaded[m % 3], 16)

            def load_tokens(first, last, signal):
                sp.dma_start(xT3[:, first:last, :], xT3_d[first:last].rearrange("b p n -> p b n")).then_inc(signal, 16)

            def store_last_T(i):
                sp.dma_start(xT3_d[i * 2 + 1, :, :], cxT[1].rearrange("p a b -> p (a b)")).then_inc(xT_stored[1], 16)

            for i in range(PAIRS):
                if i:
                    wait_drained(sp, i, "xT3", 1)
                    store_last_T(i - 1)
                sp.wait_ge(x1_ready, i * 2 + 2)
                sp.wait_ge(xr_ready.sem, xr_ready.at(i, (0, 1)))
                load_x(min(i + 1, PAIRS - 1))
                if i + 1 < PAIRS:
                    sp.wait_ge(full[7].sem, full[7].at(i, ("vx",) + KV_UNITS[-1]))
                    load_context(i + 1)
                else:
                    sp.wait_ge(full[1].sem, full[1].at(i, ("o", 1)))
                    for j in range(2):
                        sp.wait_ge(xT_stored[j], 16 * i + 1)
                    load_tokens(0, 2 * i, xT3_early)
                    for m in range(3):
                        load_up(m)
                for j in range(2):
                    sp.wait_ge(xn_ready.sem, xn_ready.at(i, (3, j)))
                    if j == 0:
                        wait_drained(sp, i, "xT3", 0)
                        sp.dma_start(xT3_d[i * 2, :, :], xT[0].rearrange("p a b -> p (a b)")).then_inc(xT_stored[0], 16)
                    elif i == PAIRS - 1:
                        sp.wait_ge(xT_stored[0], 16 * PAIRS + 1)
                        load_tokens(2 * i, 2 * i + 1, xT3_loaded)
                        sp.wait_ge(late_free, 1)
                        store_last_T(i)
                    sp.dma_start(xn3_d[i * 2 + j, :, :], xn[j][0:S, :]).then_inc(xn_stored[j], 16)
                    sp.dma_start(x2_d[i * 2 + j, :, :], xr[j][0:S, :]).then_inc(x2_stored[j], 16)

            for k in range(8):
                sp.wait_ge(full[k].sem, full[k].before(PAIRS))
                sp.wait_ge(free[k].sem, free[k].before(PAIRS))
            sp.wait_ge(late_free, 2)
            for j in range(2):
                sp.wait_ge(xn_stored[j], 16 * PAIRS + 1)
                sp.wait_ge(x2_stored[j], 16 * PAIRS + 1)
                sp.wait_ge(xT_stored[j], 16 * PAIRS + 1)
            load_tokens(2 * PAIRS - 1, 2 * PAIRS, xT3_loaded)
            sp.dma_start(xn3[0:S], xn3_d.rearrange("b s d -> s b d")).then_inc(xn3_loaded, 16)
            sp.dma_start(acc[0:S], x2_d.rearrange("b s d -> s b d")).then_inc(acc_loaded, 16)
            sp.dma_start(w_down, se_down.rearrange("(c p) n -> p c n", p=P)).then_inc(down_loaded, 16)
            for m in range(3, MC):
                load_up(m)
            def load_13(r, turn, e):
                sp.wait_ge(up1_full[r], turn + 1)
                sp.sem_inc(load_gate, 1)
                sp.dma_start(w13_s[r], w13[e, :, :, :]).then_inc(w13_loaded[r], 16)

            def load_rows(r, turn, e):
                sp.wait_ge(xst_full[r], turn + 1)
                sp.sem_inc(load_gate, 1)
                sp.dma_start(xs_s[r][0:T], xs_d[bass.ds(e * T, T), :]).then_inc(xs_loaded[r], 16)

            def load_2(r, turn, e):
                sp.wait_ge(y_full[r], turn + 1)
                sp.sem_inc(load_gate, 1)
                sp.dma_start(w2_s[r][:, 0:2, :], w2[e, 0:256, :].rearrange("(c p) n -> p c n", p=P)).then_inc(w2_loaded[r], 16)
                sp.dma_start(w2_s[r][0:96, 2, :], w2[e, 256:I, :]).then_inc(w2_loaded[r], 16)

            load_13(0, 0, 0)
            load_13(1, 0, 1)
            load_2(0, 0, 0)
            load_2(1, 0, 1)
            sp.wait_ge(scattered, 16 * B * TOPK)
            load_rows(0, 0, 0)
            load_rows(1, 0, 1)
            load_rows(0, 1, 2)
            load_rows(1, 1, 3)
            load_13(0, 1, 2)
            with sp.Fori(0, E // 2 - 2) as i:
                load_rows(0, i + 2, i * 2 + 4)
                load_13(1, i + 1, i * 2 + 3)
                load_2(0, i + 1, i * 2 + 2)
                load_rows(1, i + 2, i * 2 + 5)
                load_13(0, i + 2, i * 2 + 4)
                load_2(1, i + 1, i * 2 + 3)
            load_13(1, E // 2 - 1, E - 1)
            load_2(0, E // 2 - 1, E - 2)
            load_2(1, E // 2 - 1, E - 1)
            sp.wait_ge(slots_ready, 1)
            sp.wait_ge(up1_full[1], E // 2 + 1)
            sp.wait_ge(y_full[0], E // 2 + 1)
            sp.wait_ge(xst_full[0], E // 2 + 1)
            count = sp.value_load(ov_i[0:1, NOV:NOV + 1], min_val=0, max_val=NOV)
            with sp.If(count > 0):
                with sp.Fori(0, NOV) as t:
                    with sp.If(count > t):
                        e = sp.value_load(ov_i[0:1, bass.ds(t, 1)], min_val=0, max_val=E - 1)
                        sp.wait_ge(o_y, t + 1)
                        sp.sem_inc(load_gate, 1)
                        sp.dma_start(w13_s[0], w13[e, :, :, :]).then_inc(o_w, 16)
                        sp.dma_start(xs_s[0][0:T], xs_d[bass.ds(t * T + E * T, T), :]).then_inc(o_w, 16)
                        sp.dma_start(w2_s[0][:, 0:2, :], w2[e, 0:256, :].rearrange("(c p) n -> p c n", p=P)).then_inc(o_w, 16)
                        sp.dma_start(w2_s[0][0:96, 2, :], w2[e, 256:I, :]).then_inc(o_w, 16)
            for b in range(B):
                sp.wait_ge(out_ready, b + 1)
                sp.dma_start(out[b, :, :], acc[0:S, b, :]).then_inc(out_stored, 16)
            sp.wait_ge(out_stored, 16 * B)

        @block.gpsimd
        def _(pool):
            for s in [signal.sem for signal in Signal.all] + by_turns:
                pool.sem_inc(s, 1)
            nc.gpsimd.memset(zero[:], 0.0).then_inc(pool_pre, 1)
            nc.gpsimd.memset(ones[:], 1.0).then_inc(pool_pre, 1)
            nc.gpsimd.memset(half3[:], 1.5).then_inc(pool_pre, 1)
            nc.gpsimd.memset(xn[1][:, :], 0.0).then_inc(consts_ready, 1)
            nc.gpsimd.iota(iota_e[:], pattern=[[1, E]], base=0, channel_multiplier=0,
                           allow_small_or_imprecise_dtypes=True).then_inc(consts_ready, 1)
            nc.gpsimd.iota(iota_n[:], pattern=[[1, NOV]], base=0, channel_multiplier=0,
                           allow_small_or_imprecise_dtypes=True).then_inc(consts_ready, 1)
            pool.wait_ge(pool_pre, 3)
            nc.gpsimd.affine_select(out=ident[:], in_=ones[:], compare_op=ALU.is_equal, fill=0.0, base=0,
                                    pattern=[[-1, P]], channel_multiplier=1).then_inc(consts_ready, 1)
            nc.gpsimd.affine_select(out=tri[:], in_=ones[:], compare_op=ALU.is_gt, fill=0.0, base=0,
                                    pattern=[[1, P]], channel_multiplier=-1).then_inc(consts_ready, 1)
            for width, m, n in ((HD, blk_k, 4), (DCA, blk_v, 8)):
                nc.gpsimd.affine_select(out=m, in_=ones[:, 0:n], compare_op=ALU.is_ge, fill=0.0, base=0,
                                        pattern=[[-width, n]], channel_multiplier=1).then_inc(pool_pre, 1)
            pool.wait_ge(pool_pre, 5)
            for width, m, n in ((HD, blk_k, 4), (DCA, blk_v, 8)):
                nc.gpsimd.affine_select(out=m, in_=m, compare_op=ALU.is_ge, fill=0.0, base=width - 1,
                                        pattern=[[width, n]], channel_multiplier=-1).then_inc(pool_pre, 1)
            pool.wait_ge(pool_pre, 7)
            pool.wait_ge(w_loaded["w_q"], 16)
            done = 0
            for c in range(DC):
                w3 = w_q[:, c, :].rearrange("p (a b) -> p a b", b=HD)
                m3 = kxT[1].rearrange("p a b -> p (a b)")[:, 0:D].rearrange("p (a b) -> p a b", b=HD)
                src, w = w3, HD // 2
                while w:
                    nc.gpsimd.tensor_tensor(m3[:, :, 0:w], src[:, :, 0:w], src[:, :, w:2 * w], ALU.add).then_inc(pool_pre, 1)
                    done += 1
                    pool.wait_ge(pool_pre, 7 + done)
                    src, w = m3, w // 2
                nc.gpsimd.tensor_scalar(m3[:, :, 0:1], m3[:, :, 0:1], 1.0 / HD, None, ALU.mult).then_inc(pool_pre, 1)
                done += 1
                pool.wait_ge(pool_pre, 7 + done)
                nc.gpsimd.tensor_tensor(w3, w3, m3[:, :, 0:1].to_broadcast([P, H, HD]), ALU.subtract).then_inc(q_centred, 4)
                pool.wait_ge(q_centred, 4 * (c + 1))
            pool.wait_ge(pre_load, 16 * 9)
            pool.wait_ge(vd_loaded, 16 * 16)
            pool.wait_ge(kd_ready, 1)
            with pool.Fori(0, PAIRS) as i:
                for j in range(2):
                    pool.wait_ge(x_loaded[j], i * 16 + 16)
                    pool.wait_ge(x2_stored[j], i * 16 + 1)
                    nc.gpsimd.tensor_tensor(xr[j][0:S, :], x_in[j][0:S, :], bout_bc[0:S, :], ALU.add).then_inc(xr_ready.sem, 1)
                for j in range(2):
                    pool.wait_ge(xpv_done.sem, xpv_done.before(i))
                    for c in range(DC):
                        nc.gpsimd.tensor_tensor(kdb[j][:, c, :, :],
                                                kd_all[:, c:c + 1, bass.ds((i * 2 + j) * DCA, DCA)].to_broadcast([P, 4, DCA]),
                                                blk_k.rearrange("p (a b) -> p a b", b=1).to_broadcast([P, 4, DCA]), ALU.mult)
                    for c in range(2):
                        last = nc.gpsimd.tensor_tensor(vdb[j][:, c, :, :],
                                                       vd_all[:, bass.ds(i * 2 + j, 1), c, :].to_broadcast([P, 8, HD]),
                                                       blk_v.rearrange("p (a b) -> p a b", b=1).to_broadcast([P, 8, HD]), ALU.mult)
                    last.then_inc(db_ready.sem, 1)

                def head_norm(key):
                    slot, m = NORMS.index(key) % 3, S if key[0] == "q" else LC
                    v = hn[slot][0:m, :]
                    step = [0]

                    def then(ins, carrier=False):
                        ins.then_inc(pool_step.sem, 1)
                        pool.wait_ge(pool_step.sem, pool_step.at(i, (key, step[0])))
                        step[0] += 1
                        if carrier:
                            pool.sem_inc(load_gate, 1)
                    wait_drained(pool, i, *(("xq", key[1]) if key[0] == "q" else ("kx",) + key))
                    s3 = sq[0:m, :].rearrange("p (a b) -> p a b", b=HD)
                    then(nc.gpsimd.tensor_tensor(sq[0:m, :], v, v, ALU.mult))
                    w = HD // 2
                    while w > 1:
                        then(nc.gpsimd.tensor_tensor(s3[:, :, 0:w], s3[:, :, 0:w], s3[:, :, w:2 * w], ALU.add))
                        w //= 2
                    ss, y, minus_half = [r[0:m, :] for r in root]
                    col = lambda a: a.rearrange("p (a b) -> p a b", b=1)
                    then(nc.gpsimd.tensor_tensor(col(ss), s3[:, :, 0:1], s3[:, :, 1:2], ALU.add), carrier=True)
                    then(nc.gpsimd.tensor_scalar(ss, ss, HD * 1e-6, None, ALU.add), carrier=True)
                    nc.gpsimd.tensor_scalar(y.bitcast(I32), ss.bitcast(I32), -0.5, float(0x5f3759df), ALU.mult, ALU.add)
                    then(nc.gpsimd.tensor_scalar(minus_half, ss, -0.5, None, ALU.mult))
                    for _ in range(3):
                        then(nc.gpsimd.tensor_tensor(ss, y, y, ALU.mult))
                        then(nc.gpsimd.tensor_tensor(ss, ss, minus_half, ALU.mult))
                        then(nc.gpsimd.tensor_tensor(ss, ss, half3[0:m, :], ALU.add))
                        then(nc.gpsimd.tensor_tensor(y, y, ss, ALU.mult))
                    nc.gpsimd.tensor_tensor(v.rearrange("p (a b) -> p a b", b=HD), v.rearrange("p (a b) -> p a b", b=HD),
                                            col(y).to_broadcast([m, H, HD]), ALU.mult).then_inc(hn_ready.sem, 1)
                    assert step[0] == NORM_STEPS, f"NORM_STEPS = {step[0]}"

                def normalise(j):
                    for g in range(G):
                        n = j * G + g
                        pool.wait_ge(rec_ready.sem, rec_ready.at(i, (j, g)))
                        nc.gpsimd.tensor_tensor(pr[n % NP_][0:S], pr[n % NP_][0:S],
                                                prec[j][0:S, g, :].rearrange("p (a b) -> p a b", b=1).to_broadcast([S, KV, S]),
                                                ALU.mult).then_inc(p_ready.sem, 1)

                def add_bias(j):
                    pool.wait_ge(xn_ready.sem, xn_ready.at(i, (2, j)))
                    nc.gpsimd.tensor_tensor(xr[j][0:S, :], xr[j][0:S, :], bo_bc[0:S, :], ALU.add).then_inc(xr_ready.sem, 1)

                for n in range(2):
                    head_norm(NORMS[n])
                normalise(0)
                head_norm(NORMS[2])
                normalise(1)
                for n in range(3, 6):
                    head_norm(NORMS[n])
                add_bias(0)
                head_norm(NORMS[6])
                head_norm(NORMS[7])
                add_bias(1)
                for n in range(H, 2 * H):
                    pool.wait_ge(xrec_ready.sem, xrec_ready.at(i, n))
                    nc.gpsimd.tensor_tensor(xp[n % NX][0:S, :], xp[n % NX][0:S, :], xrec[0:S, 1, n % H:n % H + 1].to_broadcast([S, LM]),
                                            ALU.mult).then_inc(xp_ready[1].sem, 1)
            pool.wait_ge(slots_ready, 1)
            pool.wait_ge(xn3_loaded, 16)
            pool.wait_ge(zeroed, 16 * ZERO_FILLS)
            for b in range(B):
                for k in range(TOPK):
                    n = b * TOPK + k
                    pool.indirect_dma_start(out=xs_d, out_offset=bass.IndirectOffsetOnAxis(ap=slot_u[0:S, n:n + 1], axis=0),
                                            in_=xn3[0:S, b, :], in_offset=None).then_inc(scattered, 16)
            for r in range(2):
                pool.wait_ge(y_stored[r], 16 * (E // 2) + 1)
            count = pool.value_load(ov_i[0:1, NOV:NOV + 1], min_val=0, max_val=NOV)
            pool.wait_ge(o_st, count * 16 + 1)
            pool.sem_inc(load_gate, 1)
            for n in range(B * TOPK):
                if n >= 4:
                    pool.wait_ge(added[n % 4], n // 4)
                pool.indirect_dma_start(out=xn3[0:S, n % 4, :], out_offset=None, in_=ys_d,
                                        in_offset=bass.IndirectOffsetOnAxis(ap=slot_u[0:S, n:n + 1], axis=0)).then_inc(gathered[n % 4], 16)

        @block.tensor
        def _(pe):
            pe.wait_ge(consts_ready, 5)
            pe.wait_ge(dca_load, 16 * 3)
            pe.wait_ge(weights_centred, 3)
            for half in range(2):
                for c in range(CC):
                    last = nc.tensor.matmul(bank(half), c_dca[:, c, :], w_dca[:, c, half * D:(half + 1) * D],
                                            start=(c == 0), stop=(c == CC - 1))
            last.then_inc(dca_mm, 1)
            pe.wait_ge(dca_n, 3)
            for c in range(DC):
                last = nc.tensor.transpose(ps[:, 4, c * P:(c + 1) * P], t0[:, c * P:(c + 1) * P], ident[:])
            last.then_inc(dca_t, 1)
            pe.wait_ge(kd_ready, 1)
            pe.wait_ge(kv_centred, 1)
            pe.wait_ge(w_loaded["w_attn"], 16)

            with pe.Fori(0, PAIRS) as i:
                order = iter(fills)

                def begin(*key):
                    k, n = next(order)
                    assert k == key, (k, key)
                    n = bank_of[key]
                    pe.wait_ge(free[n].sem, free[n].prior(i, key))
                    return n

                def end(ins, *key):
                    ins.then_inc(full[bank_of[key]].sem, 1)

                def transpose_x(name, n, j):
                    if n == 1:
                        pe.wait_ge(x1_ready, i * 2 + (j + 1))
                    elif (n, j) == (3, 1):
                        pe.wait_ge(xn_ready.sem, xn_ready.before(i))
                    else:
                        pe.wait_ge(xn_ready.sem, xn_ready.at(i, (n, j)))
                    src = x1[j] if n == 1 else xn[j]
                    k = begin(name, j)
                    for c in range(DC):
                        last = nc.tensor.transpose(ps[:, k, c * S:(c + 1) * S], src[0:S, c * P:(c + 1) * P], ident[0:S, 0:S])
                    end(last, name, j)

                def project(key, m, lhs, w, cols, n_c):
                    k = begin(*key)
                    for c in range(n_c):
                        last = nc.tensor.matmul(ps[0:m, k, 0:cols[1] - cols[0]], lhs(c), w[:, c, cols[0]:cols[1]],
                                                start=(c == 0), stop=(c == n_c - 1))
                    end(last, *key)

                def kv_project(n, between=None):
                    j, c = KV_UNITS[n]
                    if c == 0:
                        pe.wait_ge(c_loaded[j], i * 16 + 16)
                    rows = lambda a: c_in[j][:, a, c * LC:(c + 1) * LC]
                    project(("kx", j, c), LC, rows, w_kv, (0, D), CC)
                    if between:
                        between()
                    project(("vx", j, c), LC, rows, w_kv, (D, 2 * D), CC)

                def transpose_normed(key, fill, m):
                    pe.wait_ge(hn_ready.sem, hn_ready.at(i, key))
                    k = begin(*fill)
                    for a in range(DC):
                        last = nc.tensor.transpose(ps[:, k, a * m:(a + 1) * m], hn[NORMS.index(key) % 3][0:m, a * P:(a + 1) * P],
                                                   ident[0:m, 0:m])
                    end(last, *fill)

                def kv_transpose(n):
                    transpose_normed(KV_UNITS[n], ("kxT",) + KV_UNITS[n], LC)

                def self_project(j):
                    wait_drained(pe, i, "xT1", j)
                    rows = lambda a: xT[j][:, a, :]
                    project(("q", j), S, rows, w_attn, (0, D), DC)
                    project(("k", j), S, rows, w_attn, (D, QK), DC)
                    project(("v", j), S, rows, w_attn, (QK, QK + D), DC)

                def transpose_qk(j):
                    wait_drained(pe, i, "k", j)
                    k = begin("qT", j)
                    for c in range(KV):
                        last = nc.tensor.transpose(ps[:, k, c * S:(c + 1) * S], qr[j][0:S, c * P:(c + 1) * P], ident[0:S, 0:S])
                    end(last, "qT", j)
                    k = begin("kT", j)
                    for c in range(KV):
                        last = nc.tensor.transpose(ps[:, k, c * S:(c + 1) * S], kr[j][0:S, c, :, :].rearrange("p a b -> p (a b)"), ident[0:S, 0:S])
                    end(last, "kT", j)

                def scores(j):
                    wait_drained(pe, i, "qT", j)
                    wait_drained(pe, i, "kT", j)
                    ks = [begin("s", j, g) for g in range(G)]
                    for c in range(KV):
                        for g in range(G):
                            rows_ = slice(g * HD, (g + 1) * HD)
                            last = nc.tensor.matmul(ps[0:S, ks[g], c * S:(c + 1) * S], qT[j][rows_, c, :], kT[j][rows_, c, :],
                                                    start=True, stop=True)
                            if c == KV - 1:
                                end(last, "s", j, g)

                def transpose_probs(j):
                    for g in range(G):
                        n = j * G + g
                        pe.wait_ge(p_ready.sem, p_ready.at(i, (j, g)))
                        k = begin("pT", j, g)
                        for c in range(KV):
                            last = nc.tensor.transpose(ps[0:S, k, c * S:(c + 1) * S], pr[n % NP_][0:S, c, :], ident[0:S, 0:S])
                        end(last, "pT", j, g)

                def values(j, c):
                    if c == 0:
                        for g in range(G):
                            wait_drained(pe, i, "pT", j, g)
                        wait_drained(pe, i, "v", j)
                    k = begin("pv", j, c)
                    last = nc.tensor.matmul(ps[:, k, 0:G * S], v_s[j][0:S, c * VD:(c + 1) * VD],
                                            pT[0:S, c, :, :].rearrange("p a b -> p (a b)"), start=True, stop=True)
                    end(last, "pv", j, c)

                def attend_out(j, c):
                    wait_drained(pe, i, "pv", j, c)
                    if c == 0:
                        pe.wait_ge(w_loaded["w_out"], 16)
                        pe.wait_ge(free[j].sem, free[j].prior(i, ("o", j)))
                    for g in range(G):
                        last = nc.tensor.matmul(ps[0:S, j, :], cT[c % 2][:, g, :], w_out[:, c * G + g, :],
                                                start=(c == 0 and g == 0), stop=(c == KV - 1 and g == G - 1))
                    if c < KV - 1:
                        last.then_inc(cT_used.sem, 1)
                    return last

                def x_project(name, j, lhs, w, cols):
                    project((name, j), S, lhs, w, cols, DC)

                def dca_scores(j):
                    wait_drained(pe, i, "xqT", j)
                    pe.wait_ge(db_ready.sem, db_ready.at(i, j))
                    k = begin("ds", j)
                    for c in range(DC):
                        last = nc.tensor.matmul(ps[0:S, k, c * 64:(c + 1) * 64], xqT[j][:, c, :],
                                                kdb[j][:, c, :, :].rearrange("p a b -> p (a b)"), start=True, stop=True)
                    end(last, "ds", j)

                def dca_transpose(j):
                    pe.wait_ge(dp_ready.sem, dp_ready.at(i, j))
                    k = begin("dpT", j)
                    for c in range(2):
                        last = nc.tensor.transpose(ps[:, k, c * S:(c + 1) * S],
                                                   dp[j][0:S, c * 8:(c + 1) * 8, :].rearrange("p a b -> p (a b)"), ident[0:S, 0:S])
                    end(last, "dpT", j)

                def dca_values(j, a):
                    if a == 0:
                        wait_drained(pe, i, "dpT", j)
                        pe.wait_ge(free[6 + j].sem, free[6 + j].prior(i, ("ctx", j)))
                    four = vdb[j][:, a // 2, (a % 2) * 4:(a % 2) * 4 + 4, :].rearrange("p a b -> p (a b)")
                    nc.tensor.matmul(ps[:, 6 + j, a * S:(a + 1) * S], four, dpT[j][:, a // 2, :], start=True, stop=False)

                def query_project(j):
                    wait_drained(pe, i, "xT2", j)
                    pe.wait_ge(q_centred, 4 * DC)
                    x_project("xq", j, lambda a: xT[j][:, a, :], w_q, (0, D))

                def context_out(j):
                    wait_drained(pe, i, "ctx", j)
                    pe.wait_ge(w_loaded["w_o"], 16)
                    x_project("xo", j, lambda a: cxT[j][:, a, :], w_o, (0, D))

                def gate(j):
                    wait_drained(pe, i, "xT3", j)
                    pe.wait_ge(w_loaded["w_gate"], 16)
                    src = cxT[1] if j else xT[0]
                    x_project("gate", j, lambda a: src[:, a, :], w_gate, (0, NG))

                transpose_x("xT1", 1, 0)
                transpose_x("xT1", 1, 1)
                self_project(0)
                transpose_x("xT3", 3, 1)
                kv_project(0, between=lambda: gate(1))
                self_project(1)
                kv_project(1)
                transpose_qk(0)
                kv_project(2)
                kv_transpose(0)
                transpose_qk(1)
                scores(0)
                kv_project(3)
                kv_transpose(1)
                scores(1)
                kv_project(4)
                transpose_probs(0)
                values(0, 0)
                values(0, 1)
                kv_transpose(2)
                attend_out(0, 0)
                values(0, 2)
                attend_out(0, 1)
                values(0, 3)
                transpose_probs(1)
                attend_out(0, 2)
                values(1, 0)
                begin("o", 0)
                end(attend_out(0, 3), "o", 0)
                values(1, 1)
                attend_out(1, 0)
                values(1, 2)
                transpose_x("xT2", 2, 0)
                attend_out(1, 1)
                query_project(0)
                kv_transpose(3)
                values(1, 3)
                attend_out(1, 2)
                begin("o", 1)
                end(attend_out(1, 3), "o", 1)
                kv_project(5)
                kv_transpose(4)
                transpose_normed(("q", 0), ("xqT", 0), S)
                dca_scores(0)

                hooks = {"xT2": lambda j: transpose_x("xT2", 2, j), "xq": query_project, "dpT": dca_transpose,
                         "kxT": lambda j, c: kv_transpose(KV_UNITS.index((j, c))), "xqT": lambda j: transpose_normed(("q", j), ("xqT", j), S),
                         "ds": dca_scores, "xo": context_out, "xT3": lambda j: transpose_x("xT3", 3, j), "gate": gate}
                for n in range(2 * H + PV_LAG):
                    for key in HEAD_HOOKS.get(n, []):
                        hooks[key[0]](*key[1:])
                    if n < 2 * H:
                        j, h = n // H, n % H
                        if h == 0:
                            wait_drained(pe, i, "xqT", j)
                            last_in = {bank_of["kxT", j, c]: c for c in range(LN_)}
                            for c in last_in.values():
                                wait_drained(pe, i, "kxT", j, c)
                            wait_drained(pe, i, "vx", j, LN_ - 1)
                        k = begin("xs", n)
                        rows_ = slice((h % 4) * HD, (h % 4 + 1) * HD)
                        end(nc.tensor.matmul(ps[0:S, k, 0:LM], xqT[j][rows_, h // 4, :], kxT[j][rows_, h // 4, :],
                                             start=True, stop=True), "xs", n)
                    if XS_LAG <= n < 2 * H + XS_LAG:
                        m = n - XS_LAG
                        pe.wait_ge(xp_ready[m // H].sem, xp_ready[m // H].at(i, m % H))
                        k = begin("xpT", m)
                        for c in range(LN_):
                            last = nc.tensor.transpose(ps[0:LC, k, c * S:(c + 1) * S], xp[m % NX][0:S, c * LC:(c + 1) * LC], ident[0:S, 0:S])
                        end(last, "xpT", m)
                    if n >= PV_LAG:
                        m = n - PV_LAG
                        j, h = m // H, m % H
                        wait_drained(pe, i, "xpT", m)
                        if h % 4 == 0:
                            dca_values(j, h // 4)
                        for c in range(LN_):
                            last = nc.tensor.matmul(ps[(h % 4) * HD:(h % 4 + 1) * HD, 6 + j, (h // 4) * S:(h // 4 + 1) * S],
                                                    vx[j][0:LC, c, h * HD:(h + 1) * HD], xpT[m % NX][0:LC, c, :],
                                                    start=False, stop=(c == LN_ - 1))
                        last.then_inc(xpv_done.sem, 1)
                        if h == H - 1:
                            assert next(order)[0] == ("ctx", j)
                context_out(1)

            def shared_up(m, half):
                for gu in range(2):
                    for c in range(DC):
                        tok = xT3[:, half * 4:(half + 1) * 4, c * S:(c + 1) * S]
                        last = nc.tensor.matmul(ps[:, (m % 2) * 4 + half * 2 + gu, 0:400].rearrange("p (a b) -> p a b", a=4),
                                                se_w[m % 3][:, c, gu * P:(gu + 1) * P], tok,
                                                start=(c == 0), stop=(c == DC - 1))
                    last.then_inc(up_full[m % 2], 1)

            pe.wait_ge(free[0].sem, free[0].before(PAIRS))
            pe.wait_ge(free[1].sem, free[1].before(PAIRS))
            pe.wait_ge(xT3_early, 16)
            pe.wait_ge(se_loaded[0], 16)
            shared_up(0, 0)
            pe.wait_ge(xn_ready.sem, xn_ready.before(PAIRS))
            pe.wait_ge(free[4].sem, free[4].before(PAIRS))
            for c in range(DC):
                last = nc.tensor.transpose(ps[:, 4, c * S:(c + 1) * S], xn[1][0:S, c * P:(c + 1) * P], ident[0:S, 0:S])
            last.then_inc(late_full, 1)
            pe.wait_ge(late_free, 1)
            pe.wait_ge(free[5].sem, free[5].before(PAIRS))
            for c in range(DC):
                last = nc.tensor.matmul(ps[0:S, 5, 0:NG], cxT[1][:, c, :], w_gate[:, c, :], start=(c == 0), stop=(c == DC - 1))
            last.then_inc(late_full, 1)
            pe.wait_ge(late_free, 2)

            for n in range(8):
                pe.wait_ge(free[n].sem, free[n].before(PAIRS))
            pe.wait_ge(xT3_loaded, 16 * 2)
            shared_up(0, 1)
            for m in range(1, MC):
                pe.wait_ge(se_loaded[m % 3], 16 * (m // 3 + 1))
                for half in range(2):
                    if m >= 2:
                        pe.wait_ge(hs_ready[m % 2], 2 * ((m - 2) // 2) + half + 1)
                    shared_up(m, half)
            pe.wait_ge(mask_ready, 1)
            pe.wait_ge(hs_ready[0], 2 * ((MC + 1) // 2))
            pe.wait_ge(hs_ready[1], 2 * (MC // 2))
            for b in range(B):
                nc.tensor.matmul(ps[0:S, 0, b * E:(b + 1) * E], tri[0:S, 0:S], mask[0:S, b, :], start=True, stop=(b == 0))
                if b:
                    nc.tensor.matmul(ps[0:S, 0, b * E:(b + 1) * E], ones[0:S, 0:S], mask_sum[0:S, b - 1, :], start=False, stop=True)
            nc.tensor.matmul(ps[:, 1, 0:E], ones[0:S, :], mask_sum[0:S, B - 1, :], start=True, stop=True).then_inc(rank_full, 1)
            pe.wait_ge(down_loaded, 16)
            for b in range(B):
                if b >= 2:
                    pe.wait_ge(dn_free, b - 1)
                for m in range(MC):
                    last = nc.tensor.matmul(ps[0:S, 2 + b % 2, :], hT_all[:, m, b * S:(b + 1) * S], w_down[:, m, :],
                                            start=(m == 0), stop=(m == MC - 1))
                last.then_inc(dn_full, 1)
            pe.wait_ge(slots_ready, 1)
            pe.wait_ge(dn_free, B)

            def rows_T(r, turn):
                pe.wait_ge(xs_loaded[r], turn * 16 + 16)
                pe.wait_ge(xst_ready[r], turn + 1)
                for c in range(DC):
                    last = nc.tensor.transpose(ps[:, r, c * T:(c + 1) * T], xs_s[r][0:T, c * P:(c + 1) * P], ident[0:T, 0:T])
                last.then_inc(xst_full[r], 1)

            def gate_up(r, turn):
                pe.wait_ge(w13_loaded[r], turn * 16 + 16)
                pe.wait_ge(xst_ready[r], turn + 2)
                pe.wait_ge(h_ready[r], turn + 1)
                gate_up_products(r)[-1].then_inc(up1_full[r], 1)

            def gate_up_products(r):
                done = []
                for gu in range(2):
                    for n, w in enumerate(IC):
                        at = gu * I + n * P
                        for c in range(DC):
                            done.append(nc.tensor.matmul(ps[0:w, 2 + 2 * gu + r, n * T:(n + 1) * T], w13_s[r][:, c, at:at + w],
                                                         xsT[r][:, c, :], start=(c == 0), stop=(c == DC - 1)))
                return done

            def down_products(r):
                for n, w in enumerate(IC):
                    last = nc.tensor.matmul(ps[0:T, 6 + r, :], hT[r][0:w, n, :], w2_s[r][0:w, n, :],
                                            start=(n == 0), stop=(n == len(IC) - 1))
                return last

            def down(r, turn):
                pe.wait_ge(w2_loaded[r], turn * 32 + 32)
                pe.wait_ge(h_ready[r], turn + 2)
                pe.wait_ge(y_ready[r], turn + 1)
                down_products(r).then_inc(y_full[r], 1)

            rows_T(0, 0)
            rows_T(1, 0)
            gate_up(0, 0)
            with pe.Fori(0, E // 2 - 1) as i:
                rows_T(0, i + 1)
                gate_up(1, i)
                down(0, i)
                rows_T(1, i + 1)
                gate_up(0, i + 1)
                down(1, i)
            gate_up(1, E // 2 - 1)
            down(0, E // 2 - 1)
            down(1, E // 2 - 1)
            pe.wait_ge(y_ready[0], E // 2 + 1)
            count = pe.value_load(ov_i[0:1, NOV:NOV + 1], min_val=0, max_val=NOV)
            with pe.If(count > 0):
                with pe.Fori(0, NOV) as t:
                    with pe.If(count > t):
                        pe.wait_ge(o_w, t * 64 + 64)
                        pe.wait_ge(o_yc, t + 1)
                        for c in range(DC):
                            last = nc.tensor.transpose(ps[:, 0, c * T:(c + 1) * T], xs_s[0][0:T, c * P:(c + 1) * P], ident[0:T, 0:T])
                        last.then_inc(o_t, 1)
                        pe.wait_ge(o_tc, t + 1)
                        gate_up_products(0)[-1].then_inc(o_g, 1)
                        pe.wait_ge(o_h, t + 1)
                        down_products(0).then_inc(o_y, 1)

        @block.scalar
        def _(act):
            act.wait_ge(dca_t, 1)
            act.wait_ge(weights_centred, 3)
            for c in range(DC):
                last = nc.scalar.activation(kd_all[:, c, :], ps[:, 4, c * P:(c + 1) * P], ACT.Identity, bias=nrm[:, 5:6], scale=nrm[:, 4:5])
            last.then_inc(kd_ready, 1)

            with act.Fori(0, PAIRS) as i:
                def filled(*key):
                    return wait_filled(act, i, *key)

                def x_T(name, j):
                    k = filled(name, j)
                    nc.scalar.activation(xT[j].rearrange("p a b -> p (a b)"), ps[:, k, 0:DC * S], ACT.Copy).then_inc(free[k].sem, 1)

                def kv(n):
                    j, c = KV_UNITS[n]
                    k = filled("kxT", j, c)
                    nc.scalar.activation(kxT[j][:, :, c * LC:(c + 1) * LC], ps[:, k, 0:DC * LC].rearrange("p (a b) -> p a b", a=DC),
                                         ACT.Identity, bias=nrm[:, 3:4], scale=nrm[:, 2:3]).then_inc(free[k].sem, 1)

                def q_T(j):
                    k = filled("xqT", j)
                    nc.scalar.activation(xqT[j].rearrange("p a b -> p (a b)"), ps[:, k, 0:DC * S], ACT.Identity, bias=nrm[:, 1:2],
                                         scale=nrm[:, 0:1]).then_inc(free[k].sem, 1)

                def context_T(j):
                    act.wait_ge(xpv_done.sem, xpv_done.at(i, j * H + H - 1))
                    nc.scalar.activation(cxT[j].rearrange("p a b -> p (a b)"), ps[:, 6 + j, 0:DC * S], ACT.Copy).then_inc(free[6 + j].sem, 1)

                def copy(name, j, dst, cols):
                    k = filled(name, j)
                    nc.scalar.activation(dst, ps[0:dst.shape[0], k, 0:cols], ACT.Copy).then_inc(free[k].sem, 1)

                def exps(j):
                    for g in range(G):
                        n = j * G + g
                        k = filled("s", j, g)
                        act.wait_ge(max_ready.sem, max_ready.at(i, (j, g)))
                        for c in range(KV):
                            last = nc.scalar.activation(pr[n % NP_][0:S, c, :], ps[0:S, k, c * S:(c + 1) * S], ACT.Exp,
                                                        bias=nmax[j][0:S, g, c:c + 1], scale=1.0, accum_out=psum_[j][0:S, g, c:c + 1])
                        last.then_inc(free[k].sem, 1)

                def context(j, c):
                    k = filled("pv", j, c)
                    before = 4 * j + c - 2
                    if before >= 0:
                        jj, cc = before // KV, before % KV
                        if cc == KV - 1:
                            act.wait_ge(full[jj].sem, full[jj].at(i, ("o", jj)))
                        else:
                            act.wait_ge(cT_used.sem, cT_used.at(i, (jj, cc)))
                    if (j, c) == (0, 1):
                        act.wait_ge(xT_stored[1], i * 16 + 1)
                    nc.scalar.activation(cT[c % 2].rearrange("p a b -> p (a b)"), ps[:, k, 0:G * S], ACT.Copy).then_inc(free[k].sem, 1)

                def dca_exp(j):
                    wait_drained(act, i, "ds", j)
                    nc.scalar.activation(dp[j][0:S].rearrange("p a b -> p (a b)"), dp[j][0:S].rearrange("p a b -> p (a b)"), ACT.Exp).then_inc(dexp_ready.sem, 1)

                def gate_out(j):
                    k = filled("gate", j)
                    nc.scalar.activation(lg_late[0:S, bass.ds(i * 2 + 2 - j, 1), :], ps[0:S, k:k + 1, 0:NG], ACT.Copy).then_inc(free[k].sem, 1)

                def scale_probs(n):
                    act.wait_ge(xrec_ready.sem, xrec_ready.at(i, n))
                    nc.scalar.activation(xp[n % NX][0:S, :], xp[n % NX][0:S, :], ACT.Copy,
                                         scale=xrec[0:S, n // H, n % H:n % H + 1]).then_inc(xp_ready[0].sem, 1)

                def head_probs_T(m):
                    k = filled("xpT", m)
                    act.wait_ge(xpv_done.sem, xpv_done.at(i, m - NX))
                    nc.scalar.activation(xpT[m % NX][0:LC].rearrange("p a b -> p (a b)"), ps[0:LC, k, 0:LN_ * S], ACT.Copy).then_inc(free[k].sem, 1)

                act.wait_ge(xT_stored[0], i * 16 + 1)
                x_T("xT1", 0)
                x_T("xT1", 1)
                copy("v", 0, v_s[0][0:S, :], D)
                copy("xT3", 1, cxT[1].rearrange("p a b -> p (a b)"), DC * S)
                gate_out(1)
                copy("v", 1, v_s[1][0:S, :], D)
                copy("qT", 0, qT[0].rearrange("p a b -> p (a b)"), DC * S)
                kv(0)
                copy("qT", 1, qT[1].rearrange("p a b -> p (a b)"), DC * S)
                exps(0)
                kv(1)
                exps(1)
                context(0, 0)
                context(0, 1)
                kv(2)
                context(0, 2)
                context(0, 3)
                for c in range(KV - 1):
                    context(1, c)
                x_T("xT2", 0)
                kv(3)
                context(1, 3)
                kv(4)
                q_T(0)
                dca_exp(0)
                for n in range(2 * H + XS_LAG):
                    for key in HEAD_HOOKS.get(n, []):
                        if key[0] == "dpT":
                            copy("dpT", key[1], dpT[key[1]].rearrange("p a b -> p (a b)"), 2 * S)
                        elif key[0] == "kxT":
                            kv(KV_UNITS.index(key[1:]))
                        elif key[0] == "xqT":
                            q_T(key[1])
                        elif key[0] in ("xT2", "xT3"):
                            x_T(*key)
                        elif key[0] == "gate":
                            gate_out(key[1])
                    if n == DCA_EXP_1:
                        dca_exp(1)
                    if n < 2 * H:
                        j, h = n // H, n % H
                        k = filled("xs", n)
                        act.wait_ge(xmax_ready.sem, xmax_ready.at(i, n))
                        if n >= NX:
                            kk = bank_of[("xpT", n - NX)]
                            act.wait_ge(full[kk].sem, full[kk].at(i, ("xpT", n - NX)))
                        nc.scalar.activation(xp[n % NX][0:S, :], ps[0:S, k, 0:LM], ACT.Exp, bias=xnm[0:S, j, h:h + 1], scale=1.0,
                                             accum_out=xsum[0:S, j, h:h + 1]).then_inc(free[k].sem, 1)
                    if 1 <= n < H + 1:
                        scale_probs(n - 1)
                    if scalar_copies(n - XS_LAG):
                        head_probs_T(n - XS_LAG)
                    if n == H + PV_LAG - 1:
                        context_T(0)
                context_T(1)

            act.wait_ge(late_full, 1)
            nc.scalar.activation(cxT[1].rearrange("p a b -> p (a b)"), ps[:, 4, 0:DC * S], ACT.Copy).then_inc(late_free, 1)
            act.wait_ge(late_full, 2)
            nc.scalar.activation(lg_all[0:S, B - 1, :], ps[0:S, 5, 0:NG], ACT.Copy).then_inc(late_free, 1)

            for j in range(2):
                act.wait_ge(xn_stored[j], 16 * PAIRS + 1)
                act.wait_ge(x2_stored[j], 16 * PAIRS + 1)
                act.wait_ge(xT_stored[j], 16 * PAIRS + 1)
            act.wait_ge(r_in, 1)
            for b in range(B):
                nc.scalar.activation(rsm[0:S, 1, b, 0:TOPK], rsm[0:S, 0, b, 0:TOPK], ACT.Exp, bias=rsm[0:S, 2, b, 0:1])
                nc.scalar.activation(oh[0:S, b, :], lg_all[0:S, b, 0:E], ACT.Exp, bias=rsm[0:S, 2, b, 0:1],
                                            accum_out=rsm[0:S, 3, b, 0:1])
            nc.scalar.activation(rsm[0:S, 6, :, 2:3], lg_all[0:S, :, E:NG], ACT.Sigmoid).then_inc(r_act, 1)
            for m in range(MC):
                for half in range(2):
                    act.wait_ge(up_full[m % 2], 4 * (m // 2) + 2 * half + 1)
                    if m:
                        act.wait_ge(hs_ready[(m - 1) % 2], 2 * ((m - 1) // 2) + half + 1)
                    nc.scalar.activation(s_sh[half], ps[:, (m % 2) * 4 + half * 2, 0:400], ACT.Silu).then_inc(silu_ready[m % 2], 1)

            def silu(r, turn):
                act.wait_ge(up1_full[r], turn + 2)
                act.wait_ge(h_ready[r], turn + 1)
                silu_parts(r).then_inc(sl_ready[r], 1)

            def silu_parts(r):
                nc.scalar.activation(sl[r][:, 0:2, :].rearrange("p a b -> p (a b)"), ps[:, 2 + r, 0:2 * T], ACT.Silu)
                return nc.scalar.activation(sl[r][0:96, 2, :], ps[0:96, 2 + r, 2 * T:3 * T], ACT.Silu)

            def store(r, turn, e):
                act.wait_ge(y_full[r], turn + 2)
                act.wait_ge(y_stored[r], turn * 16 + 1)
                nc.scalar.activation(y_s[r][0:T], ps[0:T, 6 + r, :], ACT.Copy).then_inc(y_ready[r], 1)
                act.wait_ge(y_ready[r], turn + 2)
                act.dma_start(ys_d[bass.ds(e * T, T), :], y_s[r][0:T]).then_inc(y_stored[r], 16)

            silu(0, 0)
            with act.Fori(0, E // 2 - 1) as i:
                silu(1, i)
                store(0, i, i * 2)
                silu(0, i + 1)
                store(1, i, i * 2 + 1)
            silu(1, E // 2 - 1)
            store(0, E // 2 - 1, E - 2)
            store(1, E // 2 - 1, E - 1)
            for r in range(2):
                act.wait_ge(y_stored[r], 16 * (E // 2) + 1)
            act.wait_ge(slots_ready, 1)
            count = act.value_load(ov_i[0:1, NOV:NOV + 1], min_val=0, max_val=NOV)
            with act.If(count > 0):
                with act.Fori(0, NOV) as t:
                    with act.If(count > t):
                        act.wait_ge(o_g, t + 1)
                        silu_parts(0).then_inc(o_s, 1)
                        act.wait_ge(o_y, t + 2)
                        act.wait_ge(o_st, t * 16 + 1)
                        nc.scalar.activation(y_s[0][0:T], ps[0:T, 6, :], ACT.Copy).then_inc(o_yc, 1)
                        act.wait_ge(o_yc, t + 2)
                        act.dma_start(ys_d[bass.ds(t * T + E * T, T), :], y_s[0][0:T]).then_inc(o_st, 16)

        @block.vector
        def _(dve):
            count_ = [0, None, 0]

            def link(ins):
                ins.then_inc(chain, 1)
                count_[0] += 1
                if count_[1] is None:
                    dve.wait_ge(chain, count_[2] + count_[0])
                else:
                    dve.wait_ge(chain, count_[1] * LINKS + (count_[2] + count_[0]))

            def centre(view, n):
                m = stat[:, 0:n]
                link(nc.vector.tensor_reduce(m, view, AX, ALU.add))
                link(nc.vector.tensor_scalar(m, m, 1.0 / HD, None, ALU.mult))
                return nc.vector.tensor_tensor(view, view, m.rearrange("p (a b) -> p a b", b=1).to_broadcast([P, n, HD]), ALU.subtract)

            def head(v):
                return v.rearrange("p (a b) -> p a b", b=HD)

            def inverse_root(v, work):
                y, minus_half, a = work
                nc.vector.tensor_scalar(y.bitcast(I32), v.bitcast(I32), -0.5, float(0x5f3759df), ALU.mult, ALU.add)
                link(nc.vector.tensor_scalar(minus_half, v, -0.5, None, ALU.mult))
                yield
                for n in range(3):
                    link(nc.vector.tensor_tensor(a, y, minus_half, ALU.mult))
                    yield
                    link(nc.vector.tensor_tensor(a, a, y, ALU.mult))
                    yield
                    link(nc.vector.scalar_tensor_tensor(out=y if n < 2 else v, in0=a, scalar=1.5, in1=y, op0=ALU.add, op1=ALU.mult))
                    yield

            def layer_norm(src, dst, signal):
                link(nc.vector.bn_stats(stat_n[0:S, 0:6], src))
                yield
                nc.vector.memset(stat_n[0:S, 15:16], 0.0)
                link(nc.vector.bn_aggr(stat_n[0:S, 8:10], stat_n[0:S, 0:6]))
                link(nc.vector.tensor_scalar(stat_n[0:S, 10:11], stat_n[0:S, 9:10], 1e-5, None, ALU.add))
                yield
                yield from inverse_root(stat_n[0:S, 10:11], [stat_n[0:S, n:n + 1] for n in (12, 13, 14)])
                nc.vector.tensor_scalar(dst, src, stat_n[0:S, 8:9], stat_n[0:S, 10:11], ALU.subtract, ALU.mult).then_inc(signal, 1)

            def run(pieces):
                for _ in pieces:
                    pass

            for j in range(2):
                dve.wait_ge(x_loaded[j], 16)
                if j:
                    dve.wait_ge(x1_ready, j)
                run(layer_norm(x_in[j][0:S, :], x1[j][0:S, :], x1_ready))

            dve.wait_ge(dca_load, 16 * 3)
            for c in range(CC):
                last = centre(head(w_dca[:, c, 0:D]), H)
                link(last)
            link(centre(head(bdca_bc[:, 0:D]), H))
            dve.wait_ge(pre_load, 16 * 9)
            link(nc.vector.tensor_scalar(nrm[:, 0:2], nrm[:, 0:2], SCALE, None, ALU.mult))
            for c in (0, 2):
                link(nc.vector.tensor_scalar(nrm[:, c:c + 1], nrm[:, c:c + 1], float(HD) ** 0.5, None, ALU.mult))
            dve.sem_inc(weights_centred, 3)
            link(centre(head(bkv_bc[:, 0:D]), H))
            link(centre(head(bq_bc), H))
            dve.wait_ge(w_loaded["w_kv"], 16)
            for c in range(CC):
                last = centre(head(w_kv[:, c, 0:D]), H)
                link(last)
            dve.sem_inc(kv_centred, 1)
            dve.wait_ge(dca_mm, 1)
            dve.wait_ge(weights_centred, 3)
            link(nc.vector.tensor_tensor(kn, ps[:, 0, :], bdca_bc[:, 0:D], ALU.add))
            nc.vector.tensor_tensor(vd_s, ps[:, 1, :], bdca_bc[:, D:2 * D], ALU.add).then_inc(dca_n, 2)

            def head_norm(src, dst, m):
                link(nc.vector.tensor_tensor(t1[0:m, :], src, src, ALU.mult))
                ss = stat[0:m, 0:H]
                link(nc.vector.tensor_reduce(ss, head(t1[0:m, :]), AX, ALU.add))
                link(nc.vector.tensor_scalar(ss, ss, HD * 1e-6, None, ALU.add))
                for _ in inverse_root(ss, [stat[0:m, n * H:(n + 1) * H] for n in (1, 2, 3)]):
                    pass
                return nc.vector.scalar_tensor_tensor(out=head(dst), in0=head(src), scalar=float(HD) ** 0.5,
                                                      in1=ss.rearrange("p (a b) -> p a b", b=1).to_broadcast([m, H, HD]),
                                                      op0=ALU.mult, op1=ALU.mult)

            head_norm(kn[:, :], t0[:, :], P).then_inc(dca_n, 1)
            dve.wait_ge(dca_n, 3)
            dve.wait_ge(kd_ready, 1)

            count_[2] = count_[0]
            count_[0] = 0
            with dve.Fori(0, PAIRS) as i:
                count_[1] = i

                def filled(*key):
                    return wait_filled(dve, i, *key)

                def norm_x(j):
                    return layer_norm(xr[j][0:S, :], xn[j][0:S, :], xn_ready.sem)

                def norm_next(j):
                    dve.wait_ge(x_loaded[j], i * 16 + 32)
                    dve.wait_ge(full[0].sem, full[0].at(i, ("qT", 1)))
                    if j == 0:
                        dve.wait_ge(xn_ready.sem, xn_ready.at(i, (2, 1)))
                    else:
                        dve.wait_ge(x1_ready, i * 2 + 3)
                    yield from layer_norm(x_in[j][0:S, :], x1[j][0:S, :], x1_ready)

                def wait_normed(k):
                    dve.wait_ge(xn_ready.sem, xn_ready.prior(i, k))

                def rope(src, n, table, dst, before):
                    s3 = src.rearrange("p (a b) -> p a b", b=HD)
                    a3 = t0[0:S, 0:n * HD].rearrange("p (a b) -> p a b", b=HD)
                    b3 = t1[0:S, 0:n * HD].rearrange("p (a b) -> p a b", b=HD)
                    half = HD // 2
                    tab = lambda r, lo, hi: cs[0:S, r:r + 1, lo:hi].to_broadcast([S, n, hi - lo])
                    sig, value = before
                    dve.wait_ge(sig.sem, value)
                    nc.vector.tensor_tensor(a3, s3, tab(table, 0, HD), ALU.mult)
                    nc.vector.tensor_tensor(b3[:, :, 0:half], s3[:, :, half:HD], tab(table + 1, 0, half), ALU.mult)
                    link(nc.vector.tensor_tensor(b3[:, :, half:HD], s3[:, :, 0:half], tab(table + 1, half, HD), ALU.mult))
                    return dst(a3, b3)

                def rotate(j):
                    k, k2 = filled("q", j), bank_of["k", j]
                    last_k = bank_of["k", 1 - j]
                    before = free[last_k].at(i, ("k", 0)) if j else free[last_k].before(i)
                    rope(ps[0:S, k, :], H, 0, lambda a, b: nc.vector.tensor_tensor(qr[j][0:S, :].rearrange("p (a b) -> p a b", b=HD), a, b, ALU.add),
                         (free[last_k], before)).then_inc(free[k].sem, 1)
                    filled("k", j)

                    def spread(a, b):
                        full_ = lambda v: v.rearrange("p (k g) e -> p k g e", g=1).to_broadcast([S, KV, G, HD])
                        return nc.vector.tensor_tensor(kr[j][0:S], full_(a), full_(b), ALU.add)
                    rope(ps[0:S, k2, 0:KV * HD], KV, 2, spread, (free[k], free[k].at(i, ("q", j)))).then_inc(free[k2].sem, 1)

                def kv(n):
                    key = KV_UNITS[n]
                    j, c = key
                    slot = claim_slot(key)
                    k = filled("kx", j, c)
                    nc.vector.tensor_tensor(hn[slot][0:LC, :], ps[0:LC, k, :], bkv_bc[0:LC, 0:D], ALU.add).then_inc(free[k].sem, 1)
                    k = filled("vx", j, c)
                    nc.vector.tensor_tensor(vx[j][0:LC, c, :], ps[0:LC, k, :], bkv_bc[0:LC, D:2 * D], ALU.add).then_inc(free[k].sem, 1)

                def query(j):
                    slot = claim_slot(("q", j))
                    k = filled("xq", j)
                    nc.vector.tensor_tensor(hn[slot][0:S, :], ps[0:S, k, :], bq_bc[0:S, :], ALU.add).then_inc(free[k].sem, 1)

                def claim_slot(key):
                    n = NORMS.index(key)
                    if n >= 3:
                        past = NORMS[n - 3]
                        past = ("xqT", past[1]) if past[0] == "q" else ("kxT",) + past
                        k = bank_of[past]
                        dve.wait_ge(full[k].sem, full[k].at(i, past))
                    return n % 3

                def key_T(j):
                    k = filled("kT", j)
                    nc.vector.tensor_copy(kT[j].rearrange("p a b -> p (a b)"), ps[:, k, 0:DC * S]).then_inc(free[k].sem, 1)

                def maxima(j):
                    for g in range(G):
                        k = filled("s", j, g)
                        nc.vector.tensor_reduce(nmax[j][0:S, g, :], ps[0:S, k, 0:KV * S].rearrange("p (a b) -> p a b", a=KV), AX, ALU.max,
                                                negate=True).then_inc(max_ready.sem, 1)

                def reciprocals(j):
                    for g in range(G):
                        wait_drained(dve, i, "s", j, g)
                        nc.vector.reciprocal(prec[j][0:S, g, :], psum_[j][0:S, g, :]).then_inc(rec_ready.sem, 1)

                def probs_T(j):
                    for g in range(G):
                        k = filled("pT", j, g)
                        if j:
                            dve.wait_ge(full[7].sem, full[7].at(i, ("pv", 0, 3)))
                        nc.vector.tensor_copy(pT[0:S, :, g, :], ps[0:S, k, 0:KV * S].rearrange("p (a b) -> p a b", a=KV)).then_inc(free[k].sem, 1)

                def residual(name, j):
                    k = filled(name, j)
                    dve.wait_ge(xr_ready.sem, xr_ready.at(i, (0 if name == "o" else 1, j)))
                    nc.vector.tensor_tensor(xr[j][0:S, :], xr[j][0:S, :], ps[0:S, k, :], ALU.add).then_inc(free[k].sem, 1)
                    dve.wait_ge(free[k].sem, free[k].at(i, (name, j)))

                def dca_softmax(j):
                    k = filled("ds", j)
                    d3 = ps[0:S, k, 0:H * DCA].rearrange("p (a b) -> p a b", a=H)
                    per_head = lambda v: v.rearrange("p (a b) -> p a b", b=1).to_broadcast([S, H, DCA])
                    link(nc.vector.tensor_reduce(dnm[0:S, j, :], d3, AX, ALU.max, negate=True))
                    nc.vector.tensor_tensor(dp[j][0:S], d3, per_head(dnm[0:S, j, :]), ALU.add).then_inc(free[k].sem, 1)
                    yield
                    dve.wait_ge(dexp_ready.sem, dexp_ready.at(i, j))
                    link(nc.vector.tensor_reduce(dsum[0:S, j, :], dp[j][0:S], AX, ALU.add))
                    yield
                    link(nc.vector.reciprocal(drec[0:S, j, :], dsum[0:S, j, :]))
                    nc.vector.tensor_tensor(dp[j][0:S], dp[j][0:S], per_head(drec[0:S, j, :]), ALU.mult).then_inc(dp_ready.sem, 1)

                rotate(0)
                kv(0)
                rotate(1)
                kv(1)
                key_T(0)
                kv(2)
                key_T(1)
                maxima(0)
                reciprocals(0)
                kv(3)
                maxima(1)
                reciprocals(1)
                kv(4)
                probs_T(0)
                probs_T(1)
                residual("o", 0)
                dve.wait_ge(xn_stored[0], i * 16 + 1)
                dve.wait_ge(x1_ready, i * 2 + 2)
                wait_normed((2, 0))
                run(norm_x(0))
                query(0)
                residual("o", 1)
                dve.wait_ge(xn_stored[1], i * 16 + 1)
                wait_normed((2, 1))
                run(norm_x(1))
                kv(5)
                dca0, dca1 = dca_softmax(0), dca_softmax(1)
                next(dca0)
                ahead = [norm_next(0), norm_next(1)]
                for n in range(2 * H + XS_LAG):
                    if ("xq", 1) in HEAD_HOOKS.get(n, []):
                        query(1)
                    if n < 2 * H:
                        j, h = n // H, n % H
                        k = filled("xs", n)
                        nc.vector.tensor_reduce(xnm[0:S, j, h:h + 1], ps[0:S, k, 0:LM], AX, ALU.max, negate=True).then_inc(xmax_ready.sem, 1)
                    if 1 <= n < 2 * H + 1:
                        m = n - 1
                        wait_drained(dve, i, "xs", m)
                        nc.vector.reciprocal(xrec[0:S, m // H, m % H:m % H + 1], xsum[0:S, m // H, m % H:m % H + 1]).then_inc(xrec_ready.sem, 1)
                    if n >= XS_LAG and not scalar_copies(n - XS_LAG):
                        m = n - XS_LAG
                        k = filled("xpT", m)
                        if m >= NX:
                            dve.wait_ge(xpv_done.sem, xpv_done.at(i, m - NX))
                        nc.vector.tensor_copy(xpT[m % NX][0:LC].rearrange("p a b -> p (a b)"), ps[0:LC, k, 0:LN_ * S]).then_inc(free[k].sem, 1)
                    if n in (1, 2):
                        next(dca0, None)
                    if n in (DCA_EXP_1 - 1, DCA_EXP_1 + 1, DCA_EXP_1 + 2):
                        next(dca1, None)
                    for pieces in [ahead[0]] * (5 <= n < 19) + [ahead[1]] * (2 if 19 <= n <= H + PV_LAG + 1 else 0):
                        next(pieces, None)
                    if n == H + PV_LAG + 2:
                        run(ahead[0])
                        run(ahead[1])
                        residual("xo", 0)
                        dve.wait_ge(x1_ready, i * 2 + 4)
                        norm3 = norm_x(0)
                    if n > H + PV_LAG + 2:
                        next(norm3, None)
                        next(norm3, None)
                run(norm3)
                residual("xo", 1)
                wait_normed((3, 1))
                run(norm_x(1))
                assert count_[0] == LINKS, f"LINKS = {count_[0]}"
            count_[2] += LINKS * PAIRS
            count_[0] = 0
            count_[1] = None

            for j in range(2):
                dve.wait_ge(xn_stored[j], 16 * PAIRS + 1)
                dve.wait_ge(x2_stored[j], 16 * PAIRS + 1)
                dve.wait_ge(xT_stored[j], 16 * PAIRS + 1)
            dve.wait_ge(free[3].sem, free[3].before(PAIRS))
            dve.wait_ge(late_free, 2)
            for b in range(B):
                link(nc.vector.max(rsm[0:S, 0, b, :], lg_all[0:S, b, 0:E]))
                link(nc.vector.max_index(idx_u[0:S, b, :], rsm[0:S, 0, b, :], lg_all[0:S, b, 0:E]))
            link(nc.vector.tensor_copy(rsm[0:S, 4], idx_u[0:S]))
            nc.vector.tensor_scalar(rsm[0:S, 2, :, 0:1], rsm[0:S, 0, :, 0:1], -1.0, None, ALU.mult).then_inc(r_in, 1)
            for b in range(B):
                link(nc.vector.tensor_scalar(mask[0:S, b, :], iota_e[0:S, :], rsm[0:S, 4, b, 0:1], None, ALU.is_equal))
                for k in range(1, TOPK):
                    link(nc.vector.scalar_tensor_tensor(out=mask[0:S, b, :], in0=iota_e[0:S, :], scalar=rsm[0:S, 4, b, k:k + 1],
                                                        in1=mask[0:S, b, :], op0=ALU.is_equal, op1=ALU.add))
            link(nc.vector.tensor_copy(mask_sum[0:S, 0, :], mask[0:S, 0, :]))
            for b in range(1, B):
                link(nc.vector.tensor_tensor(mask_sum[0:S, b, :], mask_sum[0:S, b - 1, :], mask[0:S, b, :], ALU.add))
            dve.sem_inc(mask_ready, 1)
            dve.wait_ge(r_act, 1)
            link(nc.vector.reciprocal(rsm[0:S, 3, :, 1:2], rsm[0:S, 3, :, 0:1]))
            link(nc.vector.tensor_tensor(rsm[0:S, 5, :, 0:TOPK], rsm[0:S, 1, :, 0:TOPK],
                                         rsm[0:S, 3, :, 1:2].to_broadcast([S, B, TOPK]), ALU.mult))

            for m in range(MC):
                for half in range(2):
                    dve.wait_ge(silu_ready[m % 2], 2 * (m // 2) + half + 1)
                    dve.wait_ge(up_full[m % 2], 4 * (m // 2) + 2 * half + 2)
                    nc.vector.tensor_tensor(hT_all[:, m, half * 400:(half + 1) * 400], s_sh[half],
                                            ps[:, (m % 2) * 4 + half * 2 + 1, 0:400], ALU.mult).then_inc(hs_ready[m % 2], 1)

            dve.wait_ge(rank_full, 1)
            cnt, tiles, incl, obase = bts[:, 0, :], bts[:, 1, :], bts[:, 2, :], bts[:, 3, :]
            link(nc.vector.tensor_copy(cnt, ps[:, 1, 0:E]))
            link(nc.vector.tensor_scalar(tiles, cnt, float(T), None, ALU.is_gt))
            for n in range(2, (B * S + T - 1) // T):
                link(nc.vector.scalar_tensor_tensor(out=tiles, in0=cnt, scalar=float(n * T), in1=tiles, op0=ALU.is_gt, op1=ALU.add))
            link(nc.vector.memset(bts[:, 4, :], 1.0))
            link(nc.vector.tensor_tensor_scan(incl, bts[:, 4, :], tiles, 0.0, ALU.mult, ALU.add))
            link(nc.vector.tensor_tensor(obase, incl, tiles, ALU.subtract))
            link(nc.vector.tensor_scalar(obase, obase, float(T), float((E - 1) * T), ALU.mult, ALU.add))
            link(nc.vector.tensor_scalar(base_e[:], iota_e[:], float(T), None, ALU.mult))
            link(nc.vector.tensor_tensor(obase, obase, base_e[:], ALU.subtract))
            rank = ps[0:S, 0, 0:B * E].rearrange("p (a b) -> p a b", a=B)
            over = lambda v: v.rearrange("p (a b) -> p a b", a=1).to_broadcast([S, B, E])
            link(nc.vector.tensor_scalar(slot_e[0:S], rank, float(T), None, ALU.is_ge))
            link(nc.vector.tensor_tensor(slot_e[0:S], slot_e[0:S], over(obase[0:S]), ALU.mult))
            link(nc.vector.tensor_tensor(slot_e[0:S], slot_e[0:S], rank, ALU.add))
            link(nc.vector.tensor_tensor(slot_e[0:S], slot_e[0:S], over(base_e[0:S, :]), ALU.add))
            for k in range(TOPK):
                link(nc.vector.tensor_tensor(oh[0:S], over(iota_e[0:S, :]), rsm[0:S, 4, :, k:k + 1].to_broadcast([S, B, E]), ALU.is_equal))
                link(nc.vector.tensor_tensor(oh[0:S], oh[0:S], slot_e[0:S], ALU.mult))
                link(nc.vector.tensor_reduce(rsm[0:S, 7, :, k:k + 1], oh[0:S], AX, ALU.add))
            link(nc.vector.tensor_copy(slot_u[0:S, :].rearrange("p (a b) -> p a b", a=B), rsm[0:S, 7, :, 0:TOPK]))
            link(nc.vector.tensor_tensor(ovc, incl[0:1, :].rearrange("p (a b) -> p a b", a=1).to_broadcast([1, NOV, E]),
                                         iota_n[0:1, :].rearrange("p (a b) -> p a b", b=1).to_broadcast([1, NOV, E]), ALU.is_le))
            link(nc.vector.tensor_reduce(bts[0:1, 5, 0:NOV], ovc, AX, ALU.add))
            link(nc.vector.tensor_scalar(bts[0:1, 5, 0:NOV], bts[0:1, 5, 0:NOV], float(E - 1), None, ALU.min))
            link(nc.vector.tensor_copy(ov_i[0:1, 0:NOV], bts[0:1, 5, 0:NOV]))
            nc.vector.tensor_copy(ov_i[0:1, NOV:NOV + 1], incl[0:1, E - 1:E]).then_inc(slots_ready, 1)

            dve.wait_ge(acc_loaded, 16)
            for b in range(B):
                dve.wait_ge(dn_full, b + 1)
                nc.vector.scalar_tensor_tensor(out=acc[0:S, b, :], in0=ps[0:S, 2 + b % 2, :], scalar=rsm[0:S, 6, b, 2:3],
                                               in1=acc[0:S, b, :], op0=ALU.mult, op1=ALU.add).then_inc(dn_free, 1)

            def rows_T(r, turn):
                dve.wait_ge(xst_full[r], turn + 2)
                dve.wait_ge(up1_full[r], turn + 1)
                nc.vector.tensor_copy(xsT[r].rearrange("p a b -> p (a b)"), ps[:, r, 0:DC * T]).then_inc(xst_ready[r], 1)

            def hidden_parts(r):
                nc.vector.tensor_tensor(hT[r][:, 0:2, :].rearrange("p a b -> p (a b)"), sl[r][:, 0:2, :].rearrange("p a b -> p (a b)"),
                                        ps[:, 4 + r, 0:2 * T], ALU.mult)
                return nc.vector.tensor_tensor(hT[r][0:96, 2, :], sl[r][0:96, 2, :], ps[0:96, 4 + r, 2 * T:3 * T], ALU.mult)

            def hidden(r, turn):
                dve.wait_ge(sl_ready[r], turn + 1)
                dve.wait_ge(y_full[r], turn + 1)
                hidden_parts(r).then_inc(h_ready[r], 1)

            rows_T(0, 0)
            rows_T(1, 0)
            hidden(0, 0)
            with dve.Fori(0, E // 2 - 1) as i:
                rows_T(0, i + 1)
                hidden(1, i)
                rows_T(1, i + 1)
                hidden(0, i + 1)
            hidden(1, E // 2 - 1)
            dve.wait_ge(slots_ready, 1)
            count = dve.value_load(ov_i[0:1, NOV:NOV + 1], min_val=0, max_val=NOV)
            with dve.If(count > 0):
                with dve.Fori(0, NOV) as t:
                    with dve.If(count > t):
                        dve.wait_ge(o_t, t + 1)
                        nc.vector.tensor_copy(xsT[0].rearrange("p a b -> p (a b)"), ps[:, 0, 0:DC * T]).then_inc(o_tc, 1)
                        dve.wait_ge(o_s, t + 1)
                        hidden_parts(0).then_inc(o_h, 1)
            dve.wait_ge(dn_free, B)
            for b in range(B):
                for k in range(TOPK):
                    n = b * TOPK + k
                    dve.wait_ge(gathered[n % 4], 16 * (n // 4 + 1))
                    ins = nc.vector.scalar_tensor_tensor(out=acc[0:S, b, :], in0=xn3[0:S, n % 4, :], scalar=rsm[0:S, 5, b, k:k + 1],
                                                         in1=acc[0:S, b, :], op0=ALU.mult, op1=ALU.add)
                    ins.then_inc(added[n % 4], 1)
                    dve.wait_ge(added[n % 4], n // 4 + 1)
                dve.sem_inc(out_ready, 1)


def kernel(x, ctx_1024, L0_attn_W_attn, L0_attn_W_out, L0_attn_b_out, L0_xattn_Wq, L0_xattn_bq, L0_xattn_Wk, L0_xattn_bk,
           L0_xattn_Wv, L0_xattn_bv, L0_xattn_Wkv_dca, L0_xattn_bkv_dca, L0_xattn_qn_w, L0_xattn_qn_b, L0_xattn_kn_w,
           L0_xattn_kn_b, L0_xattn_kn_dca_w, L0_xattn_kn_dca_b, L0_xattn_Wo, L0_xattn_bo, L0_ffn_gate_w,
           L0_ffn_shared_gate_w, L0_ffn_w13, L0_ffn_w2, L0_ffn_se_gate_up_w, L0_ffn_se_down_w):
    import numpy as np
    import concourse.bacc as bacc
    from concourse.bass_utils import run_bass_kernel_spmd

    a = np.asarray
    ctx = a(ctx_1024)
    by_kind = lambda w: w.reshape(w.shape[:-1] + (H, 2, HD)).swapaxes(-3, -2).reshape(w.shape)
    inv = (1.0 / np.float32(10000.0) ** (np.arange(0, HD, 2, dtype=np.float32) / np.float32(HD))).astype(np.float32)
    ang = np.arange(S, dtype=np.float32)[:, None] * inv[None, :]
    cos, sin = np.cos(ang), np.sin(ang)
    table = np.stack([np.concatenate([cos, cos], 1), np.concatenate([-sin, sin], 1)], 1)
    cos_sin = np.concatenate([table * np.float32(SCALE), table], 1).astype(np.float32)
    se_up = a(L0_ffn_se_gate_up_w).T.reshape(DC, P, 2, MC, P).transpose(3, 1, 0, 2, 4).reshape(MC, P, DC, 2 * P)
    arrays = {
        "x": a(x),
        "ctxT": ctx[:, :LM, :].transpose(0, 2, 1).reshape(B, CC, P, LM).transpose(0, 2, 1, 3),
        "dcaT": ctx[:, LM:, :].reshape(B * DCA, CC * P).T.reshape(CC, P, B * DCA),
        "W_attn": a(L0_attn_W_attn), "W_out": a(L0_attn_W_out), "b_out": a(L0_attn_b_out),
        "Wq": a(L0_xattn_Wq), "bq": a(L0_xattn_bq),
        "Wkv": by_kind(np.concatenate([a(L0_xattn_Wk), a(L0_xattn_Wv)], 1)),
        "bkv": by_kind(np.concatenate([a(L0_xattn_bk), a(L0_xattn_bv)])),
        "Wdca": a(L0_xattn_Wkv_dca), "bdca": a(L0_xattn_bkv_dca),
        "norm": np.stack([a(v) for v in (L0_xattn_qn_w, L0_xattn_qn_b, L0_xattn_kn_w, L0_xattn_kn_b,
                                         L0_xattn_kn_dca_w, L0_xattn_kn_dca_b)], 1),
        "Wo": a(L0_xattn_Wo), "bo": a(L0_xattn_bo),
        "gates": np.concatenate([a(L0_ffn_gate_w).T, a(L0_ffn_shared_gate_w).T], 1),
        "w13": a(L0_ffn_w13).transpose(0, 2, 1).reshape(E, DC, P, 2 * I).transpose(0, 2, 1, 3),
        "w2": a(L0_ffn_w2).transpose(0, 2, 1),
        "se_up": se_up, "se_down": a(L0_ffn_se_down_w).T, "cos_sin": cos_sin,
    }
    nc = bacc.Bacc("TRN2", target_bir_lowering=False, num_devices=1)
    sent, args = {}, []
    for name, v in arrays.items():
        v = np.ascontiguousarray(v)
        sent[f"in_{name}"] = v
        args.append(nc.dram_tensor(f"in_{name}", v.shape, mybir.dt.from_np(v.dtype), kind="ExternalInput").ap())
    result = nc.dram_tensor("result", (B, S, D), F32, kind="ExternalOutput").ap()
    decoder_kernel(nc, *args, result)
    return run_bass_kernel_spmd(nc, [sent], core_ids=[0]).results[0]["result"]
```
